# Optimizing a Trainium2 kernel written in Bass

```python
import numpy as np
import jax
import jax.numpy as jnp

def _softmax(x, axis=-1):
    return jax.nn.softmax(x, axis=axis)

def _gelu(x):
    return jax.nn.gelu(x, approximate=True)

def _silu(x):
    return jax.nn.silu(x)

def _sigmoid(x):
    return jax.nn.sigmoid(x)

def _layernorm(x, axis=-1, eps=1e-05):
    m = jnp.mean(x, axis=axis, keepdims=True)
    v = jnp.var(x, axis=axis, keepdims=True)
    return (x - m) / jnp.sqrt(v + eps)

def _scatter_add(tgt, idx, src, axis=0):
    return tgt.at[idx].add(src)

def _segment_sum(src, seg, n):
    return jax.ops.segment_sum(src, seg, n)
kernel_name = 'mk_adaln_ffn_d2_seqx_r8_030343'

def setup_inputs(seed: int=0):
    np.random.seed(seed)
    _w = jnp.asarray

    def _rec_inputs():
        import jax
        import jax.numpy as jnp
        _rk = jax.random.key(seed)
        x = -0.000125 + 0.9999 * jax.random.normal(jax.random.fold_in(_rk, 1), (8, 128, 512), jnp.float32)
        _lenS = 128 - jax.random.randint(jax.random.fold_in(_rk, 7), (8,), 0, max(1, 128 // 4) + 1, jnp.int32)
        _lenS2 = 128 - jax.random.randint(jax.random.fold_in(_rk, 8), (8,), 0, max(1, 128 // 4) + 1, jnp.int32)
        itok_B_0_7 = jax.random.randint(jax.random.fold_in(_rk, 11), (8,), 0, 8, jnp.int32)
        itok_Bx16_0_63 = jax.random.randint(jax.random.fold_in(_rk, 12), (8, 16), 0, 64, jnp.int32)
        itok_B_207_1644 = jax.random.randint(jax.random.fold_in(_rk, 13), (8,), 207, 1645, jnp.int32)
        return (x, itok_B_0_7, itok_Bx16_0_63, itok_B_207_1644)
    x, itok_B_0_7, itok_Bx16_0_63, itok_B_207_1644 = _rec_inputs()

    def _L0_cond_setup():
        import jax, jax.numpy as jnp
        import numpy as np
        TOP_K = 2
        LANG_BIAS = 5.0
        SCALING = 32.0 / 16.0
        LANGUAGE_PAD_ID = -1
        key = jax.random.key(seed)
        ks = jax.random.split(key, 6)
        B, T, D, O, E, R = (4, 256, 512, 512, 8, 16)
        x = jax.random.normal(ks[0], (B, T, D), dtype=jnp.float32)
        language_ids = jax.random.randint(ks[1], (B,), 0, E).astype(jnp.int64)
        W = jax.random.normal(ks[2], (O, D), dtype=jnp.float32) * (1.0 / np.sqrt(D))
        Wr = jax.random.normal(ks[3], (E, D), dtype=jnp.float32) * (1.0 / np.sqrt(D))
        A = jax.random.normal(ks[4], (E, R, D), dtype=jnp.float32) * (1.0 / np.sqrt(D))
        Bm = jax.random.normal(ks[5], (O, R), dtype=jnp.float32) * 0.0
        Bm = jnp.broadcast_to(Bm, (E, O, R)) + jax.random.normal(ks[5], (E, O, R), dtype=jnp.float32) * 0.02
        return {'x': x, 'language_ids': language_ids, 'W': W, 'Wr': Wr, 'A': A, 'B': Bm}
    _L0_cond_all = _L0_cond_setup()
    _L0_cond_in = {k: v for k, v in _L0_cond_all.items() if k in ('W', 'Wr', 'A', 'B')}
    del _L0_cond_all

    def _L0_ffn_setup():
        import jax, jax.numpy as jnp
        import numpy as np
        SCALING = 32.0 / 16.0
        key = jax.random.key(seed)
        ks = jax.random.split(key, 7)
        B, T, D, O, R, E = (4, 256, 512, 512, 16, 8)
        x = jax.random.normal(ks[0], (B, T, D), dtype=jnp.float32)
        base_W = jax.random.normal(ks[1], (O, D), dtype=jnp.float32) * D ** (-0.5)
        base_b = jax.random.normal(ks[2], (O,), dtype=jnp.float32) * 0.01
        router_W = jax.random.normal(ks[3], (2 * E - 1, D), dtype=jnp.float32) * D ** (-0.5)
        router_b = jax.random.normal(ks[4], (2 * E - 1,), dtype=jnp.float32) * 0.01
        A = jax.random.normal(ks[5], (E, R, D), dtype=jnp.float32) * D ** (-0.5)
        Bm = jax.random.normal(ks[6], (E, O, R), dtype=jnp.float32) * R ** (-0.5)
        assigned_idx = 0
        others = [i for i in range(E) if i != assigned_idx]
        expert_map = jnp.array([assigned_idx] * E + others, dtype=jnp.int32)
        return {'x': x, 'base_W': base_W, 'base_b': base_b, 'router_W': router_W, 'router_b': router_b, 'A': A, 'B': Bm, 'expert_map': expert_map}
    _L0_ffn_all = _L0_ffn_setup()
    _L0_ffn_in = {k: v for k, v in _L0_ffn_all.items() if k in ('base_W', 'base_b', 'router_W', 'router_b', 'A', 'B', 'expert_map')}
    del _L0_ffn_all

    def _L1_cond_setup():
        import jax, jax.numpy as jnp
        import numpy as np
        B, S, HID = (4, 128, 512)
        D, HQ, HK = (128, 32, 8)
        PAGES, PSIZE, NPP = (64, 32, 16)
        THETA = 10000.0
        EPS = 1e-06
        SCALE = 1.0 / float(np.sqrt(D))

        def _rmsnorm(t, w):
            var = jnp.mean(t * t, axis=-1, keepdims=True)
            return t * jax.lax.rsqrt(var + EPS) * w

        def _rope(t, pos):
            inv_freq = 1.0 / THETA ** (jnp.arange(0, D, 2, dtype=jnp.float32) / D)
            freqs = pos[..., None].astype(jnp.float32) * inv_freq
            cos = jnp.cos(freqs)[:, :, None, :]
            sin = jnp.sin(freqs)[:, :, None, :]
            t1, t2 = (t[..., :D // 2], t[..., D // 2:])
            return jnp.concatenate([t1 * cos - t2 * sin, t2 * cos + t1 * sin], axis=-1)
        key = jax.random.key(seed)
        ks = jax.random.split(key, 10)
        x = jax.random.normal(ks[0], (B, S, HID), jnp.float32)
        Wq = jax.random.normal(ks[1], (HQ * D, HID), jnp.float32) * 0.02
        Wk = jax.random.normal(ks[2], (HK * D, HID), jnp.float32) * 0.02
        Wv = jax.random.normal(ks[3], (HK * D, HID), jnp.float32) * 0.02
        Wo = jax.random.normal(ks[4], (HID, HQ * D), jnp.float32) * 0.02
        q_norm_w = jax.random.uniform(ks[5], (D,), jnp.float32)
        k_norm_w = jax.random.uniform(ks[6], (D,), jnp.float32)
        k_cache = jax.random.normal(ks[7], (PAGES, PSIZE, HK, D), jnp.float32)
        v_cache = jax.random.normal(ks[8], (PAGES, PSIZE, HK, D), jnp.float32)
        block_table = jnp.arange(B * NPP, dtype=jnp.int32).reshape(B, NPP)
        cache_seqlens = jax.random.randint(ks[9], (B,), 0, 475).astype(jnp.int32)
        return dict(x=x, Wq=Wq, Wk=Wk, Wv=Wv, Wo=Wo, q_norm_w=q_norm_w, k_norm_w=k_norm_w, k_cache=k_cache, v_cache=v_cache, block_table=block_table, cache_seqlens=cache_seqlens)
    _L1_cond_all = _L1_cond_setup()
    _L1_cond_in = {k: v for k, v in _L1_cond_all.items() if k in ('Wq', 'Wk', 'Wv', 'Wo', 'q_norm_w', 'k_norm_w', 'k_cache', 'v_cache')}
    del _L1_cond_all

    def _L1_ffn_setup():
        import jax, jax.numpy as jnp
        import numpy as np
        B, S, IN, OUT = (4, 256, 512, 512)
        E, K, R = (8, 2, 16)
        CAP_FACTOR = 3.0
        ALPHA = 1.0 / R
        LN_EPS = 1e-05
        key = jax.random.key(seed)
        ks = jax.random.split(key, 6)
        return {'x': jax.random.normal(ks[0], (B, S, IN), dtype=jnp.float32), 'weight': jax.random.normal(ks[1], (OUT, IN), dtype=jnp.float32) * 0.02, 'lora_A': jax.random.normal(ks[2], (E, IN, R), dtype=jnp.float32) / np.sqrt(R), 'lora_B': jax.random.normal(ks[3], (E, R, OUT), dtype=jnp.float32) * 0.02, 'gw1': jax.random.normal(ks[4], (4 * E, IN), dtype=jnp.float32) * 0.02, 'gb1': jnp.zeros((4 * E,), dtype=jnp.float32), 'ln_gamma': jnp.ones((4 * E,), dtype=jnp.float32), 'ln_beta': jnp.zeros((4 * E,), dtype=jnp.float32), 'gw2': jax.random.normal(ks[5], (E, 4 * E), dtype=jnp.float32) * 0.02, 'gb2': jnp.zeros((E,), dtype=jnp.float32)}
    _L1_ffn_all = _L1_ffn_setup()
    _L1_ffn_in = {k: v for k, v in _L1_ffn_all.items() if k in ('weight', 'lora_A', 'lora_B', 'gw1', 'gb1', 'ln_gamma', 'ln_beta', 'gw2', 'gb2')}
    del _L1_ffn_all
    return {'x': x, 'itok_B_0_7': itok_B_0_7, 'itok_Bx16_0_63': itok_Bx16_0_63, 'itok_B_207_1644': itok_B_207_1644, 'L0_cond_W': _L0_cond_in['W'], 'L0_cond_Wr': _L0_cond_in['Wr'], 'L0_cond_A': _L0_cond_in['A'], 'L0_cond_B': _L0_cond_in['B'], 'L0_ffn_base_W': _L0_ffn_in['base_W'], 'L0_ffn_base_b': _L0_ffn_in['base_b'], 'L0_ffn_router_W': _L0_ffn_in['router_W'], 'L0_ffn_router_b': _L0_ffn_in['router_b'], 'L0_ffn_A': _L0_ffn_in['A'], 'L0_ffn_B': _L0_ffn_in['B'], 'L0_ffn_expert_map': _L0_ffn_in['expert_map'], 'L1_cond_Wq': _L1_cond_in['Wq'], 'L1_cond_Wk': _L1_cond_in['Wk'], 'L1_cond_Wv': _L1_cond_in['Wv'], 'L1_cond_Wo': _L1_cond_in['Wo'], 'L1_cond_q_norm_w': _L1_cond_in['q_norm_w'], 'L1_cond_k_norm_w': _L1_cond_in['k_norm_w'], 'L1_cond_k_cache': _L1_cond_in['k_cache'], 'L1_cond_v_cache': _L1_cond_in['v_cache'], 'L1_ffn_weight': _L1_ffn_in['weight'], 'L1_ffn_lora_A': _L1_ffn_in['lora_A'], 'L1_ffn_lora_B': _L1_ffn_in['lora_B'], 'L1_ffn_gw1': _L1_ffn_in['gw1'], 'L1_ffn_gb1': _L1_ffn_in['gb1'], 'L1_ffn_ln_gamma': _L1_ffn_in['ln_gamma'], 'L1_ffn_ln_beta': _L1_ffn_in['ln_beta'], 'L1_ffn_gw2': _L1_ffn_in['gw2'], 'L1_ffn_gb2': _L1_ffn_in['gb2']}

def reference(x, itok_B_0_7, itok_Bx16_0_63, itok_B_207_1644, L0_cond_W, L0_cond_Wr, L0_cond_A, L0_cond_B, L0_ffn_base_W, L0_ffn_base_b, L0_ffn_router_W, L0_ffn_router_b, L0_ffn_A, L0_ffn_B, L0_ffn_expert_map, L1_cond_Wq, L1_cond_Wk, L1_cond_Wv, L1_cond_Wo, L1_cond_q_norm_w, L1_cond_k_norm_w, L1_cond_k_cache, L1_cond_v_cache, L1_ffn_weight, L1_ffn_lora_A, L1_ffn_lora_B, L1_ffn_gw1, L1_ffn_gb1, L1_ffn_ln_gamma, L1_ffn_ln_beta, L1_ffn_gw2, L1_ffn_gb2):
    import jax
    import jax.numpy as jnp

    def _L0_cond_ref(x, language_ids, W, Wr, A, B):
        import jax, jax.numpy as jnp
        import numpy as np
        TOP_K = 2
        LANG_BIAS = 5.0
        SCALING = 32.0 / 16.0
        LANGUAGE_PAD_ID = -1
        base = jnp.einsum('btd,od->bto', x, W)
        E = Wr.shape[0]
        logits = jnp.einsum('btd,ed->bte', x.astype(jnp.float32), Wr.astype(jnp.float32))
        expert_targets = language_ids
        valid = expert_targets >= 0
        tgt = jnp.where(valid, expert_targets, 0)
        bias = jax.nn.one_hot(tgt, E, dtype=logits.dtype) * LANG_BIAS
        bias = jnp.where(valid[:, None], bias, 0.0)
        logits = logits + bias[:, None, :]
        topw, topi = jax.lax.top_k(logits, TOP_K)
        weights = jax.nn.softmax(topw, axis=-1)
        gates = jnp.sum(jax.nn.one_hot(topi, E, dtype=weights.dtype) * weights[..., None], axis=-2)
        gates = gates.astype(x.dtype)
        h = jnp.einsum('btd,erd->bter', x, A)
        lora_out = jnp.einsum('bter,bte,eor->bto', h, gates, B)
        return base + SCALING * lora_out

    def _L0_ffn_ref(x, base_W, base_b, router_W, router_b, A, B, expert_map):
        import jax, jax.numpy as jnp
        import numpy as np
        SCALING = 32.0 / 16.0
        E = A.shape[0]
        base_out = jnp.einsum('btd,od->bto', x, base_W) + base_b
        logits = jnp.einsum('btd,nd->btn', x, router_W) + router_b
        probs = jax.nn.softmax(logits, axis=-1)
        topk_p, topk_i = jax.lax.top_k(probs, E)
        mapped = expert_map[topk_i]
        onehot = (mapped[..., None] == jnp.arange(E)).astype(x.dtype)
        w = jnp.einsum('btk,btke->bte', topk_p, onehot)
        h = jnp.einsum('btd,erd->bter', x, A)
        lora = jnp.einsum('bter,eor->bto', h * w[..., None], B) * SCALING
        return base_out + lora

    def _L1_cond_ref(x, Wq, Wk, Wv, Wo, q_norm_w, k_norm_w, k_cache, v_cache, block_table, cache_seqlens):
        import jax, jax.numpy as jnp
        import numpy as np
        B, S, HID = (4, 128, 512)
        D, HQ, HK = (128, 32, 8)
        PAGES, PSIZE, NPP = (64, 32, 16)
        THETA = 10000.0
        EPS = 1e-06
        SCALE = 1.0 / float(np.sqrt(D))

        def _rmsnorm(t, w):
            var = jnp.mean(t * t, axis=-1, keepdims=True)
            return t * jax.lax.rsqrt(var + EPS) * w

        def _rope(t, pos):
            inv_freq = 1.0 / THETA ** (jnp.arange(0, D, 2, dtype=jnp.float32) / D)
            freqs = pos[..., None].astype(jnp.float32) * inv_freq
            cos = jnp.cos(freqs)[:, :, None, :]
            sin = jnp.sin(freqs)[:, :, None, :]
            t1, t2 = (t[..., :D // 2], t[..., D // 2:])
            return jnp.concatenate([t1 * cos - t2 * sin, t2 * cos + t1 * sin], axis=-1)
        bsz, seqlen, _ = x.shape
        q = jnp.einsum('bsd,ed->bse', x, Wq).reshape(bsz, seqlen, HQ, D)
        k = jnp.einsum('bsd,ed->bse', x, Wk).reshape(bsz, seqlen, HK, D)
        v = jnp.einsum('bsd,ed->bse', x, Wv).reshape(bsz, seqlen, HK, D)
        q = _rmsnorm(q, q_norm_w)
        k = _rmsnorm(k, k_norm_w)
        pos = cache_seqlens[:, None] + jnp.arange(seqlen)[None, :]
        q = _rope(q, pos)
        k = _rope(k, pos)
        L = NPP * PSIZE
        kc = k_cache[block_table].reshape(bsz, L, HK, D)
        vc = v_cache[block_table].reshape(bsz, L, HK, D)
        k_all = jnp.concatenate([kc, k], axis=1)
        v_all = jnp.concatenate([vc, v], axis=1)
        valid_c = jnp.arange(L)[None, :] < cache_seqlens[:, None]
        valid = jnp.concatenate([valid_c, jnp.ones((bsz, seqlen), dtype=bool)], axis=1)
        rep = HQ // HK
        k_all = jnp.repeat(k_all, rep, axis=2)
        v_all = jnp.repeat(v_all, rep, axis=2)
        scores = jnp.einsum('bqhd,bkhd->bhqk', q, k_all) * SCALE
        scores = jnp.where(valid[:, None, None, :], scores, -1e+30)
        probs = jax.nn.softmax(scores, axis=-1)
        o = jnp.einsum('bhqk,bkhd->bqhd', probs, v_all)
        o = o.reshape(bsz, seqlen, HQ * D)
        return jnp.einsum('bse,de->bsd', o, Wo)

    def _L1_ffn_ref(x, weight, lora_A, lora_B, gw1, gb1, ln_gamma, ln_beta, gw2, gb2):
        import jax, jax.numpy as jnp
        import numpy as np
        B, S, IN, OUT = (4, 256, 512, 512)
        E, K, R = (8, 2, 16)
        CAP_FACTOR = 3.0
        ALPHA = 1.0 / R
        LN_EPS = 1e-05
        orig_shape = x.shape
        xf = x.reshape(-1, orig_shape[-1])
        N = xf.shape[0]
        capacity = int(CAP_FACTOR * N / E)
        h = xf @ gw1.T + gb1
        mu = jnp.mean(h, axis=-1, keepdims=True)
        var = jnp.mean((h - mu) ** 2, axis=-1, keepdims=True)
        h = (h - mu) * jax.lax.rsqrt(var + LN_EPS) * ln_gamma + ln_beta
        h = jax.nn.relu(h)
        gates = h @ gw2.T + gb2
        top_v, top_i = jax.lax.top_k(gates, K)
        top_g = jax.nn.softmax(top_v, axis=-1)
        onehot = (top_i[..., None] == jnp.arange(E)).astype(xf.dtype)
        counts = onehot.sum(axis=0)
        allowed = (counts <= capacity).astype(xf.dtype)
        w = jnp.einsum('nke,nk,ke->ne', onehot, top_g, allowed)
        main = xf @ weight.T
        tmp = jnp.einsum('ni,eir->enr', xf, lora_A)
        tmp = tmp * w.T[:, :, None]
        lora = jnp.einsum('enr,ero->no', tmp, lora_B) * ALPHA
        out = main + lora
        return out.reshape(*orig_shape[:-1], weight.shape[0])
    x = x + _L0_ffn_ref(_L0_cond_ref(x, itok_B_0_7, L0_cond_W, L0_cond_Wr, L0_cond_A, L0_cond_B), L0_ffn_base_W, L0_ffn_base_b, L0_ffn_router_W, L0_ffn_router_b, L0_ffn_A, L0_ffn_B, L0_ffn_expert_map)
    x = x + _L1_ffn_ref(_L1_cond_ref(x, L1_cond_Wq, L1_cond_Wk, L1_cond_Wv, L1_cond_Wo, L1_cond_q_norm_w, L1_cond_k_norm_w, L1_cond_k_cache, L1_cond_v_cache, itok_Bx16_0_63, itok_B_207_1644), L1_ffn_weight, L1_ffn_lora_A, L1_ffn_lora_B, L1_ffn_gw1, L1_ffn_gb1, L1_ffn_ln_gamma, L1_ffn_ln_beta, L1_ffn_gw2, L1_ffn_gb2)
    return x

_drawn_inputs = setup_inputs


def setup_inputs(seed=0):
    import zlib

    import numpy as np

    out = dict(_drawn_inputs(seed))
    spreads = {'L1_ffn_gb1': (0.0, 0.8),
     'L1_ffn_ln_gamma': (1.0, 0.6),
     'L1_ffn_ln_beta': (0.0, 0.8),
     'L1_ffn_gb2': (0.0, 0.8)}
    factors = {'L0_cond_Wr': 3.565,
     'L0_ffn_base_b': 8.0,
     'L0_ffn_router_b': 7.682,
     'L1_cond_Wq': 6.457,
     'L1_cond_Wk': 8.0,
     'L1_cond_Wv': 8.0,
     'L1_cond_Wo': 3.468,
     'L1_cond_q_norm_w': 8.0,
     'L1_cond_k_norm_w': 8.0,
     'L1_cond_k_cache': 6.615,
     'L1_cond_v_cache': 3.647,
     'L1_ffn_weight': 3.503,
     'L1_ffn_lora_A': 8.0,
     'L1_ffn_lora_B': 8.0,
     'L1_ffn_gw1': 8.0,
     'L1_ffn_gw2': 8.0}
    for name, (base, spread) in spreads.items():
        noise = np.random.default_rng([zlib.crc32(name.encode()), seed]).standard_normal(out[name].shape)
        drawn = base * np.exp(spread * noise) if base else spread * noise
        out[name] = jnp.asarray(drawn.astype(out[name].dtype))
    for name, factor in factors.items():
        out[name] = (out[name] * factor).astype(out[name].dtype)
    return out
```

```python
from contextlib import ExitStack

import numpy as np

import concourse.bass as bass
from concourse import mybir

F32 = mybir.dt.float32
F32R = mybir.dt.float32r
I32 = mybir.dt.int32
U32 = mybir.dt.uint32
ALU = mybir.AluOpType
ACT = mybir.ActivationFunctionType
AX = mybir.AxisListType
ds = bass.ds

P = 128
SEQS = 8
TOK = SEQS * P
DM = 512
CT = DM // P
HALF = TOK // 2
KVH = 8
QPK = 4
PSIZE = 32
NPP = 16
CACHE = PSIZE * NPP
KT = CACHE // P
KEYS = CACHE + P
STEPS = KVH * SEQS
EXP = 8
RANK = 16
NR1 = 2 * EXP - 1
GH = 4 * EXP
CAPACITY = int(3.0 * TOK / EXP)
QW, KVW, OW = CT * DM, CT * 2 * P, QPK * DM
GW = QW + KVW + OW
CHUNK = GW // SEQS
SCALE = 1.0 / float(np.sqrt(P))
MASKED = -1e30

TWO_PI_1 = 6.28125
TWO_PI_2 = float(np.float32(np.round((2 * np.pi - TWO_PI_1) * 2.0**21) / 2.0**21))
TWO_PI_3 = float(np.float32(2 * np.pi - TWO_PI_1 - TWO_PI_2))
ROUND = 1.5 * 2.0**23

C_ID, C_IOTA, C_FREQ, C_KEY = 0, P, P + 16, P + 80
C_ALL = C_KEY + CACHE


class Step:

    def __init__(self, off, trip=0):
        self.off, self.trip = off, trip

    @property
    def parity(self):
        return self.off % 2

    def half(self, add=0):
        return self.trip + (self.off // 2 + add)

    def times(self, m, add=0):
        if isinstance(self.trip, int):
            return m * (2 * self.trip + self.off) + add
        return self.trip * (2 * m) + (m * self.off + add)

    def plus(self, n):
        return Step(self.off + n, self.trip)

    @property
    def first(self):
        return isinstance(self.trip, int) and 2 * self.trip + self.off <= 0

    @property
    def after_last(self):
        return isinstance(self.trip, int) and self.off == STEPS

    def turned(self, add=0):
        if self.first:
            return 2 * (self.off + 1) + add
        if self.after_last:
            add -= 2
        return self.times(7, add - 3)


TURNS = dict(kc=5, q=6)


def turn_no(i, name):
    j = name if isinstance(name, int) else TURNS[name]
    return i.turned(j - 5) if i.first else i.turned(j)


def turn_bank(i, name):
    j = name if isinstance(name, int) else TURNS[name]
    return BANK_T + (i.off + j + 1) % 2


def build(nc, t):
    top = ExitStack()
    with top:
        ps = top.enter_context(nc.psum_tensor("ps", [P, 8, 512], F32))
        cst = top.enter_context(nc.sbuf_tensor("cst", [P, C_ALL], F32))
        ident = cst[:, C_ID:C_ID + P]
        ones = top.enter_context(nc.sbuf_tensor("ones", [P, P], F32))
        x1_split = nc.dram_tensor("x1_split", (SEQS, P, 2 * DM), F32, kind="Internal").ap()
        x1_whole = nc.dram_tensor("x1_whole", (P, CT, TOK), F32, kind="Internal").ap()
        rope_tab = nc.dram_tensor("rope_tab", (SEQS, P, 4 * P), F32, kind="Internal").ap()
        mask_tab = nc.dram_tensor("mask_tab", (SEQS, P, KEYS), F32, kind="Internal").ap()
        tables(nc, t, cst, ones, rope_tab, mask_tab)
        first_block(nc, t, ps, cst, x1_split, x1_whole)
        with nc.sbuf_tensor("att", [P, SEQS, DM], F32) as att:
            attention(nc, t, ps, cst, x1_split, rope_tab, mask_tab, att)
            last_layer(nc, t, ps, cst, ones, x1_whole, att)


def tables(nc, t, cst, ones, rope_tab, mask_tab):
    with ExitStack() as ctx:
        sb = lambda n, s, d=F32: ctx.enter_context(nc.sbuf_tensor(n, s, d))
        sem = lambda n: ctx.enter_context(nc.semaphore(n))
        lens = sb("lens", [P, SEQS], I32)
        tokid = sb("tokid", [P, 1])
        normw = sb("normw", [P, 2 * P])
        lenf, pos = sb("lenf", [P, SEQS]), sb("pos", [P, SEQS])
        ang, turns, red, cosr, over = (sb(n, [P, SEQS, 64]) for n in ("ang", "turns", "red", "cosr", "over"))
        sin, cos = sb("sin", [P, SEQS, 64]), sb("cos", [P, SEQS, 64])
        tab = sb("tab", [P, SEQS, 4 * P])
        msk = sb("msk", [P, SEQS, KEYS])
        loaded, chain, reduced, trig, tabbed, masked, stored = (
            sem(n) for n in ("loaded", "chain", "reduced", "trig", "tabbed", "masked", "stored"))
        block = ctx.enter_context(nc.Block())

        @block.sync
        def _(sp):
            sp.dma_start(cst[:, :], t["consts"]).then_inc(loaded, 16)
            sp.dma_start(lens[:, :], t["lens"]).then_inc(loaded, 16)
            sp.dma_start(tokid[:, :], t["tokid"]).then_inc(loaded, 16)
            sp.dma_start(normw[:, :], t["normw"]).then_inc(loaded, 16)
            sp.wait_ge(masked, 1)
            sp.dma_start(mask_tab.rearrange("b p k -> p b k"), msk[:, :, :]).then_inc(stored, 16)
            sp.wait_ge(tabbed, 8)
            sp.dma_start(rope_tab.rearrange("b p k -> p b k"), tab[:, :, :]).then_inc(stored, 16)
            sp.wait_ge(stored, 32)

        @block.vector
        def _(dve):
            n = [0]

            def link(ins):
                n[0] += 1
                ins.then_inc(chain, 1)
                dve.wait_ge(chain, n[0])

            dve.memset(ones[:, :], 1.0)
            dve.wait_ge(loaded, 64)
            link(dve.tensor_copy(lenf[:, :], lens[:, :]))
            link(dve.tensor_scalar(pos[:, :], lenf[:, :], tokid[:, 0:1], None, ALU.add))
            freq = cst[:, C_FREQ:C_FREQ + 64].unsqueeze(1).broadcast_to([P, SEQS, 64])
            link(dve.tensor_tensor(ang[:, :, :], pos[:, :].unsqueeze(2).broadcast_to([P, SEQS, 64]), freq, ALU.mult))
            link(dve.tensor_scalar(turns[:, :, :], ang[:, :, :], float(1 / (2 * np.pi)), None, ALU.mult))
            link(dve.tensor_scalar(turns[:, :, :], turns[:, :, :], ROUND, None, ALU.add))
            link(dve.tensor_scalar(turns[:, :, :], turns[:, :, :], ROUND, None, ALU.subtract))
            for part, src in ((TWO_PI_1, ang), (TWO_PI_2, red), (TWO_PI_3, red)):
                link(dve.scalar_tensor_tensor(out=red[:, :, :], in0=turns[:, :, :], scalar=-part, in1=src[:, :, :],
                                              op0=ALU.mult, op1=ALU.add))
            link(dve.tensor_scalar(red[:, :, :], red[:, :, :], float(np.float32(3.1415925)), float(np.float32(-3.1415925)), ALU.min, ALU.max))
            link(dve.tensor_scalar(cosr[:, :, :], red[:, :, :], float(np.pi / 2), None, ALU.add))
            link(dve.tensor_scalar(over[:, :, :], cosr[:, :, :], float(np.pi), float(-2 * np.pi), ALU.is_gt, ALU.mult))
            link(dve.tensor_tensor(cosr[:, :, :], cosr[:, :, :], over[:, :, :], ALU.add))
            dve.tensor_scalar(cosr[:, :, :], cosr[:, :, :], float(np.float32(3.1415925)), float(np.float32(-3.1415925)), ALU.min,
                              ALU.max).then_inc(reduced, 1)
            link(dve.memset(msk[:, :, CACHE:], 0.0))
            for b in range(SEQS):
                ins = dve.tensor_scalar(msk[:, b, 0:CACHE], cst[:, C_KEY:C_KEY + CACHE], lenf[:, b:b + 1], MASKED,
                                        ALU.is_ge, ALU.mult)
            ins.then_inc(masked, 1)
            dve.wait_ge(trig, 2)
            for who in range(2):
                for half in range(2):
                    w = normw[:, who * P + half * 64:who * P + half * 64 + 64].unsqueeze(1).broadcast_to([P, SEQS, 64])
                    at = 2 * who * P + half * 64
                    dve.tensor_tensor(tab[:, :, at:at + 64], cos[:, :, :], w, ALU.mult).then_inc(tabbed, 1)
                    if half == 0:
                        dve.tensor_tensor(tab[:, :, at + P:at + P + 64], sin[:, :, :], w, ALU.mult).then_inc(tabbed, 1)
                    else:
                        if who:
                            dve.wait_ge(tabbed, 4)
                        link(dve.tensor_scalar(over[:, :, :], sin[:, :, :], -1.0, None, ALU.mult))
                        dve.tensor_tensor(tab[:, :, at + P:at + P + 64], over[:, :, :], w, ALU.mult).then_inc(tabbed, 1)

        @block.scalar
        def _(act):
            act.wait_ge(reduced, 1)
            act.activation(sin[:, :, :], red[:, :, :], ACT.Sin).then_inc(trig, 1)
            act.activation(cos[:, :, :], cosr[:, :, :], ACT.Sin).then_inc(trig, 1)


class Layer:

    def __init__(self, sb, name, routes):
        self.name, self.routes = name, routes
        self.w_hi, self.w_lo = sb(name + "_w_hi", [P, CT, DM + P], F32R), sb(name + "_w_lo", [P, CT, DM + P], F32R)
        self.b_hi, self.b_lo = sb(name + "_b_hi", [P, DM], F32R), sb(name + "_b_lo", [P, DM], F32R)
        self.route_w = sb(name + "_route_w", [P, CT, routes])


class Work:

    def __init__(self, sb, sem, name):
        self.hid = sb(name + "_hid", [P, 2, HALF])
        self.gate = sb(name + "_gate", [P, SEQS, EXP])
        self.gate_wide = sb(name + "_gate_wide", [P, SEQS, P])
        self.hg = sb(name + "_hg", [P, 2, HALF])
        self.hg_hi, self.hg_lo = sb(name + "_hg_hi", [P, 2, HALF], F32R), sb(name + "_hg_lo", [P, 2, HALF], F32R)
        self.split_w = sem(name + "_split_w")
        self.inputs_ready = sem(name + "_inputs_ready")
        self.logits_done = sem(name + "_logits_done")
        self.hid_done = sem(name + "_hid_done")
        self.hid_copied = sem(name + "_hid_copied")
        self.gates_wide = sem(name + "_gates_wide")
        self.gates_turned = sem(name + "_gates_turned")
        self.gated = sem(name + "_gated")
        self.gated_hi = sem(name + "_gated_hi")
        self.gated_lo = sem(name + "_gated_lo")
        self.out_done = sem(name + "_out_done")
        self.out_hi = sem(name + "_out_hi")
        self.bank_free = sem(name + "_bank_free")


def mm3(pe, out, lhs, rhs, start, stop):
    pe.matmul(out, lhs[0], rhs[0], start=start, stop=False)
    pe.matmul(out, lhs[0], rhs[1], start=False, stop=False)
    return pe.matmul(out, lhs[1], rhs[0], start=False, stop=stop)


def halves(h):
    return slice(h * HALF, (h + 1) * HALF)


def layer_tensor(pe, k, ps, ident, x, x_hi, x_lo, L, wk, routing):
    pe.wait_ge(wk.inputs_ready, 2 * k + 2)
    routing(pe)
    pe.wait_ge(wk.split_w, 2 * k + 2)
    for h in range(2):
        if k:
            pe.wait_ge(wk.hid_copied, 2 * k)
        for c in range(CT):
            a = slice(DM, DM + P)
            ins = mm3(pe, ps[:, 4 + h, :], (L.w_hi[:, c, a], L.w_lo[:, c, a]),
                      (x_hi[:, c, halves(h)], x_lo[:, c, halves(h)]), c == 0, c == CT - 1)
        ins.then_inc(wk.hid_done, 1)

    def base(h):
        for o in range(CT):
            pe_free = 8 * k + 4 * h + o - 3
            if pe_free > 0:
                pe.wait_ge(wk.bank_free, pe_free)
            for c in range(CT):
                w = slice(o * P, o * P + P)
                mm3(pe, ps[:, o, :], (L.w_hi[:, c, w], L.w_lo[:, c, w]),
                    (x_hi[:, c, halves(h)], x_lo[:, c, halves(h)]), c == 0, False)

    def turn_gates(h):
        pe.wait_ge(wk.gates_wide, k + 1)
        if h or k:
            pe.wait_ge(wk.gated, 2 * k + h)
        for b in range(4):
            ins = pe.transpose(ps[:, 6, b * P:b * P + P], wk.gate_wide[:, 4 * h + b, :], ident)
        ins.then_inc(wk.gates_turned, 1)

    def experts(h):
        pe.wait_ge(wk.gated_lo, 2 * k + h + 1)
        for o in range(CT):
            w = slice(o * P, o * P + P)
            mm3(pe, ps[:, o, :], (L.b_hi[:, w], L.b_lo[:, w]), (wk.hg_hi[:, h, :], wk.hg_lo[:, h, :]),
                False, True).then_inc(wk.out_done, 1)

    base(0)
    turn_gates(0)
    experts(0)
    turn_gates(1)
    base(1)
    experts(1)


def layer_gated_vector(dve, k, h, ps, wk):
    dve.wait_ge(wk.hid_copied, 2 * k + h + 1)
    dve.wait_ge(wk.gates_turned, 2 * k + h + 1)
    if k:
        dve.wait_ge(wk.out_done, 8 * k)
    dve.tensor_tensor(wk.hg[:, h, :], wk.hid[:, h, :], ps[:, 6, :], ALU.mult).then_inc(wk.gated, 1)
    dve.wait_ge(wk.gated_hi, 2 * k + h + 1)
    dve.tensor_tensor(wk.hg_lo[:, h, :], wk.hg[:, h, :], wk.hg_hi[:, h, :].bitcast(F32), ALU.subtract).then_inc(wk.gated_lo, 1)


def layer_hidden_scalar(act, k, ps, wk):
    for h in range(2):
        act.wait_ge(wk.hid_done, 2 * k + h + 1)
        if k:
            act.wait_ge(wk.gated, 2 * k)
        act.activation(wk.hid[:, h, :], ps[:, 4 + h, :], ACT.Copy).then_inc(wk.hid_copied, 1)


def layer_gated_scalar(act, k, h, wk):
    act.wait_ge(wk.gated, 2 * k + h + 1)
    act.activation(wk.hg_hi[:, h, :], wk.hg[:, h, :], ACT.Copy).then_inc(wk.gated_hi, 1)


def logits_fp32(pe, ps, col, x, route_w, n, done):
    for b in range(SEQS):
        for c in range(CT):
            ins = pe.matmul(ps[:, 7, col + b * n:col + b * n + n], x[:, c, b * P:b * P + P], route_w[:, c, :],
                            start=(c == 0), stop=(c == CT - 1))
    ins.then_inc(done, 1)


def bcast(ap, shape, at):
    return ap.unsqueeze(at).broadcast_to(shape)


def top2_gates(dve, link, lg, iota, buf, exp_wait, exp_in, gate_scale):
    for b in range(SEQS):
        ins = dve.max(buf["best"][:, b, :], lg[:, b, :])
    link(ins)
    for b in range(SEQS):
        ins = dve.max_index(buf["where"][:, b, :], buf["best"][:, b, :], lg[:, b, :])
    link(ins)
    best, where_f, sm = buf["best"], buf["where_f"], buf["small"]
    link(dve.tensor_copy(where_f[:, :, :], buf["where"][:, :, :]))
    dve.tensor_tensor(sm[:, 0, :], best[:, :, 1], best[:, :, 0], ALU.subtract).then_inc(exp_in, 1)
    shape = [P, SEQS, EXP]
    for c in range(2):
        link(dve.tensor_tensor(buf["hot"][:, :, c, :], bcast(iota, shape, 1),
                               where_f[:, :, c:c + 1].broadcast_to(shape), ALU.is_equal))
    exp_wait()
    link(dve.tensor_scalar(sm[:, 2, :], sm[:, 1, :], 1.0, None, ALU.add))
    link(dve.reciprocal(sm[:, 3, :], sm[:, 2, :]))
    link(dve.tensor_scalar(sm[:, 4, :], sm[:, 3, :], gate_scale, None, ALU.mult))
    link(dve.tensor_tensor(sm[:, 5, :], sm[:, 4, :], sm[:, 1, :], ALU.mult))
    for c in range(2):
        link(dve.tensor_tensor(buf["hot_g"][:, :, c, :], buf["hot"][:, :, c, :], bcast(sm[:, 4 + c, :], shape, 2), ALU.mult))


def top2_buffers(sb, name):
    return dict(best=sb(name + "_best", [P, SEQS, 8]), where=sb(name + "_where", [P, SEQS, 8], U32),
                where_f=sb(name + "_where_f", [P, SEQS, 8]), hot=sb(name + "_hot", [P, SEQS, 2, EXP]),
                hot_g=sb(name + "_hot_g", [P, SEQS, 2, EXP]), small=sb(name + "_small", [P, 6, SEQS]))


def widen_gates(dve, wk):
    dve.tensor_copy(wk.gate_wide[:, :, :].rearrange("p b (e r) -> p b e r", r=RANK),
                    wk.gate[:, :, :].unsqueeze(3).broadcast_to([P, SEQS, EXP, RANK])).then_inc(wk.gates_wide, 1)


def first_block(nc, t, ps, cst, x1_split, x1_whole):
    ident, iota = cst[:, C_ID:C_ID + P], cst[:, C_IOTA:C_IOTA + EXP]
    with ExitStack() as ctx:
        sb = lambda n, s, d=F32: ctx.enter_context(nc.sbuf_tensor(n, s, d))
        sem = lambda n: ctx.enter_context(nc.semaphore(n))
        x = sb("x", [P, CT, TOK])
        x_hi, x_lo = sb("x_hi", [P, CT, TOK], F32R), sb("x_lo", [P, CT, TOK], F32R)
        y = sb("y", [P, CT, TOK])
        y_hi, y_lo = sb("y_hi", [P, CT, TOK], F32R), sb("y_lo", [P, CT, TOK], F32R)
        raw_w = sb("raw_w", [P, CT, DM + P])
        raw_b = sb("raw_b", [P, DM])
        L = [Layer(sb, "cond0", EXP), Layer(sb, "ffn0", NR1)]
        wk = Work(sb, sem, "b0")
        lang, lang_f = sb("lang", [P, SEQS], I32), sb("lang_f", [P, SEQS])
        base_b, route_b = sb("base_b", [P, CT]), sb("route_b", [P, NR1])
        emap, emap_f = sb("emap", [P, NR1], I32), sb("emap_f", [P, NR1])
        onehot = sb("onehot", [P, EXP, NR1])
        lg0, bias0 = sb("lg0", [P, SEQS, EXP]), sb("bias0", [P, SEQS, EXP])
        t2 = top2_buffers(sb, "t2")
        lg1, pr1, rest1 = (sb(n, [P, SEQS, NR1]) for n in ("lg1", "pr1", "rest1"))
        st1 = sb("st1", [P, 3, SEQS])
        best1 = sb("best1", [P, SEQS, 8])
        spread = sb("spread", [P, SEQS, EXP, NR1])
        s_x, s_w, s_small = [sem("x_in0"), sem("x_in1")], [sem("w_in0"), sem("w_in1")], sem("small_in")
        x_hi_done, w_hi_done, chain, exp_in, exp_out, stored = (
            sem(n) for n in ("x_hi_done", "w_hi_done", "chain", "exp_in", "exp_out", "stored"))
        block = ctx.enter_context(nc.Block())

        @block.sync
        def _(sp):
            for h in range(2):
                sp.dma_start(x[:, :, halves(h)], t["x"][:, :, halves(h)]).then_inc(s_x[h], 16)
            for dst, src in ((L[0].route_w[:, :, :], t["cond0_route"]), (L[1].route_w[:, :, :], t["ffn0_route"]),
                             (lang[:, :], t["lang"]), (base_b[:, :], t["ffn0_b"]), (route_b[:, :], t["ffn0_route_b"]),
                             (emap[:, :], t["emap"])):
                sp.dma_start(dst, src).then_inc(s_small, 16)
            for k in range(2):
                if k:
                    sp.wait_ge(wk.split_w, 2)
                sp.dma_start(raw_w[:, :, :], t[L[k].name + "_w"]).then_inc(s_w[k], 16)
                sp.dma_start(raw_b[:, :], t[L[k].name + "_lb"]).then_inc(s_w[k], 16)
            for h in range(2):
                sp.wait_ge(wk.inputs_ready, 5 + h)
                sp.dma_start(x1_whole[:, :, halves(h)], x[:, :, halves(h)]).then_inc(stored, 16)
                for b in range(4 * h, 4 * h + 4):
                    for j, part in enumerate((x_hi, x_lo)):
                        sp.dma_start(x1_split[b, :, j * DM:(j + 1) * DM].rearrange("p (c n) -> p c n", c=CT),
                                     part[:, :, b * P:b * P + P].bitcast(F32)).then_inc(stored, 16)
            sp.wait_ge(stored, 16 * 18)

        @block.gpsimd
        def _(pool):
            for k in range(2):
                pool.wait_ge(w_hi_done, 2 * k + 1)
                pool.tensor_tensor(L[k].w_lo[:, :, :], raw_w[:, :, :], L[k].w_hi[:, :, :].bitcast(F32), ALU.subtract).then_inc(wk.split_w, 1)
                pool.wait_ge(w_hi_done, 2 * k + 2)
                pool.tensor_tensor(L[k].b_lo[:, :], raw_b[:, :], L[k].b_hi[:, :].bitcast(F32), ALU.subtract).then_inc(wk.split_w, 1)

        @block.scalar
        def _(act):
            def split_weights(k):
                act.wait_ge(s_w[k], 32)
                act.activation(L[k].w_hi[:, :, :], raw_w[:, :, :], ACT.Copy).then_inc(w_hi_done, 1)
                act.activation(L[k].b_hi[:, :], raw_b[:, :], ACT.Copy).then_inc(w_hi_done, 1)

            for h in range(2):
                act.wait_ge(s_x[h], 16)
                act.activation(x_hi[:, :, halves(h)], x[:, :, halves(h)], ACT.Copy).then_inc(x_hi_done, 1)
            split_weights(0)
            split_weights(1)
            for k in range(2):
                act.wait_ge(exp_in, k + 1)
                if k == 0:
                    act.activation(t2["small"][:, 1, :], t2["small"][:, 0, :], ACT.Exp).then_inc(exp_out, 1)
                else:
                    act.activation(pr1[:, :, :], lg1[:, :, :], ACT.Exp).then_inc(exp_out, 1)
                layer_hidden_scalar(act, k, ps, wk)
                for h in range(2):
                    layer_gated_scalar(act, k, h, wk)
                    for o in range(CT):
                        if k == 0:
                            act.wait_ge(wk.out_done, 4 * h + o + 1)
                            act.activation(y[:, o, halves(h)], ps[:, o, :], ACT.Copy)
                            act.activation(y_hi[:, o, halves(h)], ps[:, o, :], ACT.Copy).then_inc(wk.bank_free, 1)
                        else:
                            act.wait_ge(wk.bank_free, 8 + 4 * h + o + 1)
                            act.activation(x_hi[:, o, halves(h)], x[:, o, halves(h)], ACT.Copy).then_inc(wk.out_hi, 1)

        @block.vector
        def _(dve):
            n = [0]

            def link(ins):
                n[0] += 1
                ins.then_inc(chain, 1)
                dve.wait_ge(chain, n[0])

            for h in range(2):
                dve.wait_ge(x_hi_done, h + 1)
                dve.tensor_tensor(x_lo[:, :, halves(h)], x[:, :, halves(h)], x_hi[:, :, halves(h)].bitcast(F32),
                                  ALU.subtract).then_inc(wk.inputs_ready, 1)
            dve.wait_ge(s_small, 96)
            link(dve.tensor_copy(lang_f[:, :], lang[:, :]))
            shape = [P, SEQS, EXP]
            link(dve.tensor_tensor(bias0[:, :, :], bcast(iota, shape, 1), bcast(lang_f[:, :], shape, 2), ALU.is_equal))
            link(dve.tensor_copy(emap_f[:, :], emap[:, :]))
            hot_shape = [P, EXP, NR1]
            link(dve.tensor_tensor(onehot[:, :, :], bcast(iota, hot_shape, 2), bcast(emap_f[:, :], hot_shape, 1), ALU.is_equal))
            dve.wait_ge(wk.logits_done, 1)
            link(dve.scalar_tensor_tensor(out=lg0[:, :, :], in0=bias0[:, :, :], scalar=5.0,
                                          in1=ps[:, 7, 0:SEQS * EXP].rearrange("p (b e) -> p b e", b=SEQS),
                                          op0=ALU.mult, op1=ALU.add))
            top2_gates(dve, link, lg0, iota, t2, lambda: dve.wait_ge(exp_out, 1), exp_in, 2.0)
            link(dve.tensor_tensor(wk.gate[:, :, :], t2["hot_g"][:, :, 0, :], t2["hot_g"][:, :, 1, :], ALU.add))
            widen_gates(dve, wk)
            for h in range(2):
                layer_gated_vector(dve, 0, h, ps, wk)
                for o in range(CT):
                    dve.wait_ge(wk.bank_free, 4 * h + o + 1)
                    ins = dve.tensor_tensor(y_lo[:, o, halves(h)], y[:, o, halves(h)], y_hi[:, o, halves(h)].bitcast(F32), ALU.subtract)
                ins.then_inc(wk.inputs_ready, 1)
            dve.wait_ge(wk.logits_done, 2)
            lshape = [P, SEQS, NR1]
            link(dve.tensor_tensor(lg1[:, :, :], ps[:, 7, 0:SEQS * NR1].rearrange("p (b e) -> p b e", b=SEQS),
                                   bcast(route_b[:, :], lshape, 1), ALU.add))
            link(dve.tensor_reduce(st1[:, 0, :], lg1[:, :, :], AX.X, ALU.max))
            dve.tensor_tensor(lg1[:, :, :], lg1[:, :, :], bcast(st1[:, 0, :], lshape, 2), ALU.subtract).then_inc(exp_in, 1)
            dve.wait_ge(exp_out, 2)
            link(dve.tensor_reduce(st1[:, 1, :], pr1[:, :, :], AX.X, ALU.add))
            link(dve.reciprocal(st1[:, 2, :], st1[:, 1, :]))
            link(dve.tensor_tensor(pr1[:, :, :], pr1[:, :, :], bcast(st1[:, 2, :], lshape, 2), ALU.mult))
            for b in range(SEQS):
                ins = dve.max(best1[:, b, :], pr1[:, b, :])
            link(ins)
            for b in range(SEQS):
                ins = dve.match_replace(rest1[:, b, :], best1[:, b, :], pr1[:, b, :], 0.0)
            link(ins)
            link(dve.tensor_tensor(pr1[:, :, :], pr1[:, :, :], rest1[:, :, :], ALU.subtract))
            wide = [P, SEQS, EXP, NR1]
            link(dve.tensor_tensor(spread[:, :, :, :], pr1[:, :, :].unsqueeze(2).broadcast_to(wide),
                                   onehot[:, :, :].unsqueeze(1).broadcast_to(wide), ALU.mult))
            link(dve.tensor_reduce(wk.gate[:, :, :], spread[:, :, :, :], AX.X, ALU.add))
            link(dve.tensor_scalar(wk.gate[:, :, :], wk.gate[:, :, :], 2.0, None, ALU.mult))
            dve.wait_ge(wk.gates_turned, 2)
            widen_gates(dve, wk)
            for h in range(2):
                layer_gated_vector(dve, 1, h, ps, wk)
                for o in range(CT):
                    dve.wait_ge(wk.out_done, 8 + 4 * h + o + 1)
                    dve.scalar_tensor_tensor(out=x[:, o, halves(h)], in0=ps[:, o, :], scalar=base_b[:, o:o + 1],
                                             in1=x[:, o, halves(h)], op0=ALU.add, op1=ALU.add).then_inc(wk.bank_free, 1)
                for o in range(CT):
                    dve.wait_ge(wk.out_hi, 4 * h + o + 1)
                    ins = dve.tensor_tensor(x_lo[:, o, halves(h)], x[:, o, halves(h)], x_hi[:, o, halves(h)].bitcast(F32), ALU.subtract)
                ins.then_inc(wk.inputs_ready, 1)

        @block.tensor
        def _(pe):
            pe.wait_ge(s_small, 96)
            pe.wait_ge(s_x[1], 16)
            layer_tensor(pe, 0, ps, ident, x, x_hi, x_lo, L[0], wk,
                         lambda pe: logits_fp32(pe, ps, 0, x, L[0].route_w, EXP, wk.logits_done))
            layer_tensor(pe, 1, ps, ident, y, y_hi, y_lo, L[1], wk,
                         lambda pe: logits_fp32(pe, ps, 0, y, L[1].route_w, NR1, wk.logits_done))


BANK_S, BANK_T, BANK_O, BANK_P = 0, 4, 6, 7
SPARE = slice(KEYS // 2, KEYS // 2 + P)


def attention(nc, t, ps, cst, x1_split, rope_tab, mask_tab, att):
    ident = cst[:, C_ID:C_ID + P]
    with ExitStack() as ctx:
        sb = lambda n, s, d=F32: ctx.enter_context(nc.sbuf_tensor(n, s, d))
        sem = lambda n: ctx.enter_context(nc.semaphore(n))
        pair = lambda n, s, d=F32: [sb(f"{n}{p}", s, d) for p in range(2)]
        w_hi, w_lo = sb("w_hi", [P, 2 * GW], F32R), sb("w_lo", [P, 2 * GW], F32R)
        w_raw = pair("w_raw", [P, CHUNK])
        xs = pair("xs", [P, 2 * DM], F32R)
        rope = pair("rope", [P, 4 * P])
        mask = pair("mask", [P, KEYS])
        kv = pair("kv", [P, KT + 1, 2 * P])
        page_row = sb("page_row", [P, SEQS * KT], I32)
        page_in, row_of, head_no = sb("page_in", [P, SEQS * KT], I32), sb("row_of", [P, SEQS * KT], I32), sb("head_no", [P, KVH * KT], I32)
        rows = pair("rows", [P, KT], I32)
        q_raw, q_a, q_b = sb("q_raw", [P, QPK * P]), sb("q_a", [P, QPK * P]), sb("q_b", [P, QPK * P])
        k_a, k_b = sb("k_a", [P, P]), sb("k_b", [P, P])
        sq = sb("sq", [P, (QPK + 1) * P])
        ssq_q, ssq_k = sb("ssq_q", [P, QPK]), sb("ssq_k", [P, 1])
        rms_q, rms_k = sb("rms_q", [P, QPK]), sb("rms_k", [P, 1])
        minus_half = sb("minus_half", [P, QPK])
        r_q, neg_r_q = pair("r_q", [P, QPK]), pair("neg_r_q", [P, QPK])
        qt_hi, qt_lo = sb("qt_hi", [P, QPK * P], F32R), sb("qt_lo", [P, QPK * P], F32R)
        kt_hi, kt_lo = sb("kt_hi", [P, KEYS], F32R), sb("kt_lo", [P, KEYS], F32R)
        v_hi, v_lo = pair("v_hi", [P, KT + 1, P], F32R), pair("v_lo", [P, KT + 1, P], F32R)
        prob = pair("prob", [P, QPK, KEYS])
        top, neg_top = sb("top", [P, QPK]), sb("neg_top", [P, QPK])
        den, inv = sb("den", [P, QPK]), sb("inv", [P, QPK])
        pt_hi, pt_lo = pair("pt_hi", [P, DM], F32R), pair("pt_lo", [P, DM], F32R)
        ot_hi, ot_lo = sb("ot_hi", [P, DM], F32R), sb("ot_lo", [P, DM], F32R)

        w_in, x_in, mask_in, kv_in = ([sem(f"{n}{p}") for p in range(2)] for n in ("w_in", "x_in", "mask_in", "kv_in"))
        pages_in = sem("pages_in")
        q_done, kv_done, s_done, turned, kn_turned, pv_done, o_done = (
            sem(n) for n in ("q_done", "kv_done", "s_done", "turned", "kn_turned", "pv_done", "o_done"))
        q_copied, kv_copied, q_squared, k_squared, expd, normed_1, hi_done, kn_hi_done, v_hi_done, w_hi_done, o_hi_done = (
            sem(n) for n in ("q_copied", "kv_copied", "q_squared", "k_squared", "expd", "normed_1", "hi_done", "kn_hi_done", "v_hi_done", "w_hi_done", "o_hi_done"))
        lo_done, kn_lo_done, maxed, biased, inverted, normed, q_scaled, q_cos, k_cos, k_roped, o_lo_done, summed, cleared = (
            sem(n) for n in ("lo_done", "kn_lo_done", "maxed", "biased", "inverted", "normed", "q_scaled", "q_cos", "k_cos",
                             "k_roped", "o_lo_done", "summed", "cleared"))
        q_sin, q_roped, k_sin, q_mean, q_rms, k_mean, k_rms, v_lo_done, w_lo_done, rows_done, setup = (
            sem(n) for n in ("q_sin", "q_roped", "k_sin", "q_mean", "q_rms", "k_mean", "k_rms", "v_lo_done", "w_lo_done", "rows_done", "setup"))
        dve_held, pool_held = sem("dve_held"), sem("pool_held")
        block = ctx.enter_context(nc.Block())

        def held(eng, sem):
            eng.sem_inc(sem, 1)

        def run(eng, body):
            body(Step(-1), False, False, True)
            body(Step(0), False, True, True)
            with eng.Fori(0, (STEPS - 4) // 2) as trip:
                body(Step(1, trip), True, True, True)
                body(Step(2, trip), True, True, True)
            body(Step(STEPS - 3), True, True, True)
            body(Step(STEPS - 2), True, True, True)
            body(Step(STEPS - 1), True, True, False)
            body(Step(STEPS), True, False, False)

        @block.sync
        def _(sp):
            def load_w(w):
                sp.dma_start(w_raw[w.parity][:, :], t["att_w"][ds(w.times(1) % STEPS, 1), :, :].rearrange("a p n -> (a p) n")).then_inc(w_in[w.parity], 16)

            def load_x(m):
                b = m.times(1) % SEQS
                sp.dma_start(xs[m.parity][:, :].bitcast(F32), x1_split[ds(b, 1), :, :].rearrange("a p n -> (a p) n")).then_inc(x_in[m.parity], 16)
                sp.dma_start(rope[m.parity][:, :], rope_tab[ds(b, 1), :, :].rearrange("a p n -> (a p) n")).then_inc(x_in[m.parity], 16)

            def load_mask(m):
                sp.dma_start(mask[m.parity][:, :], mask_tab[ds(m.times(1) % SEQS, 1), :, :].rearrange("a p n -> (a p) n")).then_inc(mask_in[m.parity], 16)

            sp.dma_start(page_in[:, :], t["pages"]).then_inc(pages_in, 16)
            sp.dma_start(row_of[:, :], t["row_of"]).then_inc(pages_in, 16)
            sp.dma_start(head_no[:, :], t["head_no"]).then_inc(pages_in, 16)
            load_w(Step(0))
            load_w(Step(1))
            load_x(Step(0))
            for w in range(2, SEQS):
                sp.wait_ge(w_lo_done, w - 1)
                load_w(Step(w))

            def body(i, prev, cur, nxt):
                w, m = i.plus(9), i.plus(2)
                if not nxt:
                    return
                if not (isinstance(i.trip, int) and i.off == STEPS - 2):
                    sp.wait_ge(w_lo_done, w.times(1, -1))
                    load_w(w)
                if not m.first and not (isinstance(m.trip, int) and m.off in (1,)):
                    sp.wait_ge(kv_done, m.times(1, -1))
                    sp.wait_ge(k_roped, m.times(1, -1))
                if not (isinstance(i.trip, int) and i.off == STEPS - 2):
                    load_x(m)
                k = i.plus(1)
                if not isinstance(k.trip, int) or k.off >= 2:
                    sp.wait_ge(maxed, k.times(4, -4))
                load_mask(k)

            run(sp, body)

        @block.gpsimd
        def _(pool):
            pool.wait_ge(pages_in, 48)
            pool.tensor_scalar(page_row[:, :], page_in[:, :], PSIZE * KVH, None, ALU.mult).then_inc(setup, 1)
            pool.wait_ge(setup, 1)
            pool.tensor_tensor(page_row[:, :], page_row[:, :], row_of[:, :], ALU.add).then_inc(setup, 1)
            pool.wait_ge(setup, 2)
            pool.memset(minus_half[:, :], -0.5).then_inc(setup, 1)
            pool.wait_ge(setup, 3)

            def gather(m, tiles):
                p = m.parity
                if tiles[0] == 0:
                    pool.tensor_tensor(rows[p][:, :], page_row[:, ds((m.times(1) % SEQS) * KT, KT)],
                                       head_no[:, ds((m.times(1) // SEQS) * KT, KT)], ALU.add).then_inc(rows_done, 1)
                    pool.wait_ge(rows_done, m.times(1, 1))
                    held(pool, pool_held)
                for j in tiles:
                    pool.indirect_dma_start(kv[p][:, j, :], None, t["kv"],
                                            bass.IndirectOffsetOnAxis(ap=rows[p][:, j:j + 1], axis=0)).then_inc(kv_in[p], 16)

            def split_w(w):
                p = w.parity
                at = ((w.times(1) // SEQS) % 2) * GW + (w.times(1) % SEQS) * CHUNK
                pool.wait_ge(w_hi_done, w.times(1, 1))
                pool.tensor_tensor(w_lo[:, ds(at, CHUNK)], w_raw[p][:, :], w_hi[:, ds(at, CHUNK)].bitcast(F32), ALU.subtract).then_inc(w_lo_done, 1)

            gather(Step(0), range(KT))
            for w in range(SEQS):
                split_w(Step(w))

            def body(i, prev, cur, nxt):
                n, m = i.plus(1), i.plus(2)
                more = nxt and not (isinstance(i.trip, int) and i.off >= STEPS - 2)
                if cur and nxt:
                    split_w(i.plus(SEQS))
                if nxt:
                    pool.wait_ge(q_copied, n.times(1, 1))
                    if not n.first:
                        pool.wait_ge(q_roped, n.times(1))
                    sine = rope[n.parity][:, P:2 * P].unsqueeze(1).broadcast_to([P, QPK, P])
                    pool.wait_ge(x_in[n.parity], n.half(1) * 32)
                    pool.tensor_tensor(q_b[:, :].rearrange("p (h d) -> p h d", h=QPK), q_raw[:, :].rearrange("p (h d) -> p h d", h=QPK),
                                       sine, ALU.mult).then_inc(q_sin, 1)
                    pool.wait_ge(q_sin, n.times(1, 1))
                    pool.wait_ge(q_cos, n.times(1, 1))
                    by_half = [ap.rearrange("p (h s d) -> p h s d", h=QPK, s=2) for ap in (q_a[:, :], q_b[:, :])]
                    for s in range(2):
                        ins = pool.tensor_tensor(by_half[0][:, :, s, :], by_half[0][:, :, s, :], by_half[1][:, :, 1 - s, :], ALU.add)
                    ins.then_inc(q_roped, 1)
                if cur:
                    pool.wait_ge(v_hi_done, i.times(1, 1))
                    if i.off >= 2 or not isinstance(i.trip, int):
                        pool.wait_ge(pv_done, i.times(5, -5))
                    pool.tensor_tensor(v_lo[i.parity][:, :, :], kv[i.parity][:, :, P:2 * P], v_hi[i.parity][:, :, :].bitcast(F32),
                                       ALU.subtract).then_inc(v_lo_done, 1)
                if more:
                    if cur:
                        pool.wait_ge(v_lo_done, i.times(1, 1))
                        pool.wait_ge(turned, turn_no(i.plus(-1), "kc") + 1)
                        pool.wait_ge(k_roped, i.times(1, 1))
                    gather(m, range(KT - 1))
                if nxt:
                    pool.wait_ge(k_squared, n.times(1, 1))
                    if not n.first:
                        pool.wait_ge(k_roped, n.times(1))
                    held(pool, pool_held)
                    pool.tensor_scalar(rms_k[:, :], ssq_k[:, :], 1.0 / P, 1e-6, ALU.mult, ALU.add).then_inc(k_mean, 1)
                    pool.wait_ge(k_mean, n.times(1, 1))
                    pool.tensor_tensor(rms_k[:, :], rms_k[:, :], minus_half[:, 0:1], ALU.pow).then_inc(k_rms, 1)
                    pool.tensor_tensor(k_b[:, :], kv[n.parity][:, KT, 0:P], rope[n.parity][:, 3 * P:4 * P], ALU.mult).then_inc(k_sin, 1)
                if nxt:
                    pool.wait_ge(q_squared, n.times(1, 1))
                    if not n.first:
                        pool.wait_ge(q_scaled, n.times(1))
                    held(pool, pool_held)
                    pool.tensor_scalar(rms_q[:, :], ssq_q[:, :], 1.0 / P, 1e-6, ALU.mult, ALU.add).then_inc(q_mean, 1)
                    pool.wait_ge(q_mean, n.times(1, 1))
                    pool.tensor_tensor(rms_q[:, :], rms_q[:, :], minus_half[:, :], ALU.pow).then_inc(q_rms, 1)
                if more:
                    gather(m, range(KT - 1, KT))

            run(pool, body)

        @block.scalar
        def _(act):
            def split_w(w):
                p = w.parity
                at = ((w.times(1) // SEQS) % 2) * GW + (w.times(1) % SEQS) * CHUNK
                act.wait_ge(w_in[p], w.half(1) * 16)
                act.activation(w_hi[:, ds(at, CHUNK)], w_raw[p][:, :], ACT.Copy).then_inc(w_hi_done, 1)

            for w in range(SEQS):
                split_w(Step(w))

            def hi(i, name, out, width):
                no = turn_no(i, name)
                act.wait_ge(turned, no + 1)
                bank = turn_bank(i, name)
                act.activation(out, ps[:, bank, 0:width], ACT.Copy).then_inc(hi_done, 1)

            def softmax_exp(i, h):
                act.wait_ge(biased, i.times(4, h + 1))
                act.activation(prob[i.parity][:, h, :], prob[i.parity][:, h, :], ACT.Exp, bias=neg_top[:, h:h + 1],
                               scale=r_q[i.parity][:, h:h + 1], accum_out=den[:, h:h + 1]).then_inc(expd, 1)

            def body(i, prev, cur, nxt):
                n = i.plus(1)
                if cur and nxt:
                    act.wait_ge(kv_done, i.times(1))
                    if prev and not (isinstance(i.trip, int) and i.off == 1):
                        act.wait_ge(o_done, i.times(1, -1))
                    split_w(i.plus(SEQS))
                if prev:
                    hi(i, 1, pt_hi[1][:, :], DM)
                if cur:
                    softmax_exp(i, 0)
                if nxt:
                    act.wait_ge(q_done, n.times(1, 1))
                    if not n.first:
                        act.wait_ge(q_sin, n.times(1))
                        act.wait_ge(q_cos, n.times(1))
                        act.wait_ge(q_squared, n.times(1))
                    act.activation(q_raw[:, :], ps[:, BANK_P, :], ACT.Copy).then_inc(q_copied, 1)
                if prev:
                    hi(i, 2, pt_hi[0][:, :], DM)
                if cur:
                    act.wait_ge(kv_in[i.parity], i.half(1) * 16 * KT)
                    act.wait_ge(kv_copied, i.times(1, 1))
                    if i.off >= 2 or not isinstance(i.trip, int):
                        act.wait_ge(pv_done, i.times(5, -5))
                    act.activation(v_hi[i.parity][:, :, :], kv[i.parity][:, :, P:2 * P], ACT.Copy).then_inc(v_hi_done, 1)
                if prev:
                    hi(i, 3, pt_hi[1][:, :], DM)
                if cur:
                    softmax_exp(i, 1)
                if prev:
                    hi(i, 4, pt_hi[0][:, :], DM)
                if cur:
                    softmax_exp(i, 2)
                    act.wait_ge(inverted, i.times(4, 2))
                    act.activation(prob[i.parity][:, 1, :], prob[i.parity][:, 1, :], ACT.Copy, scale=inv[:, 1:2]).then_inc(normed_1, 1)
                    softmax_exp(i, 3)
                if nxt:
                    act.wait_ge(kv_done, n.times(1, 1))
                    if i.off >= 1 or not isinstance(i.trip, int):
                        act.wait_ge(v_lo_done, n.times(1, -1))
                        act.wait_ge(k_rms, n.times(1))
                        act.wait_ge(k_squared, n.times(1))
                    act.activation(kv[n.parity][:, KT, :], ps[:, BANK_P, 0:2 * P], ACT.Copy).then_inc(kv_copied, 1)
                    hi(i, "kc", kt_hi[:, 0:CACHE], CACHE)
                if prev:
                    act.wait_ge(pv_done, i.times(5, 0))
                    act.activation(ot_hi[:, :], ps[:, BANK_O, :], ACT.Copy).then_inc(o_hi_done, 1)
                if nxt:
                    act.wait_ge(kv_copied, n.times(1, 1))
                    act.activation(sq[:, QPK * P:], kv[n.parity][:, KT, 0:P], ACT.Square, accum_out=ssq_k[:, 0:1]).then_inc(k_squared, 1)
                    hi(i, "q", qt_hi[:, :], DM)
                if cur:
                    hi(n, 0, pt_hi[0][:, :], DM)
                if nxt:
                    act.wait_ge(q_copied, n.times(1, 1))
                    if not n.first:
                        act.wait_ge(q_rms, n.times(1))
                    for h in range(QPK):
                        ins = act.activation(sq[:, h * P:h * P + P], q_raw[:, h * P:h * P + P], ACT.Square, accum_out=ssq_q[:, h:h + 1])
                    ins.then_inc(q_squared, 1)
                    act.wait_ge(kn_turned, n.times(1, 1))
                    act.activation(kt_hi[:, CACHE:KEYS], ps[:, BANK_S, SPARE], ACT.Copy).then_inc(kn_hi_done, 1)

            run(act, body)

        @block.vector
        def _(dve):
            dve.memset(att[:, :, :], 0.0).then_inc(cleared, 1)

            def lo(i, name, out, width, hi_part):
                no = turn_no(i, name)
                dve.wait_ge(hi_done, no + 1)
                bank = turn_bank(i, name)
                dve.tensor_tensor(out, ps[:, bank, 0:width], hi_part.bitcast(F32), ALU.subtract).then_inc(lo_done, 1)

            def masked_max(i, h):
                p = i.parity
                if h == 0:
                    dve.wait_ge(mask_in[p], i.half(1) * 16)
                    dve.wait_ge(q_scaled, i.times(1, 1))
                dve.wait_ge(s_done, i.times(4, h + 1))
                held(dve, dve_held)
                dve.tensor_tensor_reduce(prob[p][:, h, :].rearrange("p (a k) -> p a k", a=2),
                                         ps[:, BANK_S + 2 * (h % 2):BANK_S + 2 * (h % 2) + 2, 0:KEYS // 2],
                                         mask[p][:, :].rearrange("p (a k) -> p a k", a=2), 1.0, -3.0e38, ALU.add, ALU.max,
                                         top[:, h:h + 1]).then_inc(maxed, 1)
                dve.wait_ge(maxed, i.times(4, h + 1))
                if not i.first:
                    dve.wait_ge(expd, i.times(4, h - 3))
                dve.tensor_tensor(neg_top[:, h:h + 1], top[:, h:h + 1], neg_r_q[p][:, h:h + 1], ALU.mult).then_inc(biased, 1)

            def invert(i, h):
                dve.wait_ge(expd, i.times(4, h + 1))
                if not i.first:
                    dve.wait_ge(normed_1, i.times(1))
                dve.reciprocal(inv[:, h:h + 1], den[:, h:h + 1]).then_inc(inverted, 1)

            def normalise(i, h):
                p = i.parity
                invert(i, h)
                dve.wait_ge(inverted, i.times(4, h + 1))
                dve.tensor_scalar(prob[p][:, h, :], prob[p][:, h, :], inv[:, h:h + 1], None, ALU.mult).then_inc(normed, 1)

            def body(i, prev, cur, nxt):
                n = i.plus(1)
                if prev:
                    lo(i, 1, pt_lo[1][:, :], DM, pt_hi[1][:, :])
                if cur:
                    masked_max(i, 0)
                    normalise(i, 0)
                if nxt:
                    dve.wait_ge(q_copied, n.times(1, 1))
                    dve.wait_ge(x_in[n.parity], n.half(1) * 32)
                    if not n.first:
                        dve.wait_ge(turned, turn_no(i.plus(-1), "q") + 1)
                    cosine = rope[n.parity][:, 0:P].unsqueeze(1).broadcast_to([P, QPK, P])
                    dve.tensor_tensor(q_a[:, :].rearrange("p (h d) -> p h d", h=QPK), q_raw[:, :].rearrange("p (h d) -> p h d", h=QPK),
                                      cosine, ALU.mult).then_inc(q_cos, 1)
                if cur:
                    masked_max(i, 1)
                if prev:
                    lo(i, 2, pt_lo[0][:, :], DM, pt_hi[0][:, :])
                    lo(i, 3, pt_lo[1][:, :], DM, pt_hi[1][:, :])
                if cur:
                    masked_max(i, 2)
                    invert(i, 1)
                if cur:
                    masked_max(i, 3)
                if prev:
                    lo(i, 4, pt_lo[0][:, :], DM, pt_hi[0][:, :])
                if cur:
                    normalise(i, 2)
                    normalise(i, 3)
                if nxt:
                    lo(i, "kc", kt_lo[:, 0:CACHE], CACHE, kt_hi[:, 0:CACHE])
                if prev:
                    dve.wait_ge(o_hi_done, i.times(1, 0))
                    dve.tensor_tensor(ot_lo[:, :], ps[:, BANK_O, :], ot_hi[:, :].bitcast(F32), ALU.subtract).then_inc(o_lo_done, 1)
                if nxt:
                    dve.wait_ge(k_rms, n.times(1, 1))
                    if not n.first:
                        dve.wait_ge(kn_turned, n.times(1))
                    dve.scalar_tensor_tensor(out=k_a[:, :], in0=kv[n.parity][:, KT, 0:P], scalar=rms_k[:, 0:1],
                                             in1=rope[n.parity][:, 2 * P:3 * P], op0=ALU.mult, op1=ALU.mult).then_inc(k_cos, 1)
                    dve.wait_ge(k_cos, n.times(1, 1))
                    dve.wait_ge(k_sin, n.times(1, 1))
                    dve.scalar_tensor_tensor(out=k_a[:, 0:64], in0=k_b[:, 64:P], scalar=rms_k[:, 0:1], in1=k_a[:, 0:64],
                                             op0=ALU.mult, op1=ALU.add)
                    dve.scalar_tensor_tensor(out=k_a[:, 64:P], in0=k_b[:, 0:64], scalar=rms_k[:, 0:1], in1=k_a[:, 64:P],
                                             op0=ALU.mult, op1=ALU.add).then_inc(k_roped, 1)
                    lo(i, "q", qt_lo[:, :], DM, qt_hi[:, :])
                if cur:
                    lo(n, 0, pt_lo[0][:, :], DM, pt_hi[0][:, :])
                if nxt:
                    dve.wait_ge(kn_hi_done, n.times(1, 1))
                    dve.tensor_tensor(kt_lo[:, CACHE:KEYS], ps[:, BANK_S, SPARE], kt_hi[:, CACHE:KEYS].bitcast(F32),
                                      ALU.subtract).then_inc(kn_lo_done, 1)
                if prev:
                    dve.wait_ge(o_done, i.times(1, 0))
                    dve.wait_ge(cleared, 1)
                    if not (isinstance(i.trip, int) and i.off == 1):
                        dve.wait_ge(summed, i.times(1, -1))
                    here = att[:, ds(i.plus(-1).times(1) % SEQS, 1), :].rearrange("p a n -> p (a n)")
                    dve.tensor_tensor(here, ps[:, BANK_P, :], here, ALU.add).then_inc(summed, 1)
                if nxt:
                    dve.wait_ge(q_rms, n.times(1, 1))
                    if i.off >= 1 or not isinstance(i.trip, int):
                        dve.wait_ge(expd, n.times(4, -4))
                    dve.tensor_scalar(r_q[n.parity][:, :], rms_q[:, :], SCALE, None, ALU.mult)
                    dve.tensor_scalar(neg_r_q[n.parity][:, :], rms_q[:, :], -SCALE, None, ALU.mult).then_inc(q_scaled, 1)

            run(dve, body)

        @block.tensor
        def _(pe):
            def group_base(m):
                base = ((m.times(1) // SEQS) % 2) * GW
                return base if isinstance(base, int) else pe.snap(base)

            def project(n, base, at, width, out, done):
                for c in range(CT):
                    x = xs[n.parity][:, c * P:c * P + P], xs[n.parity][:, DM + c * P:DM + c * P + P]
                    w = [part[:, ds(base + (at + c * width), width)] for part in (w_hi, w_lo)]
                    ins = mm3(pe, out, x, w, c == 0, c == CT - 1)
                ins.then_inc(done, 1)

            def turn(i, name, blocks, no_wait=False):
                no = turn_no(i, name)
                if i.first or i.after_last:
                    pe.wait_ge(lo_done, no)
                else:
                    pe.wait_ge(lo_done, no - 1)
                bank = turn_bank(i, name)
                for j, block_ap in enumerate(blocks):
                    ins = pe.transpose(ps[:, bank, j * P:j * P + P], block_ap, ident)
                ins.then_inc(turned, 1)

            def turn_probs(i, j):
                if j == 0:
                    pe.wait_ge(normed, i.times(3, 0))
                    pe.wait_ge(normed_1, i.times(1, 0))
                turn(i, j, [prob[1 - i.parity][:, h, j * P:j * P + P] for h in range(QPK)])

            def scores(i, h):
                if h == 0:
                    pe.wait_ge(lo_done, turn_no(i.plus(-1), "q") + 1)
                    pe.wait_ge(kn_lo_done, i.times(1, 1))
                if not (isinstance(i.trip, int) and i.off == 0 and h < 2):
                    pe.wait_ge(maxed, i.times(4, h - 1))
                q = slice(h * P, h * P + P)
                banks = [(ps[:, BANK_S + 2 * (h % 2) + a, 0:KEYS // 2], slice(a * KEYS // 2, (a + 1) * KEYS // 2)) for a in range(2)]
                for out, k in banks:
                    ins = mm3(pe, out, (qt_hi[:, q], qt_lo[:, q]), (kt_hi[:, k], kt_lo[:, k]), True, True)
                ins.then_inc(s_done, 1)

            def values(i, j):
                v = 1 - i.parity
                if j == 0:
                    pe.wait_ge(v_lo_done, i.times(1, 0))
                    if not (isinstance(i.trip, int) and i.off == 1):
                        pe.wait_ge(o_lo_done, i.times(1, -1))
                pe.wait_ge(lo_done, turn_no(i, j) + 1)
                mm3(pe, ps[:, BANK_O, :], (v_hi[v][:, j, :], v_lo[v][:, j, :]), (pt_hi[j % 2][:, :], pt_lo[j % 2][:, :]),
                    j == 0, j == KT).then_inc(pv_done, 1)

            def output(i, base, heads):
                for h in heads:
                    w = [part[:, ds(base + (QW + KVW + h * DM), DM)] for part in (w_hi, w_lo)]
                    ins = mm3(pe, ps[:, BANK_P, :], (ot_hi[:, h * P:h * P + P], ot_lo[:, h * P:h * P + P]), w, h == 0, h == QPK - 1)
                return ins

            def body(i, prev, cur, nxt):
                n = i.plus(1)
                if nxt:
                    qkv_base = group_base(n)
                if prev:
                    o_base = group_base(i.plus(-1))
                    turn_probs(i, 1)
                if cur:
                    scores(i, 0)
                if nxt:
                    pe.wait_ge(x_in[n.parity], n.half(1) * 32)
                    pe.wait_ge(w_lo_done, i.times(1, 6))
                    if prev and not (isinstance(i.trip, int) and i.off == 1):
                        pe.wait_ge(summed, i.times(1, -1))
                    project(n, qkv_base, 0, DM, ps[:, BANK_P, :], q_done)
                if prev:
                    values(i, 0)
                    turn_probs(i, 2)
                if cur:
                    scores(i, 1)
                if prev:
                    values(i, 1)
                    turn_probs(i, 3)
                if cur:
                    scores(i, 2)
                if prev:
                    values(i, 2)
                    turn_probs(i, 4)
                if cur:
                    scores(i, 3)
                if nxt:
                    pe.wait_ge(q_copied, n.times(1, 1))
                    project(n, qkv_base, QW, 2 * P, ps[:, BANK_P, 0:2 * P], kv_done)
                if prev:
                    values(i, 3)
                if nxt:
                    pe.wait_ge(kv_in[n.parity], n.half(1) * 16 * KT)
                    turn(i, "kc", [kv[n.parity][:, j, 0:P] for j in range(KT)])
                if prev:
                    values(i, 4)
                if nxt:
                    pe.wait_ge(q_roped, n.times(1, 1))
                    turn(i, "q", [q_a[:, h * P:h * P + P] for h in range(QPK)])
                if cur:
                    turn_probs(n, 0)
                if prev:
                    if nxt:
                        pe.wait_ge(kv_copied, n.times(1, 1))
                    elif not cur:
                        pe.wait_ge(summed, i.times(1, -1))
                    pe.wait_ge(w_lo_done, (i.times(1, 7) if nxt else STEPS + SEQS - 1))
                    pe.wait_ge(o_lo_done, i.times(1, 0))
                    output(i, o_base, range(QPK // 2))
                if nxt:
                    pe.wait_ge(k_roped, n.times(1, 1))
                    pe.transpose(ps[:, BANK_S, SPARE], k_a[:, :], ident).then_inc(kn_turned, 1)
                if prev:
                    output(i, o_base, range(QPK // 2, QPK)).then_inc(o_done, 1)

            run(pe, body)


def last_layer(nc, t, ps, cst, ones, x1_whole, att):
    ident, iota = cst[:, C_ID:C_ID + P], cst[:, C_IOTA:C_IOTA + EXP]
    with ExitStack() as ctx:
        sb = lambda n, s, d=F32: ctx.enter_context(nc.sbuf_tensor(n, s, d))
        sem = lambda n: ctx.enter_context(nc.semaphore(n))
        x1 = sb("x1", [P, CT, TOK])
        z = sb("z", [P, CT, TOK])
        z_hi, z_lo = sb("z_hi", [P, CT, TOK], F32R), sb("z_lo", [P, CT, TOK], F32R)
        raw_w, raw_b = sb("raw_w1", [P, CT, DM + P]), sb("raw_b1", [P, DM])
        L = Layer(sb, "ffn1", GH)
        wk = Work(sb, sem, "b1")
        small = sb("small1", [P, 4 * GH + EXP])
        gw2 = sb("gw2", [GH, EXP])
        hid = sb("ghid", [P, SEQS, GH])
        cen = sb("gcen", [P, SEQS, GH])
        st = sb("gst", [P, 4, SEQS])
        hid_t = sb("ghid_t", [GH, SEQS, P])
        lg = sb("glg", [P, SEQS, EXP])
        t2 = top2_buffers(sb, "t3")
        allowed = sb("allowed", [P, 2, EXP])
        s_x1, s_w, s_small = sem("x1_in"), sem("w1_in"), sem("small1_in")
        blk_turned, blk_whole, blk_hi, w_hi_done, chain, exp_in, exp_out, hid_ready, hid_turned, hid_t_done, logits2, hot_ready, counted, out_ready, stored, var_ready, std_ready = (
            sem(n) for n in ("blk_turned", "blk_whole", "blk_hi", "w1_hi_done", "chain1", "exp1_in", "exp1_out", "hid_ready", "hid_turned",
                             "hid_t_done", "logits2", "hot_ready", "counted", "out_ready", "stored1", "var_ready", "std_ready"))
        block = ctx.enter_context(nc.Block())

        @block.sync
        def _(sp):
            sp.dma_start(raw_w[:, :, :], t["ffn1_w"]).then_inc(s_w, 16)
            sp.dma_start(raw_b[:, :], t["ffn1_lb"]).then_inc(s_w, 16)
            sp.dma_start(L.route_w[:, :, :], t["ffn1_route"]).then_inc(s_small, 16)
            sp.dma_start(small[:, :], t["ffn1_small"]).then_inc(s_small, 16)
            sp.dma_start(gw2[:, :], t["ffn1_gw2"]).then_inc(s_small, 16)
            sp.dma_start(x1[:, :, :], x1_whole).then_inc(s_x1, 16)
            for h in range(2):
                for o in range(CT):
                    sp.wait_ge(out_ready, 4 * h + o + 1)
                    sp.dma_start(t["out"][:, o, halves(h)], x1[:, o, halves(h)]).then_inc(stored, 16)
            sp.wait_ge(stored, 16 * 8)

        @block.gpsimd
        def _(pool):
            pool.wait_ge(w_hi_done, 1)
            pool.tensor_tensor(L.w_lo[:, :, :], raw_w[:, :, :], L.w_hi[:, :, :].bitcast(F32), ALU.subtract).then_inc(wk.split_w, 1)
            pool.wait_ge(w_hi_done, 2)
            pool.tensor_tensor(L.b_lo[:, :], raw_b[:, :], L.b_hi[:, :].bitcast(F32), ALU.subtract).then_inc(wk.split_w, 1)
            pool.wait_ge(var_ready, 1)
            pool.tensor_tensor(st[:, 2, :], st[:, 1, :], st[:, 3, :], ALU.pow).then_inc(std_ready, 1)

        @block.scalar
        def _(act):
            def split_block(b):
                act.wait_ge(blk_turned, b + 1)
                turned = ps[:, b % 4, :].rearrange("p (c n) -> p c n", c=CT)
                act.activation(z[:, :, b * P:b * P + P], turned, ACT.Copy).then_inc(blk_whole, 1)
                act.activation(z_hi[:, :, b * P:b * P + P], turned, ACT.Copy).then_inc(blk_hi, 1)

            for b in range(4):
                split_block(b)
            act.wait_ge(s_w, 32)
            act.activation(L.w_hi[:, :, :], raw_w[:, :, :], ACT.Copy).then_inc(w_hi_done, 1)
            act.activation(L.b_hi[:, :], raw_b[:, :], ACT.Copy).then_inc(w_hi_done, 1)
            for b in range(4, SEQS):
                split_block(b)
            act.wait_ge(exp_in, 1)
            act.activation(t2["small"][:, 1, :], t2["small"][:, 0, :], ACT.Exp).then_inc(exp_out, 1)
            layer_hidden_scalar(act, 0, ps, wk)
            for h in range(2):
                layer_gated_scalar(act, 0, h, wk)

        @block.vector
        def _(dve):
            n = [0]

            def link(ins):
                n[0] += 1
                ins.then_inc(chain, 1)
                dve.wait_ge(chain, n[0])

            for b in range(SEQS):
                dve.wait_ge(blk_hi, b + 1)
                ins = dve.tensor_tensor(z_lo[:, :, b * P:b * P + P], z[:, :, b * P:b * P + P],
                                        z_hi[:, :, b * P:b * P + P].bitcast(F32), ALU.subtract)
                if b % 4 == 3:
                    ins.then_inc(wk.inputs_ready, 1)
            dve.wait_ge(s_small, 48)
            dve.wait_ge(wk.logits_done, 1)
            shape = [P, SEQS, GH]
            row = lambda k: bcast(small[:, k * GH:(k + 1) * GH], shape, 1)
            link(dve.tensor_tensor(hid[:, :, :], ps[:, 7, 0:SEQS * GH].rearrange("p (b e) -> p b e", b=SEQS), row(0), ALU.add))
            link(dve.memset(st[:, 2, :], 0.0))
            link(dve.tensor_reduce(st[:, 0, :], hid[:, :, :], AX.X, ALU.add))
            link(dve.tensor_scalar(st[:, 0, :], st[:, 0, :], 1.0 / GH, None, ALU.mult))
            link(dve.tensor_tensor(hid[:, :, :], hid[:, :, :], bcast(st[:, 0, :], shape, 2), ALU.subtract))
            link(dve.tensor_tensor(cen[:, :, :], hid[:, :, :], hid[:, :, :], ALU.mult))
            link(dve.tensor_reduce(st[:, 1, :], cen[:, :, :], AX.X, ALU.add))
            link(dve.tensor_scalar(st[:, 1, :], st[:, 1, :], 1.0 / GH, 1e-5, ALU.mult, ALU.add))
            dve.tensor_scalar(st[:, 3, :], st[:, 2, :], 0.0, -0.5, ALU.mult, ALU.add).then_inc(var_ready, 1)
            dve.wait_ge(std_ready, 1)
            link(dve.tensor_tensor(hid[:, :, :], hid[:, :, :], bcast(st[:, 2, :], shape, 2), ALU.mult))
            link(dve.tensor_tensor(hid[:, :, :], hid[:, :, :], row(1), ALU.mult))
            link(dve.tensor_tensor(hid[:, :, :], hid[:, :, :], row(2), ALU.add))
            dve.tensor_scalar(hid[:, :, :], hid[:, :, :], 0.0, None, ALU.max).then_inc(hid_ready, 1)
            dve.wait_ge(hid_turned, 1)
            dve.tensor_copy(hid_t[:, :, :], ps[0:GH, 2:4, :].rearrange("p a (b n) -> p (a b) n", b=4)).then_inc(hid_t_done, 1)
            dve.wait_ge(logits2, 1)
            link(dve.tensor_tensor(lg[:, :, :], ps[:, 7, 0:SEQS * EXP].rearrange("p (b e) -> p b e", b=SEQS),
                                   bcast(small[:, 3 * GH:3 * GH + EXP], [P, SEQS, EXP], 1), ALU.add))
            top2_gates(dve, link, lg, iota, t2, lambda: dve.wait_ge(exp_out, 1), exp_in, 1.0 / RANK)
            dve.drain().then_inc(hot_ready, 1)
            dve.wait_ge(counted, 1)
            link(dve.tensor_scalar(allowed[:, :, :], ps[:, 7, 0:2 * EXP].rearrange("p (c e) -> p c e", c=2), float(CAPACITY), None, ALU.is_le))
            link(dve.tensor_tensor(t2["hot_g"][:, :, :, :], t2["hot_g"][:, :, :, :],
                                   allowed[:, :, :].unsqueeze(1).broadcast_to([P, SEQS, 2, EXP]), ALU.mult))
            link(dve.tensor_tensor(wk.gate[:, :, :], t2["hot_g"][:, :, 0, :], t2["hot_g"][:, :, 1, :], ALU.add))
            widen_gates(dve, wk)
            dve.wait_ge(s_x1, 16)
            for h in range(2):
                layer_gated_vector(dve, 0, h, ps, wk)
                for o in range(CT):
                    dve.wait_ge(wk.out_done, 4 * h + o + 1)
                    dve.tensor_tensor(x1[:, o, halves(h)], ps[:, o, :], x1[:, o, halves(h)], ALU.add).then_inc(out_ready, 1)
                    dve.sem_inc(wk.bank_free, 0) if False else None

        @block.tensor
        def _(pe):
            for b in range(SEQS):
                if b >= 4:
                    pe.wait_ge(blk_hi, b - 3)
                for c in range(CT):
                    ins = pe.transpose(ps[:, b % 4, c * P:c * P + P], att[:, b, c * P:c * P + P], ident)
                ins.then_inc(blk_turned, 1)

            def routing(pe):
                pe.wait_ge(s_small, 48)
                pe.wait_ge(blk_whole, SEQS)
                logits_fp32(pe, ps, 0, z, L.route_w, GH, wk.logits_done)
                pe.wait_ge(hid_ready, 1)
                for b in range(SEQS):
                    ins = pe.transpose(ps[0:GH, 2 + b // 4, (b % 4) * P:(b % 4) * P + P], hid[:, b, :], ident)
                ins.then_inc(hid_turned, 1)
                pe.wait_ge(hid_t_done, 1)
                for b in range(SEQS):
                    ins = pe.matmul(ps[:, 7, b * EXP:b * EXP + EXP], hid_t[:, b, :], gw2[:, :], start=True, stop=True)
                ins.then_inc(logits2, 1)
                pe.wait_ge(hot_ready, 1)
                for b in range(SEQS):
                    ins = pe.matmul(ps[:, 7, 0:2 * EXP], ones[:, :], t2["hot"][:, b, :, :].rearrange("p c e -> p (c e)"),
                                    start=(b == 0), stop=(b == SEQS - 1))
                ins.then_inc(counted, 1)

            wk.bank_free = out_ready
            layer_tensor(pe, 0, ps, ident, z, z_hi, z_lo, L, wk, routing)


def _features_first(a):
    return np.ascontiguousarray(a.reshape(a.shape[0], CT, P).transpose(2, 1, 0))


def _on_all(a):
    return np.ascontiguousarray(np.broadcast_to(np.asarray(a).reshape(1, -1), (P, np.asarray(a).size)))


def _constants():
    c = np.zeros((P, C_ALL), np.float32)
    c[:, C_ID:C_ID + P] = np.eye(P)
    c[:, C_IOTA:C_IOTA + 16] = np.arange(16)
    c[:, C_FREQ:C_FREQ + 64] = np.float32(1.0) / (10000.0 ** (np.arange(0, P, 2) / P)).astype(np.float32)
    c[:, C_KEY:C_KEY + CACHE] = np.arange(CACHE)
    return c


def kernel(**inputs):
    import concourse.bacc as bacc
    from concourse.bass_utils import run_bass_kernel_spmd

    a = {k: np.asarray(v) for k, v in inputs.items()}

    def with_lora(w, la):
        return np.ascontiguousarray(np.concatenate([_features_first(w), _features_first(la)], axis=2))

    groups = []
    for g in range(KVH):
        q = _features_first(a["L1_cond_Wq"][g * DM:(g + 1) * DM]).reshape(P, QW)
        k = _features_first(a["L1_cond_Wk"][g * P:(g + 1) * P])
        v = _features_first(a["L1_cond_Wv"][g * P:(g + 1) * P])
        kv = np.concatenate([k, v], axis=2).reshape(P, KVW)
        o = _features_first(a["L1_cond_Wo"][:, g * DM:(g + 1) * DM]).reshape(P, OW)
        groups.append(np.concatenate([q, kv, o], axis=1).reshape(P, SEQS, CHUNK).transpose(1, 0, 2))
    part = np.arange(P, dtype=np.int32)
    feed = {
        "consts": _constants(),
        "tokid": part.astype(np.float32).reshape(P, 1),
        "lens": _on_all(a["itok_B_207_1644"]),
        "normw": _on_all(np.concatenate([a["L1_cond_q_norm_w"], a["L1_cond_k_norm_w"]])),
        "x": _features_first(a["x"].reshape(TOK, DM)),
        "lang": _on_all(a["itok_B_0_7"]),
        "cond0_w": with_lora(a["L0_cond_W"], a["L0_cond_A"].reshape(P, DM)),
        "cond0_lb": np.ascontiguousarray(a["L0_cond_B"].transpose(0, 2, 1).reshape(P, DM)),
        "cond0_route": _features_first(a["L0_cond_Wr"]),
        "ffn0_w": with_lora(a["L0_ffn_base_W"], a["L0_ffn_A"].reshape(P, DM)),
        "ffn0_lb": np.ascontiguousarray(a["L0_ffn_B"].transpose(0, 2, 1).reshape(P, DM)),
        "ffn0_route": _features_first(a["L0_ffn_router_W"]),
        "ffn0_b": np.ascontiguousarray(a["L0_ffn_base_b"].reshape(CT, P).T),
        "ffn0_route_b": _on_all(a["L0_ffn_router_b"]),
        "emap": _on_all(a["L0_ffn_expert_map"]),
        "att_w": np.ascontiguousarray(np.concatenate(groups, axis=0)),
        "kv": np.ascontiguousarray(np.concatenate([a["L1_cond_k_cache"], a["L1_cond_v_cache"]], axis=3).reshape(-1, 2 * P)),
        "pages": np.ascontiguousarray(np.repeat(a["itok_Bx16_0_63"].reshape(SEQS, KT, P // PSIZE), PSIZE, axis=2).transpose(2, 0, 1).reshape(P, SEQS * KT)),
        "row_of": np.ascontiguousarray(np.broadcast_to(((part % PSIZE) * KVH)[:, None], (P, SEQS * KT))),
        "head_no": _on_all(np.repeat(np.arange(KVH, dtype=np.int32), KT)),
        "ffn1_w": with_lora(a["L1_ffn_weight"], a["L1_ffn_lora_A"].transpose(0, 2, 1).reshape(P, DM)),
        "ffn1_lb": np.ascontiguousarray(a["L1_ffn_lora_B"].reshape(P, DM)),
        "ffn1_route": _features_first(a["L1_ffn_gw1"]),
        "ffn1_small": _on_all(np.concatenate([a["L1_ffn_gb1"], a["L1_ffn_ln_gamma"], a["L1_ffn_ln_beta"], a["L1_ffn_gb2"],
                                              np.zeros(GH, np.float32)])),
        "ffn1_gw2": np.ascontiguousarray(a["L1_ffn_gw2"].T),
    }
    nc = bacc.Bacc("TRN2", target_bir_lowering=False, num_devices=1)
    t = {k: nc.dram_tensor("in_" + k, v.shape, mybir.dt.from_np(v.dtype), kind="ExternalInput").ap() for k, v in feed.items()}
    t["out"] = nc.dram_tensor("out_0", (P, CT, TOK), F32, kind="ExternalOutput").ap()
    build(nc, t)
    r = run_bass_kernel_spmd(nc, [{"in_" + k: v for k, v in feed.items()}], core_ids=[0])
    out = r.results[0]["out_0"]
    return np.ascontiguousarray(out.transpose(2, 1, 0).reshape(SEQS, P, DM))
```

```python
from contextlib import ExitStack

import numpy as np

import concourse.bass as bass
from concourse import mybir

F32 = mybir.dt.float32
F32R = mybir.dt.float32r
I32 = mybir.dt.int32
U32 = mybir.dt.uint32
ALU = mybir.AluOpType
ACT = mybir.ActivationFunctionType
AX = mybir.AxisListType
ds = bass.ds

P = 128
SEQS = 8
TOK = SEQS * P
DM = 512
CT = DM // P
HALF = TOK // 2
KVH = 8
QPK = 4
PSIZE = 32
NPP = 16
CACHE = PSIZE * NPP
KT = CACHE // P
KEYS = CACHE + P
STEPS = KVH * SEQS
EXP = 8
RANK = 16
NR1 = 2 * EXP - 1
GH = 4 * EXP
CAPACITY = int(3.0 * TOK / EXP)
QW, KVW, OW = CT * DM, CT * 2 * P, QPK * DM
GW = QW + KVW + OW
CHUNK = GW // SEQS
LW = CT * (DM + P)
SCALE = 1.0 / float(np.sqrt(P))
MASKED = -1e30

TWO_PI_1 = 6.28125
TWO_PI_2 = float(np.float32(np.round((2 * np.pi - TWO_PI_1) * 2.0**21) / 2.0**21))
TWO_PI_3 = float(np.float32(2 * np.pi - TWO_PI_1 - TWO_PI_2))
ROUND = 1.5 * 2.0**23

C_ID, C_IOTA, C_FREQ, C_KEY = 0, P, P + 16, P + 80
C_ALL = C_KEY + CACHE


class Step:

    def __init__(self, off, trip=0):
        self.off, self.trip = off, trip

    @property
    def parity(self):
        return self.off % 2

    def half(self, add=0):
        return self.trip + (self.off // 2 + add)

    def times(self, m, add=0):
        if isinstance(self.trip, int):
            return m * (2 * self.trip + self.off) + add
        return self.trip * (2 * m) + (m * self.off + add)

    def plus(self, n):
        return Step(self.off + n, self.trip)

    @property
    def first(self):
        return isinstance(self.trip, int) and 2 * self.trip + self.off <= 0

    @property
    def after_last(self):
        return isinstance(self.trip, int) and self.off == STEPS

    def turned(self, add=0):
        if self.first:
            return 2 * (self.off + 1) + add
        if self.after_last:
            add -= 2
        return self.times(7, add - 3)


TURNS = dict(kc=5, q=6)


def turn_no(i, name):
    j = name if isinstance(name, int) else TURNS[name]
    return i.turned(j - 5) if i.first else i.turned(j)


def turn_bank(i, name):
    j = name if isinstance(name, int) else TURNS[name]
    return BANK_T + (i.off + j + 1) % 2


def build(nc, t):
    top = ExitStack()
    with top:
        ps = top.enter_context(nc.psum_tensor("ps", [P, 8, 512], F32))
        cst = top.enter_context(nc.sbuf_tensor("cst", [P, C_ALL], F32))
        ident = cst[:, C_ID:C_ID + P]
        ones = top.enter_context(nc.sbuf_tensor("ones", [P, P], F32))
        x1_split = nc.dram_tensor("x1_split", (SEQS, P, 2 * DM), F32, kind="Internal").ap()
        rope_tab = nc.dram_tensor("rope_tab", (SEQS, P, 4 * P), F32, kind="Internal").ap()
        mask_tab = nc.dram_tensor("mask_tab", (SEQS, P, KEYS), F32, kind="Internal").ap()
        prob = top.enter_context(nc.sbuf_tensor("prob", [P, 2, QPK, KEYS], F32))
        first_block(nc, t, ps, cst, ones, prob, x1_split, rope_tab, mask_tab)
        att = top.enter_context(nc.sbuf_tensor("att", [P, SEQS, DM], F32))
        w_hi = top.enter_context(nc.sbuf_tensor("w_hi", [P, 2 * GW], F32R))
        w_lo = top.enter_context(nc.sbuf_tensor("w_lo", [P, 2 * GW], F32R))
        attention(nc, t, ps, cst, prob, w_hi, w_lo, x1_split, rope_tab, mask_tab, att)
        last_layer(nc, t, ps, cst, ones, prob, w_hi, w_lo, x1_split, att)


class Tables:

    def __init__(self, sb, sem, cst, rope_tab, mask_tab):
        self.cst, self.rope_tab, self.mask_tab = cst, rope_tab, mask_tab
        self.lens, self.tokid, self.normw = sb("lens", [P, SEQS], I32), sb("tokid", [P, 1]), sb("normw", [P, 2 * P])
        self.lenf, self.pos = sb("lenf", [P, SEQS]), sb("pos", [P, SEQS])
        self.sin, self.cos, self.turns = (sb(n, [P, SEQS, 64]) for n in ("sin", "cos", "turns"))
        self.part = [sb(f"table_part{p}", [P, SEQS, P]) for p in range(2)]
        self.mask = [sb(f"mask_part{p}", [P, 2, KEYS]) for p in range(2)]
        self.loaded, self.reduced, self.trig = sem("table_inputs_in"), sem("angles_reduced"), sem("trig")
        self.masked, self.tabbed = sem("masks_ready"), sem("table_part_ready")
        self.mask_stored, self.tab_stored = ([sem(f"{n}{p}") for p in range(2)] for n in ("masks_stored", "tables_stored"))

    def load(self, sp, t):
        sp.dma_start(self.cst[:, :], t["consts"]).then_inc(self.loaded, 16)
        sp.dma_start(self.lens[:, :], t["lens"]).then_inc(self.loaded, 16)
        sp.dma_start(self.tokid[:, :], t["tokid"]).then_inc(self.loaded, 16)
        sp.dma_start(self.normw[:, :], t["normw"]).then_inc(self.loaded, 16)

    def store_masks(self, sp):
        for j in range(SEQS // 2):
            sp.wait_ge(self.masked, j + 1)
            sp.dma_start(self.mask_tab[2 * j:2 * j + 2].rearrange("b p k -> p b k"), self.mask[j % 2][:, :, :]).then_inc(self.mask_stored[j % 2], 16)

    def store_tables(self, sp):
        for j in range(4):
            sp.wait_ge(self.tabbed, j + 1)
            sp.dma_start(self.rope_tab[:, :, j * P:j * P + P].rearrange("b p k -> p b k"), self.part[j % 2][:, :, :]).then_inc(self.tab_stored[j % 2], 16)

    def angles(self, dve, link):
        shape = [P, SEQS, 64]
        ang, cosr, turns = self.sin, self.cos, self.turns
        dve.wait_ge(self.loaded, 64)
        link(dve.tensor_copy(self.lenf[:, :], self.lens[:, :]))
        link(dve.tensor_scalar(self.pos[:, :], self.lenf[:, :], self.tokid[:, 0:1], None, ALU.add))
        freq = self.cst[:, C_FREQ:C_FREQ + 64].unsqueeze(1).broadcast_to(shape)
        link(dve.tensor_tensor(ang[:, :, :], self.pos[:, :].unsqueeze(2).broadcast_to(shape), freq, ALU.mult))
        link(dve.tensor_scalar(turns[:, :, :], ang[:, :, :], float(1 / (2 * np.pi)), None, ALU.mult))
        link(dve.tensor_scalar(turns[:, :, :], turns[:, :, :], ROUND, None, ALU.add))
        link(dve.tensor_scalar(turns[:, :, :], turns[:, :, :], ROUND, None, ALU.subtract))
        for part in (TWO_PI_1, TWO_PI_2, TWO_PI_3):
            link(dve.scalar_tensor_tensor(out=ang[:, :, :], in0=turns[:, :, :], scalar=-part, in1=ang[:, :, :],
                                          op0=ALU.mult, op1=ALU.add))
        below_pi = float(np.float32(3.1415925))
        link(dve.tensor_scalar(ang[:, :, :], ang[:, :, :], below_pi, -below_pi, ALU.min, ALU.max))
        link(dve.tensor_scalar(cosr[:, :, :], ang[:, :, :], float(np.pi / 2), None, ALU.add))
        link(dve.tensor_scalar(turns[:, :, :], cosr[:, :, :], float(np.pi), float(-2 * np.pi), ALU.is_gt, ALU.mult))
        link(dve.tensor_tensor(cosr[:, :, :], cosr[:, :, :], turns[:, :, :], ALU.add))
        dve.tensor_scalar(cosr[:, :, :], cosr[:, :, :], below_pi, -below_pi, ALU.min, ALU.max).then_inc(self.reduced, 1)

    def sines(self, act):
        act.wait_ge(self.reduced, 1)
        act.activation(self.sin[:, :, :], self.sin[:, :, :], ACT.Sin).then_inc(self.trig, 1)
        act.activation(self.cos[:, :, :], self.cos[:, :, :], ACT.Sin).then_inc(self.trig, 1)

    def masks(self, dve, link):
        for buf in self.mask:
            link(dve.memset(buf[:, :, CACHE:], 0.0))
        for j in range(SEQS // 2):
            if j >= 2:
                dve.wait_ge(self.mask_stored[j % 2], 16 * (j // 2))
            for b in (2 * j, 2 * j + 1):
                ins = dve.tensor_scalar(self.mask[j % 2][:, b % 2, 0:CACHE], self.cst[:, C_KEY:C_KEY + CACHE],
                                        self.lenf[:, b:b + 1], MASKED, ALU.is_ge, ALU.mult)
            ins.then_inc(self.masked, 1)

    def tables(self, dve, link):
        dve.wait_ge(self.trig, 2)
        link(dve.tensor_scalar(self.turns[:, :, :], self.sin[:, :, :], -1.0, None, ALU.mult))
        for j in range(4):
            if j >= 2:
                dve.wait_ge(self.tab_stored[j % 2], 16 * (j // 2))
            for half in range(2):
                at = (j // 2) * P + half * 64
                w = self.normw[:, at:at + 64].unsqueeze(1).broadcast_to([P, SEQS, 64])
                src = self.cos if j % 2 == 0 else (self.turns if half else self.sin)
                ins = dve.tensor_tensor(self.part[j % 2][:, :, half * 64:half * 64 + 64], src[:, :, :], w, ALU.mult)
            ins.then_inc(self.tabbed, 1)


class Layer:

    def __init__(self, sb, name, routes, placed=None):
        self.name, self.routes = name, routes
        self.route_w = sb(name + "_route_w", [P, CT, routes])
        self.route_hi, self.route_lo = (sb(name + n, [P, CT, routes], F32R) for n in ("_route_hi", "_route_lo"))
        if placed:
            w, b = slice(0, LW), slice(LW, LW + DM)
            self.w_hi, self.w_lo = (part[:, w].rearrange("p (c n) -> p c n", c=CT) for part in placed)
            self.b_hi, self.b_lo = (part[:, b] for part in placed)
            return
        self.w_hi, self.w_lo = sb(name + "_w_hi", [P, CT, DM + P], F32R), sb(name + "_w_lo", [P, CT, DM + P], F32R)
        self.b_hi, self.b_lo = sb(name + "_b_hi", [P, DM], F32R), sb(name + "_b_lo", [P, DM], F32R)


class Work:

    def __init__(self, sb, sem, name):
        self.hid = sb(name + "_hid", [P, 2, HALF])
        self.gate = sb(name + "_gate", [P, SEQS, EXP])
        self.gate_wide = sb(name + "_gate_wide", [P, SEQS, P])
        self.hg = sb(name + "_hg", [P, 2, HALF])
        self.hg_hi, self.hg_lo = sb(name + "_hg_hi", [P, 2, HALF], F32R), sb(name + "_hg_lo", [P, 2, HALF], F32R)
        self.split_w = sem(name + "_split_w")
        self.inputs_ready = sem(name + "_inputs_ready")
        self.route_hi_done, self.route_lo_done = sem(name + "_route_hi_done"), sem(name + "_route_lo_done")
        self.logits_wide = sem(name + "_logits_wide")
        self.logits_copied = sem(name + "_logits_copied")
        self.logits_done = sem(name + "_logits_done")
        self.hid_done = sem(name + "_hid_done")
        self.hid_copied = sem(name + "_hid_copied")
        self.gates_wide = sem(name + "_gates_wide")
        self.gates_turned = sem(name + "_gates_turned")
        self.gated = sem(name + "_gated")
        self.gated_hi = sem(name + "_gated_hi")
        self.gated_lo = sem(name + "_gated_lo")
        self.out_done = sem(name + "_out_done")
        self.out_hi = sem(name + "_out_hi")
        self.bank_free = sem(name + "_bank_free")


def mm3(pe, out, lhs, rhs, start, stop):
    pe.matmul(out, lhs[0], rhs[0], start=start, stop=False)
    pe.matmul(out, lhs[0], rhs[1], start=False, stop=False)
    return pe.matmul(out, lhs[1], rhs[0], start=False, stop=stop)


def halves(h):
    return slice(h * HALF, (h + 1) * HALF)


class LayerTensor:

    def __init__(self, pe, k, ps, ident, x_hi, x_lo, L, wk):
        self.pe, self.k, self.ps, self.ident, self.L, self.wk = pe, k, ps, ident, L, wk
        self.x_hi, self.x_lo = x_hi, x_lo

    def hidden(self, h):
        L, a = self.L, slice(DM, DM + P)
        for c in range(CT):
            ins = mm3(self.pe, self.ps[:, 4 + h, :], (L.w_hi[:, c, a], L.w_lo[:, c, a]),
                      (self.x_hi[:, c, halves(h)], self.x_lo[:, c, halves(h)]), c == 0, c == CT - 1)
        ins.then_inc(self.wk.hid_done, 1)

    def logits(self):
        L = self.L
        self.pe.wait_ge(self.wk.route_lo_done, self.k + 1)
        for h in range(2):
            for c in range(CT):
                ins = mm3(self.pe, self.ps[0:L.routes, 7 - h, :], (L.route_hi[:, c, :], L.route_lo[:, c, :]),
                          (self.x_hi[:, c, halves(h)], self.x_lo[:, c, halves(h)]), c == 0, c == CT - 1)
            ins.then_inc(self.wk.logits_wide, 1)

    def turn_logits(self):
        n = self.L.routes
        self.pe.wait_ge(self.wk.logits_copied, 2 * self.k + 2)
        for b in range(SEQS):
            ins = self.pe.transpose(self.ps[:, 7, b * n:b * n + n], self.wk.hg[0:n, b // 4, (b % 4) * P:(b % 4) * P + P], self.ident[0:n, 0:n])
        ins.then_inc(self.wk.logits_done, 1)

    def base(self, h, o, bank):
        L, w = self.L, slice(o * P, o * P + P)
        for c in range(CT):
            mm3(self.pe, self.ps[:, bank, :], (L.w_hi[:, c, w], L.w_lo[:, c, w]),
                (self.x_hi[:, c, halves(h)], self.x_lo[:, c, halves(h)]), c == 0, False)

    def turn_gates(self, h):
        pe, wk, k = self.pe, self.wk, self.k
        pe.wait_ge(wk.gates_wide, k + 1)
        if h or k:
            pe.wait_ge(wk.gated, 2 * k + h)
        for b in range(4):
            ins = pe.transpose(self.ps[:, 6, b * P:b * P + P], wk.gate_wide[:, 4 * h + b, :], self.ident)
        ins.then_inc(wk.gates_turned, 1)

    def experts(self, h, banks):
        wk, L = self.wk, self.L
        self.pe.wait_ge(wk.gated_lo, 2 * self.k + h + 1)
        for o in range(CT):
            w = slice(o * P, o * P + P)
            mm3(self.pe, self.ps[:, banks[o], :], (L.b_hi[:, w], L.b_lo[:, w]), (wk.hg_hi[:, h, :], wk.hg_lo[:, h, :]),
                False, True).then_inc(wk.out_done, 1)


def layer_tensor(pe, k, ps, ident, x_hi, x_lo, L, wk):
    part = LayerTensor(pe, k, ps, ident, x_hi, x_lo, L, wk)
    pe.wait_ge(wk.inputs_ready, 2 * k + 1)
    pe.wait_ge(wk.split_w, 2 * k + 2)
    if k:
        pe.wait_ge(wk.hid_copied, 2 * k)
    part.hidden(0)
    pe.wait_ge(wk.inputs_ready, 2 * k + 2)
    part.logits()
    part.hidden(1)
    part.turn_logits()
    for h in range(2):
        for o in range(CT):
            if o == CT - 1:
                part.turn_gates(h)
            if 8 * k + 4 * h + o >= CT:
                pe.wait_ge(wk.bank_free, 8 * k + 4 * h + o - 3)
            part.base(h, o, o)
        part.experts(h, range(CT))


def layer_gated_vector(dve, k, h, ps, wk):
    dve.wait_ge(wk.hid_copied, 2 * k + h + 1)
    dve.wait_ge(wk.gates_turned, 2 * k + h + 1)
    if k:
        dve.wait_ge(wk.out_done, 8 * k)
    dve.tensor_tensor(wk.hg[:, h, :], wk.hid[:, h, :], ps[:, 6, :], ALU.mult).then_inc(wk.gated, 1)
    dve.wait_ge(wk.gated_hi, 2 * k + h + 1)
    dve.tensor_tensor(wk.hg_lo[:, h, :], wk.hg[:, h, :], wk.hg_hi[:, h, :].bitcast(F32), ALU.subtract).then_inc(wk.gated_lo, 1)


def layer_hidden_scalar(act, k, ps, wk):
    for h in range(2):
        act.wait_ge(wk.hid_done, 2 * k + h + 1)
        if k:
            act.wait_ge(wk.gated, 2 * k)
        act.activation(wk.hid[:, h, :], ps[:, 4 + h, :], ACT.Copy).then_inc(wk.hid_copied, 1)


def layer_gated_scalar(act, k, h, wk):
    act.wait_ge(wk.gated, 2 * k + h + 1)
    act.activation(wk.hg_hi[:, h, :], wk.hg[:, h, :], ACT.Copy).then_inc(wk.gated_hi, 1)


def layer_logits_scalar(act, k, ps, L, wk):
    if k:
        act.wait_ge(wk.gated_lo, 2 * k)
    for h in range(2):
        act.wait_ge(wk.logits_wide, 2 * k + h + 1)
        act.activation(wk.hg[0:L.routes, h, :], ps[0:L.routes, 7 - h, :], ACT.Copy).then_inc(wk.logits_copied, 1)


def bcast(ap, shape, at):
    return ap.unsqueeze(at).broadcast_to(shape)


def top2_gates(dve, link, lg, iota, buf, exp_wait, exp_in, gate_scale):
    for b in range(SEQS):
        ins = dve.max(buf["best"][:, b, :], lg[:, b, :])
    link(ins)
    for b in range(SEQS):
        ins = dve.max_index(buf["where"][:, b, :], buf["best"][:, b, :], lg[:, b, :])
    link(ins)
    best, where_f, sm = buf["best"], buf["where_f"], buf["small"]
    link(dve.tensor_copy(where_f[:, :, :], buf["where"][:, :, :]))
    dve.tensor_tensor(sm[:, 0, :], best[:, :, 1], best[:, :, 0], ALU.subtract).then_inc(exp_in, 1)
    shape = [P, SEQS, EXP]
    for c in range(2):
        link(dve.tensor_tensor(buf["hot"][:, :, c, :], bcast(iota, shape, 1),
                               where_f[:, :, c:c + 1].broadcast_to(shape), ALU.is_equal))
    exp_wait()
    link(dve.tensor_scalar(sm[:, 2, :], sm[:, 1, :], 1.0, None, ALU.add))
    link(dve.reciprocal(sm[:, 3, :], sm[:, 2, :]))
    link(dve.tensor_scalar(sm[:, 4, :], sm[:, 3, :], gate_scale, None, ALU.mult))
    link(dve.tensor_tensor(sm[:, 5, :], sm[:, 4, :], sm[:, 1, :], ALU.mult))
    for c in range(2):
        link(dve.tensor_tensor(buf["hot_g"][:, :, c, :], buf["hot"][:, :, c, :], bcast(sm[:, 4 + c, :], shape, 2), ALU.mult))


def top2_buffers(sb, name):
    return dict(best=sb(name + "_best", [P, SEQS, 8]), where=sb(name + "_where", [P, SEQS, 8], U32),
                where_f=sb(name + "_where_f", [P, SEQS, 8]), hot=sb(name + "_hot", [P, SEQS, 2, EXP]),
                hot_g=sb(name + "_hot_g", [P, SEQS, 2, EXP]), small=sb(name + "_small", [P, 6, SEQS]))


def widen_gates(dve, wk):
    dve.tensor_copy(wk.gate_wide[:, :, :].rearrange("p b (e r) -> p b e r", r=RANK),
                    wk.gate[:, :, :].unsqueeze(3).broadcast_to([P, SEQS, EXP, RANK])).then_inc(wk.gates_wide, 1)


def first_block(nc, t, ps, cst, ones, prob, x1_split, rope_tab, mask_tab):
    ident, iota = cst[:, C_ID:C_ID + P], cst[:, C_IOTA:C_IOTA + EXP]
    with ExitStack() as ctx:
        sb = lambda n, s, d=F32: ctx.enter_context(nc.sbuf_tensor(n, s, d))
        sem = lambda n: ctx.enter_context(nc.semaphore(n))
        x = sb("x", [P, CT, TOK])
        x_hi, x_lo = sb("x_hi", [P, CT, TOK], F32R), sb("x_lo", [P, CT, TOK], F32R)
        y_hi, y_lo = x_hi, x_lo
        raw_w = sb("raw_w", [P, CT, DM + P])
        raw_b = sb("raw_b", [P, DM])
        tab = Tables(sb, sem, cst, rope_tab, mask_tab)
        L = [Layer(sb, "cond0", EXP), Layer(sb, "ffn0", NR1)]
        wk = Work(sb, sem, "b0")
        lang, lang_f = sb("lang", [P, SEQS], I32), sb("lang_f", [P, SEQS])
        base_b, route_b = sb("base_b", [P, CT]), sb("route_b", [P, NR1])
        emap, emap_f = sb("emap", [P, NR1], I32), sb("emap_f", [P, NR1])
        onehot = sb("onehot", [P, EXP, NR1])
        lg0, bias0 = sb("lg0", [P, SEQS, EXP]), sb("bias0", [P, SEQS, EXP])
        t2 = top2_buffers(sb, "t2")
        lg1, pr1, rest1 = (sb(n, [P, SEQS, NR1]) for n in ("lg1", "pr1", "rest1"))
        st1 = sb("st1", [P, 3, SEQS])
        best1 = sb("best1", [P, SEQS, 8])
        spread = sb("spread", [P, SEQS, EXP, NR1])
        s_x, s_w, s_small = [sem("x_in0"), sem("x_in1")], [sem("w_in0"), sem("w_in1")], sem("small_in")
        x_hi_done, w_hi_done, chain, exp_in, exp_out, stored, group_in, x1_lo_done, route_in = (
            sem(n) for n in ("x_hi_done", "w_hi_done", "chain", "exp_in", "exp_out", "stored", "group_in", "x1_lo_done", "route_in"))
        block = ctx.enter_context(nc.Block())

        @block.sync
        def _(sp):
            def load_w(k):
                sp.dma_start(raw_w[:, :, :], t[L[k].name + "_w"]).then_inc(s_w[k], 16)
                sp.dma_start(raw_b[:, :], t[L[k].name + "_lb"]).then_inc(s_w[k], 16)

            load_w(0)
            for k in range(2):
                sp.dma_start(L[k].route_w[:, :, :], t[L[k].name + "_route"]).then_inc(route_in, 16)
            for h in range(2):
                sp.dma_start(x[:, :, halves(h)], t["x"][:, :, halves(h)]).then_inc(s_x[h], 16)
            for dst, src in ((lang[:, :], t["lang"]), (base_b[:, :], t["ffn0_b"]), (route_b[:, :], t["ffn0_route_b"]),
                             (emap[:, :], t["emap"])):
                sp.dma_start(dst, src).then_inc(s_small, 16)
            tab.load(sp, t)
            sp.wait_ge(wk.split_w, 2)
            load_w(1)
            sp.dma_start(prob[:, :, :, :].rearrange("p a h k -> p (a h k)").rearrange("p (a n) -> p a n", a=SEQS),
                         t["att_w"][0:SEQS, :, :].rearrange("a p n -> p a n")).then_inc(group_in, 16)
            tab.store_masks(sp)
            tab.store_tables(sp)
            for h in range(2):
                for o in range(CT):
                    sp.wait_ge(x1_lo_done, 4 * h + o + 1)
                    for j, part in enumerate((x_hi, x_lo)):
                        at = j * DM + o * P
                        sp.dma_start(x1_split[4 * h:4 * h + 4, :, at:at + P].rearrange("b p n -> p b n"),
                                     part[:, o, halves(h)].bitcast(F32).rearrange("p (b n) -> p b n", b=4)).then_inc(stored, 16)
            sp.wait_ge(stored, 16 * 16)
            for p in range(2):
                sp.wait_ge(tab.mask_stored[p], 16 * 2)
                sp.wait_ge(tab.tab_stored[p], 16 * 2)
            sp.wait_ge(group_in, 16)

        @block.gpsimd
        def _(pool):
            pool.wait_ge(w_hi_done, CT + 2)
            pool.tensor_tensor(L[1].w_lo[:, :, :], raw_w[:, :, :], L[1].w_hi[:, :, :].bitcast(F32), ALU.subtract).then_inc(wk.split_w, 1)
            pool.wait_ge(w_hi_done, CT + 3)
            pool.tensor_tensor(L[1].b_lo[:, :], raw_b[:, :], L[1].b_hi[:, :].bitcast(F32), ALU.subtract).then_inc(wk.split_w, 1)

        @block.scalar
        def _(act):
            act.wait_ge(s_w[0], 32)
            for c in range(CT):
                act.activation(L[0].w_hi[:, c, :], raw_w[:, c, :], ACT.Copy).then_inc(w_hi_done, 1)
            for h in range(2):
                act.wait_ge(s_x[h], 16)
                for c in range(CT):
                    act.activation(x_hi[:, c, halves(h)], x[:, c, halves(h)], ACT.Copy).then_inc(x_hi_done, 1)
                if h == 0:
                    act.activation(L[0].b_hi[:, :], raw_b[:, :], ACT.Copy).then_inc(w_hi_done, 1)
                    act.wait_ge(route_in, 32)
                    for k in range(2):
                        act.activation(L[k].route_hi[:, :, :], L[k].route_w[:, :, :], ACT.Copy).then_inc(wk.route_hi_done, 1)
            tab.sines(act)
            for k in range(2):
                layer_logits_scalar(act, k, ps, L[k], wk)
                act.wait_ge(exp_in, k + 1)
                if k == 0:
                    act.activation(t2["small"][:, 1, :], t2["small"][:, 0, :], ACT.Exp).then_inc(exp_out, 1)
                else:
                    act.activation(pr1[:, :, :], lg1[:, :, :], ACT.Exp).then_inc(exp_out, 1)
                layer_hidden_scalar(act, k, ps, wk)
                if k == 0:
                    act.wait_ge(s_w[1], 32)
                    act.activation(L[1].w_hi[:, :, :], raw_w[:, :, :], ACT.Copy).then_inc(w_hi_done, 1)
                    act.activation(L[1].b_hi[:, :], raw_b[:, :], ACT.Copy).then_inc(w_hi_done, 1)
                for h in range(2):
                    layer_gated_scalar(act, k, h, wk)
                    for o in range(CT):
                        if k == 0:
                            act.wait_ge(wk.out_done, 4 * h + o + 1)
                            act.activation(y_hi[:, o, halves(h)], ps[:, o, :], ACT.Copy).then_inc(wk.out_hi, 1)
                        else:
                            act.wait_ge(wk.bank_free, 8 + 4 * h + o + 1)
                            act.activation(x_hi[:, o, halves(h)], x[:, o, halves(h)], ACT.Copy).then_inc(wk.out_hi, 1)

        @block.vector
        def _(dve):
            n = [0]

            def link(ins):
                n[0] += 1
                ins.then_inc(chain, 1)
                dve.wait_ge(chain, n[0])

            link(dve.memset(ones[:, :], 1.0))
            for c in range(CT):
                dve.wait_ge(w_hi_done, c + 1)
                ins = dve.tensor_tensor(L[0].w_lo[:, c, :], raw_w[:, c, :], L[0].w_hi[:, c, :].bitcast(F32), ALU.subtract)
            ins.then_inc(wk.split_w, 1)
            for h in range(2):
                for c in range(CT):
                    dve.wait_ge(x_hi_done, CT * h + c + 1)
                    ins = dve.tensor_tensor(x_lo[:, c, halves(h)], x[:, c, halves(h)], x_hi[:, c, halves(h)].bitcast(F32), ALU.subtract)
                ins.then_inc(wk.inputs_ready, 1)
                if h == 0:
                    dve.wait_ge(w_hi_done, CT + 1)
                    dve.tensor_tensor(L[0].b_lo[:, :], raw_b[:, :], L[0].b_hi[:, :].bitcast(F32), ALU.subtract).then_inc(wk.split_w, 1)
                    for k in range(2):
                        dve.wait_ge(wk.route_hi_done, k + 1)
                        dve.tensor_tensor(L[k].route_lo[:, :, :], L[k].route_w[:, :, :], L[k].route_hi[:, :, :].bitcast(F32),
                                          ALU.subtract).then_inc(wk.route_lo_done, 1)
            tab.angles(dve, link)
            dve.wait_ge(s_small, 64)
            link(dve.tensor_copy(lang_f[:, :], lang[:, :]))
            shape = [P, SEQS, EXP]
            link(dve.tensor_tensor(bias0[:, :, :], bcast(iota, shape, 1), bcast(lang_f[:, :], shape, 2), ALU.is_equal))
            link(dve.tensor_copy(emap_f[:, :], emap[:, :]))
            hot_shape = [P, EXP, NR1]
            link(dve.tensor_tensor(onehot[:, :, :], bcast(iota, hot_shape, 2), bcast(emap_f[:, :], hot_shape, 1), ALU.is_equal))
            tab.masks(dve, link)
            dve.wait_ge(wk.logits_done, 1)
            link(dve.scalar_tensor_tensor(out=lg0[:, :, :], in0=bias0[:, :, :], scalar=5.0,
                                          in1=ps[:, 7, 0:SEQS * EXP].rearrange("p (b e) -> p b e", b=SEQS),
                                          op0=ALU.mult, op1=ALU.add))
            top2_gates(dve, link, lg0, iota, t2, lambda: dve.wait_ge(exp_out, 1), exp_in, 2.0)
            link(dve.tensor_tensor(wk.gate[:, :, :], t2["hot_g"][:, :, 0, :], t2["hot_g"][:, :, 1, :], ALU.add))
            widen_gates(dve, wk)
            for h in range(2):
                layer_gated_vector(dve, 0, h, ps, wk)
                for o in range(CT):
                    dve.wait_ge(wk.out_hi, 4 * h + o + 1)
                    dve.tensor_tensor(y_lo[:, o, halves(h)], ps[:, o, :], y_hi[:, o, halves(h)].bitcast(F32), ALU.subtract).then_inc(wk.bank_free, 1)
                dve.wait_ge(wk.bank_free, 4 * h + CT)
                dve.sem_inc(wk.inputs_ready, 1)
                if h == 0:
                    tab.tables(dve, link)
            dve.wait_ge(wk.logits_done, 2)
            lshape = [P, SEQS, NR1]
            link(dve.tensor_tensor(lg1[:, :, :], ps[:, 7, 0:SEQS * NR1].rearrange("p (b e) -> p b e", b=SEQS),
                                   bcast(route_b[:, :], lshape, 1), ALU.add))
            link(dve.tensor_reduce(st1[:, 0, :], lg1[:, :, :], AX.X, ALU.max))
            dve.tensor_tensor(lg1[:, :, :], lg1[:, :, :], bcast(st1[:, 0, :], lshape, 2), ALU.subtract).then_inc(exp_in, 1)
            dve.wait_ge(exp_out, 2)
            link(dve.tensor_reduce(st1[:, 1, :], pr1[:, :, :], AX.X, ALU.add))
            link(dve.reciprocal(st1[:, 2, :], st1[:, 1, :]))
            link(dve.tensor_tensor(pr1[:, :, :], pr1[:, :, :], bcast(st1[:, 2, :], lshape, 2), ALU.mult))
            for b in range(SEQS):
                ins = dve.max(best1[:, b, :], pr1[:, b, :])
            link(ins)
            for b in range(SEQS):
                ins = dve.match_replace(rest1[:, b, :], best1[:, b, :], pr1[:, b, :], 0.0)
            link(ins)
            link(dve.tensor_tensor(pr1[:, :, :], pr1[:, :, :], rest1[:, :, :], ALU.subtract))
            wide = [P, SEQS, EXP, NR1]
            link(dve.tensor_tensor(spread[:, :, :, :], pr1[:, :, :].unsqueeze(2).broadcast_to(wide),
                                   onehot[:, :, :].unsqueeze(1).broadcast_to(wide), ALU.mult))
            link(dve.tensor_reduce(wk.gate[:, :, :], spread[:, :, :, :], AX.X, ALU.add))
            link(dve.tensor_scalar(wk.gate[:, :, :], wk.gate[:, :, :], 2.0, None, ALU.mult))
            dve.wait_ge(wk.gates_turned, 2)
            widen_gates(dve, wk)
            for h in range(2):
                layer_gated_vector(dve, 1, h, ps, wk)
                for o in range(CT + 1):
                    if o < CT:
                        dve.wait_ge(wk.out_done, 8 + 4 * h + o + 1)
                        dve.scalar_tensor_tensor(out=x[:, o, halves(h)], in0=ps[:, o, :], scalar=base_b[:, o:o + 1],
                                                 in1=x[:, o, halves(h)], op0=ALU.add, op1=ALU.add).then_inc(wk.bank_free, 1)
                    if o:
                        dve.wait_ge(wk.out_hi, 8 + 4 * h + o)
                        dve.tensor_tensor(x_lo[:, o - 1, halves(h)], x[:, o - 1, halves(h)], x_hi[:, o - 1, halves(h)].bitcast(F32),
                                          ALU.subtract).then_inc(x1_lo_done, 1)

        @block.tensor
        def _(pe):
            pe.wait_ge(tab.loaded, 64)
            layer_tensor(pe, 0, ps, ident, x_hi, x_lo, L[0], wk)
            layer_tensor(pe, 1, ps, ident, y_hi, y_lo, L[1], wk)


BANK_S, BANK_T, BANK_O, BANK_P = 0, 4, 6, 7
SPARE = slice(KEYS // 2, KEYS // 2 + P)


def attention(nc, t, ps, cst, prob, w_hi, w_lo, x1_split, rope_tab, mask_tab, att):
    ident = cst[:, C_ID:C_ID + P]
    with ExitStack() as ctx:
        sb = lambda n, s, d=F32: ctx.enter_context(nc.sbuf_tensor(n, s, d))
        sem = lambda n: ctx.enter_context(nc.semaphore(n))
        pair = lambda n, s, d=F32: [sb(f"{n}{p}", s, d) for p in range(2)]
        w_raw = pair("w_raw", [P, CHUNK])
        xs = pair("xs", [P, 2 * DM], F32R)
        rope = pair("rope", [P, 4 * P])
        mask = pair("mask", [P, KEYS])
        kv = pair("kv", [P, KT + 1, 2 * P])
        page_row = sb("page_row", [P, SEQS * KT], I32)
        page_in, row_of, head_no = sb("page_in", [P, SEQS * KT], I32), sb("row_of", [P, SEQS * KT], I32), sb("head_no", [P, KVH * KT], I32)
        rows = pair("rows", [P, KT], I32)
        q_raw, q_a, q_b = sb("q_raw", [P, QPK * P]), sb("q_a", [P, QPK * P]), sb("q_b", [P, QPK * P])
        k_a, k_b = sb("k_a", [P, P]), sb("k_b", [P, P])
        sq = sb("sq", [P, (QPK + 1) * P])
        ssq_q, ssq_k = sb("ssq_q", [P, QPK]), sb("ssq_k", [P, 1])
        rms_q, rms_k = sb("rms_q", [P, QPK]), sb("rms_k", [P, 1])
        minus_half = sb("minus_half", [P, QPK])
        r_q, neg_r_q = pair("r_q", [P, QPK]), pair("neg_r_q", [P, QPK])
        qt_hi, qt_lo = sb("qt_hi", [P, QPK * P], F32R), sb("qt_lo", [P, QPK * P], F32R)
        kt_hi, kt_lo = sb("kt_hi", [P, KEYS], F32R), sb("kt_lo", [P, KEYS], F32R)
        v_hi, v_lo = pair("v_hi", [P, KT + 1, P], F32R), pair("v_lo", [P, KT + 1, P], F32R)
        top, neg_top = sb("top", [P, QPK]), sb("neg_top", [P, QPK])
        den, inv = sb("den", [P, QPK]), sb("inv", [P, QPK])
        pt_hi, pt_lo = pair("pt_hi", [P, DM], F32R), pair("pt_lo", [P, DM], F32R)
        ot_hi, ot_lo = sb("ot_hi", [P, DM], F32R), sb("ot_lo", [P, DM], F32R)

        w_in, x_in, mask_in, kv_in = ([sem(f"{n}{p}") for p in range(2)] for n in ("w_in", "x_in", "mask_in", "kv_in"))
        pages_in = sem("pages_in")
        q_done, kv_done, s_done, turned, kn_turned, pv_done, o_done = (
            sem(n) for n in ("q_done", "kv_done", "s_done", "turned", "kn_turned", "pv_done", "o_done"))
        q_copied, kv_copied, q_squared, k_squared, expd, normed_1, hi_done, kn_hi_done, v_hi_done, w_hi_done, o_hi_done = (
            sem(n) for n in ("q_copied", "kv_copied", "q_squared", "k_squared", "expd", "normed_1", "hi_done", "kn_hi_done", "v_hi_done", "w_hi_done", "o_hi_done"))
        lo_done, kn_lo_done, maxed, biased, inverted, normed, q_scaled, q_cos, k_cos, k_roped, o_lo_done, summed, cleared = (
            sem(n) for n in ("lo_done", "kn_lo_done", "maxed", "biased", "inverted", "normed", "q_scaled", "q_cos", "k_cos",
                             "k_roped", "o_lo_done", "summed", "cleared"))
        q_sin, q_roped, k_sin, q_mean, q_rms, k_mean, k_rms, v_lo_done, w_lo_done, rows_done, setup = (
            sem(n) for n in ("q_sin", "q_roped", "k_sin", "q_mean", "q_rms", "k_mean", "k_rms", "v_lo_done", "w_lo_done", "rows_done", "setup"))
        first_lo_done = sem("first_lo_done")
        dve_held, pool_held = sem("dve_held"), sem("pool_held")
        first_group = prob[:, :, :, :].rearrange("p a h k -> p (a h k)").rearrange("p (w n) -> p w n", w=SEQS)
        block = ctx.enter_context(nc.Block())

        def held(eng, sem):
            eng.sem_inc(sem, 1)

        def run(eng, body):
            body(Step(-1), False, False, True)
            body(Step(0), False, True, True)
            with eng.Fori(0, (STEPS - 4) // 2) as trip:
                body(Step(1, trip), True, True, True)
                body(Step(2, trip), True, True, True)
            body(Step(STEPS - 3), True, True, True)
            body(Step(STEPS - 2), True, True, True)
            body(Step(STEPS - 1), True, True, False)
            body(Step(STEPS), True, False, False)

        @block.sync
        def _(sp):
            def load_w(w):
                sp.dma_start(w_raw[w.parity][:, :], t["att_w"][ds(w.times(1), 1), :, :].rearrange("a p n -> (a p) n")).then_inc(w_in[w.parity], 16)

            def load_x(m):
                b = m.times(1) % SEQS
                sp.dma_start(xs[m.parity][:, :].bitcast(F32), x1_split[ds(b, 1), :, :].rearrange("a p n -> (a p) n")).then_inc(x_in[m.parity], 16)
                sp.dma_start(rope[m.parity][:, :], rope_tab[ds(b, 1), :, :].rearrange("a p n -> (a p) n")).then_inc(x_in[m.parity], 16)

            def load_mask(m):
                sp.dma_start(mask[m.parity][:, :], mask_tab[ds(m.times(1) % SEQS, 1), :, :].rearrange("a p n -> (a p) n")).then_inc(mask_in[m.parity], 16)

            sp.dma_start(page_in[:, :], t["pages"]).then_inc(pages_in, 16)
            sp.dma_start(row_of[:, :], t["row_of"]).then_inc(pages_in, 16)
            sp.dma_start(head_no[:, :], t["head_no"]).then_inc(pages_in, 16)
            load_x(Step(0))

            def body(i, prev, cur, nxt):
                w, m = i.plus(9), i.plus(2)
                if not nxt:
                    return
                if not (isinstance(i.trip, int) and i.off == STEPS - 2):
                    sp.wait_ge(w_lo_done, w.times(1, -1))
                    load_w(w)
                if not m.first and not (isinstance(m.trip, int) and m.off in (1,)):
                    sp.wait_ge(kv_done, m.times(1, -1))
                    sp.wait_ge(k_roped, m.times(1, -1))
                if not (isinstance(i.trip, int) and i.off == STEPS - 2):
                    load_x(m)
                k = i.plus(1)
                if not isinstance(k.trip, int) or k.off >= 2:
                    sp.wait_ge(maxed, k.times(4, -4))
                load_mask(k)

            run(sp, body)

        @block.gpsimd
        def _(pool):
            pool.wait_ge(pages_in, 48)
            pool.tensor_scalar(page_row[:, :], page_in[:, :], PSIZE * KVH, None, ALU.mult).then_inc(setup, 1)
            pool.wait_ge(setup, 1)
            pool.tensor_tensor(page_row[:, :], page_row[:, :], row_of[:, :], ALU.add).then_inc(setup, 1)
            pool.wait_ge(setup, 2)
            pool.memset(minus_half[:, :], -0.5).then_inc(setup, 1)
            pool.wait_ge(setup, 3)

            def gather(m, tiles):
                p = m.parity
                if tiles[0] == 0:
                    pool.tensor_tensor(rows[p][:, :], page_row[:, ds((m.times(1) % SEQS) * KT, KT)],
                                       head_no[:, ds((m.times(1) // SEQS) * KT, KT)], ALU.add).then_inc(rows_done, 1)
                    pool.wait_ge(rows_done, m.times(1, 1))
                    held(pool, pool_held)
                for j in tiles:
                    pool.indirect_dma_start(kv[p][:, j, :], None, t["kv"],
                                            bass.IndirectOffsetOnAxis(ap=rows[p][:, j:j + 1], axis=0)).then_inc(kv_in[p], 16)

            def split_w(w):
                p = w.parity
                at = ((w.times(1) // SEQS) % 2) * GW + (w.times(1) % SEQS) * CHUNK
                pool.wait_ge(w_hi_done, w.times(1, 1))
                pool.tensor_tensor(w_lo[:, ds(at, CHUNK)], w_raw[p][:, :], w_hi[:, ds(at, CHUNK)].bitcast(F32), ALU.subtract).then_inc(w_lo_done, 1)

            gather(Step(0), range(KT))
            for n_split in (5, SEQS):
                pool.wait_ge(first_lo_done, n_split)
                pool.sem_inc(w_lo_done, 5 if n_split == 5 else SEQS - 5)

            def body(i, prev, cur, nxt):
                n, m = i.plus(1), i.plus(2)
                more = nxt and not (isinstance(i.trip, int) and i.off >= STEPS - 2)
                if cur and nxt:
                    split_w(i.plus(SEQS))
                if nxt:
                    pool.wait_ge(q_copied, n.times(1, 1))
                    if not n.first:
                        pool.wait_ge(q_roped, n.times(1))
                    sine = rope[n.parity][:, P:2 * P].unsqueeze(1).broadcast_to([P, QPK, P])
                    pool.wait_ge(x_in[n.parity], n.half(1) * 32)
                    pool.tensor_tensor(q_b[:, :].rearrange("p (h d) -> p h d", h=QPK), q_raw[:, :].rearrange("p (h d) -> p h d", h=QPK),
                                       sine, ALU.mult).then_inc(q_sin, 1)
                    pool.wait_ge(q_sin, n.times(1, 1))
                    pool.wait_ge(q_cos, n.times(1, 1))
                    by_half = [ap.rearrange("p (h s d) -> p h s d", h=QPK, s=2) for ap in (q_a[:, :], q_b[:, :])]
                    for s in range(2):
                        ins = pool.tensor_tensor(by_half[0][:, :, s, :], by_half[0][:, :, s, :], by_half[1][:, :, 1 - s, :], ALU.add)
                    ins.then_inc(q_roped, 1)
                if cur:
                    pool.wait_ge(v_hi_done, i.times(1, 1))
                    if i.off >= 2 or not isinstance(i.trip, int):
                        pool.wait_ge(pv_done, i.times(5, -5))
                    pool.tensor_tensor(v_lo[i.parity][:, :, :], kv[i.parity][:, :, P:2 * P], v_hi[i.parity][:, :, :].bitcast(F32),
                                       ALU.subtract).then_inc(v_lo_done, 1)
                if more:
                    if cur:
                        pool.wait_ge(v_lo_done, i.times(1, 1))
                        pool.wait_ge(turned, turn_no(i.plus(-1), "kc") + 1)
                        pool.wait_ge(k_roped, i.times(1, 1))
                    gather(m, range(KT - 1))
                if nxt:
                    pool.wait_ge(k_squared, n.times(1, 1))
                    if not n.first:
                        pool.wait_ge(k_roped, n.times(1))
                    held(pool, pool_held)
                    pool.tensor_scalar(rms_k[:, :], ssq_k[:, :], 1.0 / P, 1e-6, ALU.mult, ALU.add).then_inc(k_mean, 1)
                    pool.wait_ge(k_mean, n.times(1, 1))
                    pool.tensor_tensor(rms_k[:, :], rms_k[:, :], minus_half[:, 0:1], ALU.pow).then_inc(k_rms, 1)
                    pool.tensor_tensor(k_b[:, :], kv[n.parity][:, KT, 0:P], rope[n.parity][:, 3 * P:4 * P], ALU.mult).then_inc(k_sin, 1)
                if nxt:
                    pool.wait_ge(q_squared, n.times(1, 1))
                    if not n.first:
                        pool.wait_ge(q_scaled, n.times(1))
                    held(pool, pool_held)
                    pool.tensor_scalar(rms_q[:, :], ssq_q[:, :], 1.0 / P, 1e-6, ALU.mult, ALU.add).then_inc(q_mean, 1)
                    pool.wait_ge(q_mean, n.times(1, 1))
                    pool.tensor_tensor(rms_q[:, :], rms_q[:, :], minus_half[:, :], ALU.pow).then_inc(q_rms, 1)
                if more:
                    gather(m, range(KT - 1, KT))

            run(pool, body)

        @block.scalar
        def _(act):
            def split_w(w):
                p = w.parity
                at = ((w.times(1) // SEQS) % 2) * GW + (w.times(1) % SEQS) * CHUNK
                act.wait_ge(w_in[p], w.half(1 - SEQS // 2) * 16)
                act.activation(w_hi[:, ds(at, CHUNK)], w_raw[p][:, :], ACT.Copy).then_inc(w_hi_done, 1)

            for w in range(SEQS):
                act.activation(w_hi[:, w * CHUNK:(w + 1) * CHUNK], first_group[:, w, :], ACT.Copy).then_inc(w_hi_done, 1)

            def hi(i, name, out, width):
                no = turn_no(i, name)
                act.wait_ge(turned, no + 1)
                bank = turn_bank(i, name)
                act.activation(out, ps[:, bank, 0:width], ACT.Copy).then_inc(hi_done, 1)

            def softmax_exp(i, h):
                act.wait_ge(biased, i.times(4, h + 1))
                act.activation(prob[:, i.parity, h, :], prob[:, i.parity, h, :], ACT.Exp, bias=neg_top[:, h:h + 1],
                               scale=r_q[i.parity][:, h:h + 1], accum_out=den[:, h:h + 1]).then_inc(expd, 1)

            def body(i, prev, cur, nxt):
                n = i.plus(1)
                if cur and nxt:
                    act.wait_ge(kv_done, i.times(1))
                    if prev and not (isinstance(i.trip, int) and i.off == 1):
                        act.wait_ge(o_done, i.times(1, -1))
                    split_w(i.plus(SEQS))
                if prev:
                    hi(i, 1, pt_hi[1][:, :], DM)
                if cur:
                    softmax_exp(i, 0)
                if nxt:
                    act.wait_ge(q_done, n.times(1, 1))
                    if not n.first:
                        act.wait_ge(q_sin, n.times(1))
                        act.wait_ge(q_cos, n.times(1))
                        act.wait_ge(q_squared, n.times(1))
                    act.activation(q_raw[:, :], ps[:, BANK_P, :], ACT.Copy).then_inc(q_copied, 1)
                if prev:
                    hi(i, 2, pt_hi[0][:, :], DM)
                if cur:
                    act.wait_ge(kv_in[i.parity], i.half(1) * 16 * KT)
                    act.wait_ge(kv_copied, i.times(1, 1))
                    if i.off >= 2 or not isinstance(i.trip, int):
                        act.wait_ge(pv_done, i.times(5, -5))
                    act.activation(v_hi[i.parity][:, :, :], kv[i.parity][:, :, P:2 * P], ACT.Copy).then_inc(v_hi_done, 1)
                if prev:
                    hi(i, 3, pt_hi[1][:, :], DM)
                if cur:
                    softmax_exp(i, 1)
                if prev:
                    hi(i, 4, pt_hi[0][:, :], DM)
                if cur:
                    softmax_exp(i, 2)
                    act.wait_ge(inverted, i.times(4, 2))
                    act.activation(prob[:, i.parity, 1, :], prob[:, i.parity, 1, :], ACT.Copy, scale=inv[:, 1:2]).then_inc(normed_1, 1)
                    softmax_exp(i, 3)
                if nxt:
                    hi(i, "kc", kt_hi[:, 0:CACHE], CACHE)
                    act.wait_ge(kv_done, n.times(1, 1))
                    if i.off >= 1 or not isinstance(i.trip, int):
                        act.wait_ge(v_lo_done, n.times(1, -1))
                        act.wait_ge(k_rms, n.times(1))
                        act.wait_ge(k_squared, n.times(1))
                    act.activation(kv[n.parity][:, KT, :], ps[:, BANK_P, 0:2 * P], ACT.Copy).then_inc(kv_copied, 1)
                if prev:
                    act.wait_ge(pv_done, i.times(5, 0))
                    act.activation(ot_hi[:, :], ps[:, BANK_O, :], ACT.Copy).then_inc(o_hi_done, 1)
                if nxt:
                    act.wait_ge(kv_copied, n.times(1, 1))
                    act.activation(sq[:, QPK * P:], kv[n.parity][:, KT, 0:P], ACT.Square, accum_out=ssq_k[:, 0:1]).then_inc(k_squared, 1)
                    hi(i, "q", qt_hi[:, :], DM)
                if cur:
                    hi(n, 0, pt_hi[0][:, :], DM)
                if nxt:
                    act.wait_ge(q_copied, n.times(1, 1))
                    if not n.first:
                        act.wait_ge(q_rms, n.times(1))
                    for h in range(QPK):
                        ins = act.activation(sq[:, h * P:h * P + P], q_raw[:, h * P:h * P + P], ACT.Square, accum_out=ssq_q[:, h:h + 1])
                    ins.then_inc(q_squared, 1)
                    act.wait_ge(kn_turned, n.times(1, 1))
                    act.activation(kt_hi[:, CACHE:KEYS], ps[:, BANK_S, SPARE], ACT.Copy).then_inc(kn_hi_done, 1)

            run(act, body)

        @block.vector
        def _(dve):
            for w in range(SEQS):
                at = slice(w * CHUNK, (w + 1) * CHUNK)
                dve.wait_ge(w_hi_done, w + 1)
                dve.tensor_tensor(w_lo[:, at], first_group[:, w, :], w_hi[:, at].bitcast(F32), ALU.subtract).then_inc(first_lo_done, 1)
            dve.wait_ge(first_lo_done, SEQS)

            def lo(i, name, out, width, hi_part):
                no = turn_no(i, name)
                dve.wait_ge(hi_done, no + 1)
                bank = turn_bank(i, name)
                dve.tensor_tensor(out, ps[:, bank, 0:width], hi_part.bitcast(F32), ALU.subtract).then_inc(lo_done, 1)

            def masked_max(i, h):
                p = i.parity
                if h == 0:
                    dve.wait_ge(mask_in[p], i.half(1) * 16)
                    dve.wait_ge(q_scaled, i.times(1, 1))
                dve.wait_ge(s_done, i.times(4, h + 1))
                held(dve, dve_held)
                dve.tensor_tensor_reduce(prob[:, p, h, :].rearrange("p (a k) -> p a k", a=2),
                                         ps[:, BANK_S + 2 * (h % 2):BANK_S + 2 * (h % 2) + 2, 0:KEYS // 2],
                                         mask[p][:, :].rearrange("p (a k) -> p a k", a=2), 1.0, -3.0e38, ALU.add, ALU.max,
                                         top[:, h:h + 1]).then_inc(maxed, 1)
                dve.wait_ge(maxed, i.times(4, h + 1))
                if not i.first:
                    dve.wait_ge(expd, i.times(4, h - 3))
                dve.tensor_tensor(neg_top[:, h:h + 1], top[:, h:h + 1], neg_r_q[p][:, h:h + 1], ALU.mult).then_inc(biased, 1)

            def invert(i, h):
                dve.wait_ge(expd, i.times(4, h + 1))
                if not i.first:
                    dve.wait_ge(normed_1, i.times(1))
                dve.reciprocal(inv[:, h:h + 1], den[:, h:h + 1]).then_inc(inverted, 1)

            def normalise(i, h):
                p = i.parity
                invert(i, h)
                dve.wait_ge(inverted, i.times(4, h + 1))
                dve.tensor_scalar(prob[:, p, h, :], prob[:, p, h, :], inv[:, h:h + 1], None, ALU.mult).then_inc(normed, 1)

            def body(i, prev, cur, nxt):
                n = i.plus(1)
                if prev:
                    lo(i, 1, pt_lo[1][:, :], DM, pt_hi[1][:, :])
                if cur:
                    masked_max(i, 0)
                    normalise(i, 0)
                if nxt:
                    dve.wait_ge(q_copied, n.times(1, 1))
                    dve.wait_ge(x_in[n.parity], n.half(1) * 32)
                    if not n.first:
                        dve.wait_ge(turned, turn_no(i.plus(-1), "q") + 1)
                    cosine = rope[n.parity][:, 0:P].unsqueeze(1).broadcast_to([P, QPK, P])
                    dve.tensor_tensor(q_a[:, :].rearrange("p (h d) -> p h d", h=QPK), q_raw[:, :].rearrange("p (h d) -> p h d", h=QPK),
                                      cosine, ALU.mult).then_inc(q_cos, 1)
                    if not cur:
                        dve.memset(att[:, :, :], 0.0).then_inc(cleared, 1)
                if prev:
                    lo(i, 2, pt_lo[0][:, :], DM, pt_hi[0][:, :])
                if cur:
                    masked_max(i, 1)
                if prev:
                    lo(i, 3, pt_lo[1][:, :], DM, pt_hi[1][:, :])
                if cur:
                    masked_max(i, 2)
                    invert(i, 1)
                if cur:
                    masked_max(i, 3)
                if prev:
                    lo(i, 4, pt_lo[0][:, :], DM, pt_hi[0][:, :])
                if cur:
                    normalise(i, 2)
                    normalise(i, 3)
                if nxt:
                    lo(i, "kc", kt_lo[:, 0:CACHE], CACHE, kt_hi[:, 0:CACHE])
                if prev:
                    dve.wait_ge(o_hi_done, i.times(1, 0))
                    dve.tensor_tensor(ot_lo[:, :], ps[:, BANK_O, :], ot_hi[:, :].bitcast(F32), ALU.subtract).then_inc(o_lo_done, 1)
                if nxt:
                    dve.wait_ge(k_rms, n.times(1, 1))
                    if not n.first:
                        dve.wait_ge(kn_turned, n.times(1))
                    dve.scalar_tensor_tensor(out=k_a[:, :], in0=kv[n.parity][:, KT, 0:P], scalar=rms_k[:, 0:1],
                                             in1=rope[n.parity][:, 2 * P:3 * P], op0=ALU.mult, op1=ALU.mult).then_inc(k_cos, 1)
                    dve.wait_ge(k_cos, n.times(1, 1))
                    dve.wait_ge(k_sin, n.times(1, 1))
                    dve.scalar_tensor_tensor(out=k_a[:, 0:64], in0=k_b[:, 64:P], scalar=rms_k[:, 0:1], in1=k_a[:, 0:64],
                                             op0=ALU.mult, op1=ALU.add)
                    dve.scalar_tensor_tensor(out=k_a[:, 64:P], in0=k_b[:, 0:64], scalar=rms_k[:, 0:1], in1=k_a[:, 64:P],
                                             op0=ALU.mult, op1=ALU.add).then_inc(k_roped, 1)
                    lo(i, "q", qt_lo[:, :], DM, qt_hi[:, :])
                if cur:
                    lo(n, 0, pt_lo[0][:, :], DM, pt_hi[0][:, :])
                if nxt:
                    dve.wait_ge(kn_hi_done, n.times(1, 1))
                    dve.tensor_tensor(kt_lo[:, CACHE:KEYS], ps[:, BANK_S, SPARE], kt_hi[:, CACHE:KEYS].bitcast(F32),
                                      ALU.subtract).then_inc(kn_lo_done, 1)
                if prev:
                    dve.wait_ge(o_done, i.times(1, 0))
                    dve.wait_ge(cleared, 1)
                    if not (isinstance(i.trip, int) and i.off == 1):
                        dve.wait_ge(summed, i.times(1, -1))
                    here = att[:, ds(i.plus(-1).times(1) % SEQS, 1), :].rearrange("p a n -> p (a n)")
                    dve.tensor_tensor(here, ps[:, BANK_P, :], here, ALU.add).then_inc(summed, 1)
                if nxt:
                    dve.wait_ge(q_rms, n.times(1, 1))
                    if i.off >= 1 or not isinstance(i.trip, int):
                        dve.wait_ge(expd, n.times(4, -4))
                    dve.tensor_scalar(r_q[n.parity][:, :], rms_q[:, :], SCALE, None, ALU.mult)
                    dve.tensor_scalar(neg_r_q[n.parity][:, :], rms_q[:, :], -SCALE, None, ALU.mult).then_inc(q_scaled, 1)

            run(dve, body)

        @block.tensor
        def _(pe):
            def group_base(m):
                base = ((m.times(1) // SEQS) % 2) * GW
                return base if isinstance(base, int) else pe.snap(base)

            def project(n, base, at, width, out, done):
                for c in range(CT):
                    x = xs[n.parity][:, c * P:c * P + P], xs[n.parity][:, DM + c * P:DM + c * P + P]
                    w = [part[:, ds(base + (at + c * width), width)] for part in (w_hi, w_lo)]
                    ins = mm3(pe, out, x, w, c == 0, c == CT - 1)
                ins.then_inc(done, 1)

            def turn(i, name, blocks, no_wait=False):
                no = turn_no(i, name)
                if i.first:
                    pe.wait_ge(lo_done, no)
                else:
                    pe.wait_ge(lo_done, no - 1)
                bank = turn_bank(i, name)
                for j, block_ap in enumerate(blocks):
                    ins = pe.transpose(ps[:, bank, j * P:j * P + P], block_ap, ident)
                ins.then_inc(turned, 1)

            def turn_probs(i, j):
                if j == 0:
                    pe.wait_ge(normed, i.times(3, 0))
                    pe.wait_ge(normed_1, i.times(1, 0))
                turn(i, j, [prob[:, 1 - i.parity, h, j * P:j * P + P] for h in range(QPK)])

            def scores(i, h):
                if h == 0:
                    pe.wait_ge(lo_done, turn_no(i.plus(-1), "q") + 1)
                    pe.wait_ge(kn_lo_done, i.times(1, 1))
                if not (isinstance(i.trip, int) and i.off == 0 and h < 2):
                    pe.wait_ge(maxed, i.times(4, h - 1))
                q = slice(h * P, h * P + P)
                banks = [(ps[:, BANK_S + 2 * (h % 2) + a, 0:KEYS // 2], slice(a * KEYS // 2, (a + 1) * KEYS // 2)) for a in range(2)]
                for out, k in banks:
                    ins = mm3(pe, out, (qt_hi[:, q], qt_lo[:, q]), (kt_hi[:, k], kt_lo[:, k]), True, True)
                ins.then_inc(s_done, 1)

            def values(i, j):
                v = 1 - i.parity
                if j == 0:
                    pe.wait_ge(v_lo_done, i.times(1, 0))
                    if not (isinstance(i.trip, int) and i.off == 1):
                        pe.wait_ge(o_lo_done, i.times(1, -1))
                pe.wait_ge(lo_done, turn_no(i, j) + 1)
                mm3(pe, ps[:, BANK_O, :], (v_hi[v][:, j, :], v_lo[v][:, j, :]), (pt_hi[j % 2][:, :], pt_lo[j % 2][:, :]),
                    j == 0, j == KT).then_inc(pv_done, 1)

            def output(i, base, heads):
                for h in heads:
                    w = [part[:, ds(base + (QW + KVW + h * DM), DM)] for part in (w_hi, w_lo)]
                    ins = mm3(pe, ps[:, BANK_P, :], (ot_hi[:, h * P:h * P + P], ot_lo[:, h * P:h * P + P]), w, h == 0, h == QPK - 1)
                return ins

            def body(i, prev, cur, nxt):
                n = i.plus(1)
                if nxt:
                    qkv_base = group_base(n)
                if prev:
                    o_base = group_base(i.plus(-1))
                    turn_probs(i, 1)
                if nxt:
                    pe.wait_ge(x_in[n.parity], n.half(1) * 32)
                    if cur:
                        pe.wait_ge(w_lo_done, i.times(1, 6))
                    else:
                        pe.wait_ge(first_lo_done, 5)
                if cur:
                    scores(i, 0)
                if nxt:
                    if prev and not (isinstance(i.trip, int) and i.off == 1):
                        pe.wait_ge(summed, i.times(1, -1))
                    project(n, qkv_base, 0, DM, ps[:, BANK_P, :], q_done)
                if prev:
                    values(i, 0)
                    turn_probs(i, 2)
                if cur:
                    scores(i, 1)
                if prev:
                    values(i, 1)
                    turn_probs(i, 3)
                if cur:
                    scores(i, 2)
                if prev:
                    values(i, 2)
                    turn_probs(i, 4)
                if cur:
                    scores(i, 3)
                if nxt:
                    pe.wait_ge(q_copied, n.times(1, 1))
                    project(n, qkv_base, QW, 2 * P, ps[:, BANK_P, 0:2 * P], kv_done)
                if nxt:
                    pe.wait_ge(kv_in[n.parity], n.half(1) * 16 * KT)
                    turn(i, "kc", [kv[n.parity][:, j, 0:P] for j in range(KT)])
                if prev:
                    values(i, 3)
                    values(i, 4)
                if nxt:
                    pe.wait_ge(q_roped, n.times(1, 1))
                    turn(i, "q", [q_a[:, h * P:h * P + P] for h in range(QPK)])
                if prev:
                    if nxt:
                        pe.wait_ge(kv_copied, n.times(1, 1))
                    elif not cur:
                        pe.wait_ge(summed, i.times(1, -1))
                    pe.wait_ge(w_lo_done, (i.times(1, 7) if nxt else STEPS + SEQS - 1))
                if cur:
                    turn_probs(n, 0)
                if prev:
                    pe.wait_ge(o_lo_done, i.times(1, 0))
                    output(i, o_base, range(QPK // 2))
                if nxt:
                    pe.wait_ge(k_roped, n.times(1, 1))
                    pe.transpose(ps[:, BANK_S, SPARE], k_a[:, :], ident).then_inc(kn_turned, 1)
                if prev:
                    output(i, o_base, range(QPK // 2, QPK)).then_inc(o_done, 1)

            run(pe, body)


def last_layer(nc, t, ps, cst, ones, prob, w_hi, w_lo, x1_split, att):
    ident, iota = cst[:, C_ID:C_ID + P], cst[:, C_IOTA:C_IOTA + EXP]
    with ExitStack() as ctx:
        sb = lambda n, s, d=F32: ctx.enter_context(nc.sbuf_tensor(n, s, d))
        sem = lambda n: ctx.enter_context(nc.semaphore(n))
        x1 = sb("x1", [P, CT, TOK])
        x1_lo = prob[:, :, :, :].rearrange("p a h k -> p (a h k)")[:, 0:CT * TOK].rearrange("p (c n) -> p c n", c=CT)
        z_hi, z_lo = (part[:, GW:GW + CT * TOK].rearrange("p (c n) -> p c n", c=CT) for part in (w_hi, w_lo))
        L = Layer(sb, "ffn1", GH, (w_hi, w_lo))
        wk = Work(sb, sem, "b1")
        small = sb("small1", [P, 4 * GH + EXP])
        gw2 = sb("gw2", [GH, EXP])
        hid = sb("ghid", [P, SEQS, GH])
        cen = sb("gcen", [P, SEQS, GH])
        st = sb("gst", [P, 4, SEQS])
        hid_t = sb("ghid_t", [GH, SEQS, P])
        lg = sb("glg", [P, SEQS, EXP])
        t2 = top2_buffers(sb, "t3")
        allowed = sb("allowed", [P, 2, EXP])
        late_banks = (4, 5, 0, 1)
        s_x1, s_small, x1_ready = sem("x1_in"), sem("small1_in"), sem("x1_ready")
        blk_turned, blk_hi, blk_lo, chain, exp_in, exp_out, hid_ready, hid_turned, hid_t_done, logits2, hot_ready, counted, out_ready, stored, var_ready, std_ready = (
            sem(n) for n in ("blk_turned", "blk_hi", "blk_lo", "chain1", "exp1_in", "exp1_out", "hid_ready", "hid_turned",
                             "hid_t_done", "logits2", "hot_ready", "counted", "out_ready", "stored1", "var_ready", "std_ready"))
        block = ctx.enter_context(nc.Block())

        @block.sync
        def _(sp):
            sp.dma_start(L.route_w[:, :, :], t["ffn1_route"]).then_inc(s_small, 16)
            sp.dma_start(small[:, :], t["ffn1_small"]).then_inc(s_small, 16)
            sp.dma_start(gw2[:, :], t["ffn1_gw2"]).then_inc(s_small, 16)
            for j, part in enumerate((x1, x1_lo)):
                for b in range(SEQS):
                    sp.dma_start(part[:, :, b * P:b * P + P],
                                 x1_split[b, :, j * DM:(j + 1) * DM].rearrange("p (c n) -> p c n", c=CT)).then_inc(s_x1, 16)
            for h in range(2):
                for o in range(CT):
                    sp.wait_ge(out_ready, 4 * h + o + 1)
                    sp.dma_start(t["out"][:, o, halves(h)], x1[:, o, halves(h)]).then_inc(stored, 16)
            sp.wait_ge(stored, 16 * 8)

        @block.gpsimd
        def _(pool):
            pool.wait_ge(var_ready, 1)
            pool.tensor_tensor(st[:, 2, :], st[:, 1, :], st[:, 3, :], ALU.pow).then_inc(std_ready, 1)
            pool.wait_ge(s_x1, 16 * 2 * SEQS)
            pool.tensor_tensor(x1[:, :, :], x1[:, :, :], x1_lo, ALU.add).then_inc(x1_ready, 1)

        @block.scalar
        def _(act):
            def split_block(b):
                act.wait_ge(blk_turned, b + 1)
                turned = ps[:, b % 4, :].rearrange("p (c n) -> p c n", c=CT)
                act.activation(z_hi[:, :, b * P:b * P + P], turned, ACT.Copy).then_inc(blk_hi, 1)

            for b in range(SEQS):
                split_block(b)
                if b == 3:
                    act.wait_ge(s_small, 48)
                    act.activation(L.route_hi[:, :, :], L.route_w[:, :, :], ACT.Copy).then_inc(wk.route_hi_done, 1)
            layer_logits_scalar(act, 0, ps, L, wk)
            act.wait_ge(exp_in, 1)
            act.activation(t2["small"][:, 1, :], t2["small"][:, 0, :], ACT.Exp).then_inc(exp_out, 1)
            layer_hidden_scalar(act, 0, ps, wk)
            for h in range(2):
                layer_gated_scalar(act, 0, h, wk)

        @block.vector
        def _(dve):
            n = [0]

            def link(ins):
                n[0] += 1
                ins.then_inc(chain, 1)
                dve.wait_ge(chain, n[0])

            for b in range(SEQS):
                dve.wait_ge(blk_hi, b + 1)
                dve.tensor_tensor(z_lo[:, :, b * P:b * P + P], ps[:, b % 4, :].rearrange("p (c n) -> p c n", c=CT),
                                  z_hi[:, :, b * P:b * P + P].bitcast(F32), ALU.subtract).then_inc(blk_lo, 1)
                if b == 3:
                    dve.wait_ge(wk.route_hi_done, 1)
                    dve.tensor_tensor(L.route_lo[:, :, :], L.route_w[:, :, :], L.route_hi[:, :, :].bitcast(F32),
                                      ALU.subtract).then_inc(wk.route_lo_done, 1)
            dve.wait_ge(s_small, 48)
            dve.wait_ge(wk.logits_done, 1)
            shape = [P, SEQS, GH]
            row = lambda k: bcast(small[:, k * GH:(k + 1) * GH], shape, 1)
            link(dve.tensor_tensor(hid[:, :, :], ps[:, 7, 0:SEQS * GH].rearrange("p (b e) -> p b e", b=SEQS), row(0), ALU.add))
            link(dve.memset(st[:, 2, :], 0.0))
            link(dve.tensor_reduce(st[:, 0, :], hid[:, :, :], AX.X, ALU.add))
            link(dve.tensor_scalar(st[:, 0, :], st[:, 0, :], 1.0 / GH, None, ALU.mult))
            link(dve.tensor_tensor(hid[:, :, :], hid[:, :, :], bcast(st[:, 0, :], shape, 2), ALU.subtract))
            link(dve.tensor_tensor(cen[:, :, :], hid[:, :, :], hid[:, :, :], ALU.mult))
            link(dve.tensor_reduce(st[:, 1, :], cen[:, :, :], AX.X, ALU.add))
            link(dve.tensor_scalar(st[:, 1, :], st[:, 1, :], 1.0 / GH, 1e-5, ALU.mult, ALU.add))
            dve.tensor_scalar(st[:, 3, :], st[:, 2, :], 0.0, -0.5, ALU.mult, ALU.add).then_inc(var_ready, 1)
            dve.wait_ge(std_ready, 1)
            link(dve.tensor_tensor(hid[:, :, :], hid[:, :, :], bcast(st[:, 2, :], shape, 2), ALU.mult))
            link(dve.tensor_tensor(hid[:, :, :], hid[:, :, :], row(1), ALU.mult))
            link(dve.tensor_tensor(hid[:, :, :], hid[:, :, :], row(2), ALU.add))
            dve.tensor_scalar(hid[:, :, :], hid[:, :, :], 0.0, None, ALU.max).then_inc(hid_ready, 1)
            dve.wait_ge(hid_turned, 1)
            dve.tensor_copy(hid_t[:, :, :], ps[0:GH, 6:8, :].rearrange("p a (b n) -> p (a b) n", b=4)).then_inc(hid_t_done, 1)
            dve.wait_ge(logits2, 1)
            link(dve.tensor_tensor(lg[:, :, :], ps[:, 7, 0:SEQS * EXP].rearrange("p (b e) -> p b e", b=SEQS),
                                   bcast(small[:, 3 * GH:3 * GH + EXP], [P, SEQS, EXP], 1), ALU.add))
            top2_gates(dve, link, lg, iota, t2, lambda: dve.wait_ge(exp_out, 1), exp_in, 1.0 / RANK)
            dve.drain().then_inc(hot_ready, 1)
            dve.wait_ge(counted, 1)
            link(dve.tensor_scalar(allowed[:, :, :], ps[:, 7, 0:2 * EXP].rearrange("p (c e) -> p c e", c=2), float(CAPACITY), None, ALU.is_le))
            link(dve.tensor_tensor(t2["hot_g"][:, :, :, :], t2["hot_g"][:, :, :, :],
                                   allowed[:, :, :].unsqueeze(1).broadcast_to([P, SEQS, 2, EXP]), ALU.mult))
            link(dve.tensor_tensor(wk.gate[:, :, :], t2["hot_g"][:, :, 0, :], t2["hot_g"][:, :, 1, :], ALU.add))
            widen_gates(dve, wk)
            dve.wait_ge(x1_ready, 1)
            for h in range(2):
                layer_gated_vector(dve, 0, h, ps, wk)
                for o in range(CT):
                    dve.wait_ge(wk.out_done, 4 * h + o + 1)
                    dve.tensor_tensor(x1[:, o, halves(h)], ps[:, late_banks[o] if h else o, :], x1[:, o, halves(h)], ALU.add).then_inc(out_ready, 1)

        @block.tensor
        def _(pe):
            for b in range(SEQS):
                if b >= 4:
                    pe.wait_ge(blk_lo, b - 3)
                for c in range(CT):
                    ins = pe.transpose(ps[:, b % 4, c * P:c * P + P], att[:, b, c * P:c * P + P], ident)
                ins.then_inc(blk_turned, 1)

            def gate_turn(pe):
                pe.wait_ge(hid_ready, 1)
                for b in range(SEQS):
                    ins = pe.transpose(ps[0:GH, 6 + b // 4, (b % 4) * P:(b % 4) * P + P], hid[:, b, :], ident)
                ins.then_inc(hid_turned, 1)

            def gate_out(pe):
                pe.wait_ge(hid_t_done, 1)
                for b in range(SEQS):
                    ins = pe.matmul(ps[:, 7, b * EXP:b * EXP + EXP], hid_t[:, b, :], gw2[:, :], start=True, stop=True)
                ins.then_inc(logits2, 1)

            def count(pe):
                pe.wait_ge(hot_ready, 1)
                for b in range(SEQS):
                    ins = pe.matmul(ps[:, 7, 0:2 * EXP], ones[:, :], t2["hot"][:, b, :, :].rearrange("p c e -> p (c e)"),
                                    start=(b == 0), stop=(b == SEQS - 1))
                ins.then_inc(counted, 1)

            part = LayerTensor(pe, 0, ps, ident, z_hi, z_lo, L, wk)
            pe.wait_ge(blk_lo, SEQS)
            part.logits()
            part.hidden(0)
            part.turn_logits()
            part.hidden(1)
            part.base(0, 0, 0)
            gate_turn(pe)
            part.base(0, 1, 1)
            gate_out(pe)
            part.base(0, 2, 2)
            part.base(0, 3, 3)
            count(pe)
            pe.wait_ge(wk.hid_copied, 2)
            part.base(1, 0, late_banks[0])
            part.turn_gates(0)
            part.base(1, 1, late_banks[1])
            part.experts(0, range(CT))
            pe.wait_ge(out_ready, 1)
            part.base(1, 2, late_banks[2])
            part.turn_gates(1)
            pe.wait_ge(out_ready, 2)
            part.base(1, 3, late_banks[3])
            part.experts(1, late_banks)


def _features_first(a):
    return np.ascontiguousarray(a.reshape(a.shape[0], CT, P).transpose(2, 1, 0))


def _on_all(a):
    return np.ascontiguousarray(np.broadcast_to(np.asarray(a).reshape(1, -1), (P, np.asarray(a).size)))


def _constants():
    c = np.zeros((P, C_ALL), np.float32)
    c[:, C_ID:C_ID + P] = np.eye(P)
    c[:, C_IOTA:C_IOTA + 16] = np.arange(16)
    c[:, C_FREQ:C_FREQ + 64] = np.float32(1.0) / (10000.0 ** (np.arange(0, P, 2) / P)).astype(np.float32)
    c[:, C_KEY:C_KEY + CACHE] = np.arange(CACHE)
    return c


def kernel(**inputs):
    import concourse.bacc as bacc
    from concourse.bass_utils import run_bass_kernel_spmd

    a = {k: np.asarray(v) for k, v in inputs.items()}

    def with_lora(w, la):
        return np.ascontiguousarray(np.concatenate([_features_first(w), _features_first(la)], axis=2))

    groups = []
    for g in range(KVH):
        q = _features_first(a["L1_cond_Wq"][g * DM:(g + 1) * DM]).reshape(P, QW)
        k = _features_first(a["L1_cond_Wk"][g * P:(g + 1) * P])
        v = _features_first(a["L1_cond_Wv"][g * P:(g + 1) * P])
        kv = np.concatenate([k, v], axis=2).reshape(P, KVW)
        o = _features_first(a["L1_cond_Wo"][:, g * DM:(g + 1) * DM]).reshape(P, OW)
        groups.append(np.concatenate([q, kv, o], axis=1).reshape(P, SEQS, CHUNK).transpose(1, 0, 2))
    last = np.zeros((P, GW), np.float32)
    last[:, 0:LW] = with_lora(a["L1_ffn_weight"], a["L1_ffn_lora_A"].transpose(0, 2, 1).reshape(P, DM)).reshape(P, LW)
    last[:, LW:LW + DM] = a["L1_ffn_lora_B"].reshape(P, DM)
    groups.append(last.reshape(P, SEQS, CHUNK).transpose(1, 0, 2))
    part = np.arange(P, dtype=np.int32)
    feed = {
        "consts": _constants(),
        "tokid": part.astype(np.float32).reshape(P, 1),
        "lens": _on_all(a["itok_B_207_1644"]),
        "normw": _on_all(np.concatenate([a["L1_cond_q_norm_w"], a["L1_cond_k_norm_w"]])),
        "x": _features_first(a["x"].reshape(TOK, DM)),
        "lang": _on_all(a["itok_B_0_7"]),
        "cond0_w": with_lora(a["L0_cond_W"], a["L0_cond_A"].reshape(P, DM)),
        "cond0_lb": np.ascontiguousarray(a["L0_cond_B"].transpose(0, 2, 1).reshape(P, DM)),
        "cond0_route": _features_first(a["L0_cond_Wr"]),
        "ffn0_w": with_lora(a["L0_ffn_base_W"], a["L0_ffn_A"].reshape(P, DM)),
        "ffn0_lb": np.ascontiguousarray(a["L0_ffn_B"].transpose(0, 2, 1).reshape(P, DM)),
        "ffn0_route": _features_first(a["L0_ffn_router_W"]),
        "ffn0_b": np.ascontiguousarray(a["L0_ffn_base_b"].reshape(CT, P).T),
        "ffn0_route_b": _on_all(a["L0_ffn_router_b"]),
        "emap": _on_all(a["L0_ffn_expert_map"]),
        "att_w": np.ascontiguousarray(np.concatenate(groups, axis=0)),
        "kv": np.ascontiguousarray(np.concatenate([a["L1_cond_k_cache"], a["L1_cond_v_cache"]], axis=3).reshape(-1, 2 * P)),
        "pages": np.ascontiguousarray(np.repeat(a["itok_Bx16_0_63"].reshape(SEQS, KT, P // PSIZE), PSIZE, axis=2).transpose(2, 0, 1).reshape(P, SEQS * KT)),
        "row_of": np.ascontiguousarray(np.broadcast_to(((part % PSIZE) * KVH)[:, None], (P, SEQS * KT))),
        "head_no": _on_all(np.repeat(np.arange(KVH, dtype=np.int32), KT)),
        "ffn1_route": _features_first(a["L1_ffn_gw1"]),
        "ffn1_small": _on_all(np.concatenate([a["L1_ffn_gb1"], a["L1_ffn_ln_gamma"], a["L1_ffn_ln_beta"], a["L1_ffn_gb2"],
                                              np.zeros(GH, np.float32)])),
        "ffn1_gw2": np.ascontiguousarray(a["L1_ffn_gw2"].T),
    }
    nc = bacc.Bacc("TRN2", target_bir_lowering=False, num_devices=1)
    t = {k: nc.dram_tensor("in_" + k, v.shape, mybir.dt.from_np(v.dtype), kind="ExternalInput").ap() for k, v in feed.items()}
    t["out"] = nc.dram_tensor("out_0", (P, CT, TOK), F32, kind="ExternalOutput").ap()
    build(nc, t)
    r = run_bass_kernel_spmd(nc, [{"in_" + k: v for k, v in feed.items()}], core_ids=[0])
    out = r.results[0]["out_0"]
    return np.ascontiguousarray(out.transpose(2, 1, 0).reshape(SEQS, P, DM))
```

```python
from contextlib import ExitStack

import numpy as np

import concourse.bass as bass
from concourse import mybir

F32 = mybir.dt.float32
F32R = mybir.dt.float32r
I32 = mybir.dt.int32
U32 = mybir.dt.uint32
ALU = mybir.AluOpType
ACT = mybir.ActivationFunctionType
AX = mybir.AxisListType
ds = bass.ds

P = 128
SEQS = 8
TOK = SEQS * P
DM = 512
CT = DM // P
HALF = TOK // 2
KVH = 8
QPK = 4
PSIZE = 32
NPP = 16
CACHE = PSIZE * NPP
KT = CACHE // P
KEYS = CACHE + P
STEPS = KVH * SEQS
EXP = 8
RANK = 16
NR1 = 2 * EXP - 1
GH = 4 * EXP
CAPACITY = int(3.0 * TOK / EXP)
QW, KVW, OW = CT * DM, CT * 2 * P, QPK * DM
GW = QW + KVW + OW
CHUNK = GW // SEQS
LW = CT * (DM + P)
SCALE = 1.0 / float(np.sqrt(P))
MASKED = -1e30

TWO_PI_1 = 6.28125
TWO_PI_2 = float(np.float32(np.round((2 * np.pi - TWO_PI_1) * 2.0**21) / 2.0**21))
TWO_PI_3 = float(np.float32(2 * np.pi - TWO_PI_1 - TWO_PI_2))
ROUND = 1.5 * 2.0**23

C_ID, C_IOTA, C_FREQ, C_KEY = 0, P, P + 16, P + 80
C_ALL = C_KEY + CACHE


class Step:

    def __init__(self, off, trip=0):
        self.off, self.trip = off, trip

    @property
    def parity(self):
        return self.off % 2

    def half(self, add=0):
        return self.trip + (self.off // 2 + add)

    def times(self, m, add=0):
        if isinstance(self.trip, int):
            return m * (2 * self.trip + self.off) + add
        return self.trip * (2 * m) + (m * self.off + add)

    def plus(self, n):
        return Step(self.off + n, self.trip)

    @property
    def first(self):
        return isinstance(self.trip, int) and 2 * self.trip + self.off <= 0

    @property
    def after_last(self):
        return isinstance(self.trip, int) and self.off == STEPS

    def turned(self, add=0):
        if self.first:
            return self.off + 1 + add
        if self.after_last:
            add -= 1
        return self.times(6, add - 4)


QUERIES = 5


def turn_no(i, j):
    return i.turned(j - QUERIES) if i.first else i.turned(j)


class Ahead:

    def __init__(self, sb):
        self.xs = [sb(f"xs{p}", [P, 2 * DM], F32R) for p in range(2)]
        self.page_row = sb("page_row", [P, SEQS * KT], I32)
        self.page_in, self.row_of = sb("page_in", [P, SEQS * KT], I32), sb("row_of", [P, SEQS * KT], I32)
        self.head_no = sb("head_no", [P, KVH * KT], I32)


def build(nc, t):
    top = ExitStack()
    with top:
        ps = top.enter_context(nc.psum_tensor("ps", [P, 8, 512], F32))
        cst = top.enter_context(nc.sbuf_tensor("cst", [P, C_ALL], F32))
        ident = cst[:, C_ID:C_ID + P]
        ones = top.enter_context(nc.sbuf_tensor("ones", [P, P], F32))
        x1_split = nc.dram_tensor("x1_split", (SEQS, P, 2 * DM), F32, kind="Internal").ap()
        rope_tab = nc.dram_tensor("rope_tab", (SEQS, P, 4 * P), F32, kind="Internal").ap()
        mask_tab = nc.dram_tensor("mask_tab", (SEQS, P, KEYS), F32, kind="Internal").ap()
        prob = top.enter_context(nc.sbuf_tensor("prob", [P, 2, QPK, KEYS], F32))
        ahead = Ahead(lambda n, s, d=F32: top.enter_context(nc.sbuf_tensor(n, s, d)))
        first_block(nc, t, ps, cst, ones, prob, ahead, x1_split, rope_tab, mask_tab)
        att = top.enter_context(nc.sbuf_tensor("att", [P, SEQS, DM], F32))
        w_hi = top.enter_context(nc.sbuf_tensor("w_hi", [P, 2 * GW], F32R))
        w_lo = top.enter_context(nc.sbuf_tensor("w_lo", [P, 2 * GW], F32R))
        attention(nc, t, ps, cst, prob, ahead, w_hi, w_lo, x1_split, rope_tab, mask_tab, att)
        last_layer(nc, t, ps, cst, ones, prob, w_hi, w_lo, x1_split, att)


class Tables:

    def __init__(self, sb, sem, cst, rope_tab, mask_tab):
        self.cst, self.rope_tab, self.mask_tab = cst, rope_tab, mask_tab
        self.lens, self.tokid, self.normw = sb("lens", [P, SEQS], I32), sb("tokid", [P, 1]), sb("normw", [P, 2 * P])
        self.lenf, self.lenm, self.pos = sb("lenf", [P, SEQS]), sb("lenm", [P, SEQS]), sb("pos", [P, SEQS])
        self.sin, self.cos, self.turns = (sb(n, [P, SEQS, 64]) for n in ("sin", "cos", "turns"))
        self.part = [sb(f"table_part{p}", [P, SEQS, P]) for p in range(2)]
        self.mask = [sb(f"mask_part{p}", [P, KEYS]) for p in range(2)]
        self.loaded, self.reduced, self.trig = sem("table_inputs_in"), sem("angles_reduced"), sem("trig")
        self.masked, self.tabbed, self.lenm_ready = sem("masks_ready"), sem("table_part_ready"), sem("lenm_ready")
        self.mask_stored, self.tab_stored = ([sem(f"{n}{p}") for p in range(2)] for n in ("masks_stored", "tables_stored"))

    def load(self, sp, t):
        sp.dma_start(self.cst[:, :], t["consts"]).then_inc(self.loaded, 16)
        sp.dma_start(self.lens[:, :], t["lens"]).then_inc(self.loaded, 16)
        sp.dma_start(self.tokid[:, :], t["tokid"]).then_inc(self.loaded, 16)
        sp.dma_start(self.normw[:, :], t["normw"]).then_inc(self.loaded, 16)

    def store_masks(self, sp):
        for b in range(SEQS):
            sp.wait_ge(self.masked, b + 1)
            sp.dma_start(self.mask_tab[b], self.mask[b % 2][:, :]).then_inc(self.mask_stored[b % 2], 16)

    def store_tables(self, sp):
        for j in range(4):
            sp.wait_ge(self.tabbed, j + 1)
            sp.dma_start(self.rope_tab[:, :, j * P:j * P + P].rearrange("b p k -> p b k"), self.part[j % 2][:, :, :]).then_inc(self.tab_stored[j % 2], 16)

    def angles(self, dve, link):
        shape = [P, SEQS, 64]
        ang, cosr, turns = self.sin, self.cos, self.turns
        dve.wait_ge(self.loaded, 64)
        link(dve.tensor_copy(self.lenf[:, :], self.lens[:, :]))
        link(dve.tensor_scalar(self.pos[:, :], self.lenf[:, :], self.tokid[:, 0:1], None, ALU.add))
        freq = self.cst[:, C_FREQ:C_FREQ + 64].unsqueeze(1).broadcast_to(shape)
        link(dve.tensor_tensor(ang[:, :, :], self.pos[:, :].unsqueeze(2).broadcast_to(shape), freq, ALU.mult))
        link(dve.tensor_scalar(turns[:, :, :], ang[:, :, :], float(1 / (2 * np.pi)), None, ALU.mult))
        link(dve.tensor_scalar(turns[:, :, :], turns[:, :, :], ROUND, None, ALU.add))
        link(dve.tensor_scalar(turns[:, :, :], turns[:, :, :], ROUND, None, ALU.subtract))
        for part in (TWO_PI_1, TWO_PI_2, TWO_PI_3):
            link(dve.scalar_tensor_tensor(out=ang[:, :, :], in0=turns[:, :, :], scalar=-part, in1=ang[:, :, :],
                                          op0=ALU.mult, op1=ALU.add))
        below_pi = float(np.float32(3.1415925))
        link(dve.tensor_scalar(ang[:, :, :], ang[:, :, :], below_pi, -below_pi, ALU.min, ALU.max))
        link(dve.tensor_scalar(cosr[:, :, :], ang[:, :, :], float(np.pi / 2), None, ALU.add))
        link(dve.tensor_scalar(turns[:, :, :], cosr[:, :, :], float(np.pi), float(-2 * np.pi), ALU.is_gt, ALU.mult))
        link(dve.tensor_tensor(cosr[:, :, :], cosr[:, :, :], turns[:, :, :], ALU.add))
        dve.tensor_scalar(cosr[:, :, :], cosr[:, :, :], below_pi, -below_pi, ALU.min, ALU.max).then_inc(self.reduced, 1)

    def lengths(self, pool):
        pool.wait_ge(self.loaded, 64)
        pool.tensor_copy(self.lenm[:, :], self.lens[:, :]).then_inc(self.lenm_ready, 1)
        pool.wait_ge(self.lenm_ready, 1)

    def sines(self, act):
        act.wait_ge(self.reduced, 1)
        act.activation(self.sin[:, :, :], self.sin[:, :, :], ACT.Sin).then_inc(self.trig, 1)
        act.activation(self.cos[:, :, :], self.cos[:, :, :], ACT.Sin).then_inc(self.trig, 1)

    def masks(self, pool):
        for buf in self.mask:
            pool.memset(buf[:, CACHE:], 0.0)
        for b in range(SEQS):
            if b >= 2:
                pool.wait_ge(self.mask_stored[b % 2], 16 * (b // 2))
            pool.tensor_scalar(self.mask[b % 2][:, 0:CACHE], self.cst[:, C_KEY:C_KEY + CACHE],
                               self.lenm[:, b:b + 1], MASKED, ALU.is_ge, ALU.mult).then_inc(self.masked, 1)

    def tables(self, dve, link):
        dve.wait_ge(self.trig, 2)
        link(dve.tensor_scalar(self.turns[:, :, :], self.sin[:, :, :], -1.0, None, ALU.mult))
        for j in range(4):
            if j >= 2:
                dve.wait_ge(self.tab_stored[j % 2], 16 * (j // 2))
            for half in range(2):
                at = (j // 2) * P + half * 64
                w = self.normw[:, at:at + 64].unsqueeze(1).broadcast_to([P, SEQS, 64])
                src = self.cos if j % 2 == 0 else (self.turns if half else self.sin)
                ins = dve.tensor_tensor(self.part[j % 2][:, :, half * 64:half * 64 + 64], src[:, :, :], w, ALU.mult)
            ins.then_inc(self.tabbed, 1)


class Layer:

    def __init__(self, sb, name, routes, placed=None):
        self.name, self.routes = name, routes
        self.route_w = sb(name + "_route_w", [P, CT, routes])
        self.route_hi, self.route_lo = (sb(name + n, [P, CT, routes], F32R) for n in ("_route_hi", "_route_lo"))
        if placed:
            w, b = slice(0, LW), slice(LW, LW + DM)
            self.w_hi, self.w_lo = (part[:, w].rearrange("p (c n) -> p c n", c=CT) for part in placed)
            self.b_hi, self.b_lo = (part[:, b] for part in placed)
            return
        self.w_hi, self.w_lo = sb(name + "_w_hi", [P, CT, DM + P], F32R), sb(name + "_w_lo", [P, CT, DM + P], F32R)
        self.b_hi, self.b_lo = sb(name + "_b_hi", [P, DM], F32R), sb(name + "_b_lo", [P, DM], F32R)


class Work:

    def __init__(self, sb, sem, name):
        self.hid = sb(name + "_hid", [P, 2, HALF])
        self.gate = sb(name + "_gate", [P, SEQS, EXP])
        self.gate_wide = sb(name + "_gate_wide", [P, SEQS, P])
        self.hg = sb(name + "_hg", [P, 2, HALF])
        self.hg_hi, self.hg_lo = sb(name + "_hg_hi", [P, 2, HALF], F32R), sb(name + "_hg_lo", [P, 2, HALF], F32R)
        self.split_w = sem(name + "_split_w")
        self.inputs_ready = sem(name + "_inputs_ready")
        self.route_hi_done, self.route_lo_done = sem(name + "_route_hi_done"), sem(name + "_route_lo_done")
        self.logits_wide = sem(name + "_logits_wide")
        self.logits_copied = sem(name + "_logits_copied")
        self.logits_done = sem(name + "_logits_done")
        self.hid_done = sem(name + "_hid_done")
        self.hid_copied = sem(name + "_hid_copied")
        self.gates_wide = sem(name + "_gates_wide")
        self.gates_turned = sem(name + "_gates_turned")
        self.gated = sem(name + "_gated")
        self.gated_hi = sem(name + "_gated_hi")
        self.gated_lo = sem(name + "_gated_lo")
        self.out_done = sem(name + "_out_done")
        self.out_hi = sem(name + "_out_hi")
        self.bank_free = sem(name + "_bank_free")


def mm3(pe, out, lhs, rhs, start, stop):
    pe.matmul(out, lhs[0], rhs[0], start=start, stop=False)
    pe.matmul(out, lhs[0], rhs[1], start=False, stop=False)
    return pe.matmul(out, lhs[1], rhs[0], start=False, stop=stop)


def halves(h):
    return slice(h * HALF, (h + 1) * HALF)


class LayerTensor:

    def __init__(self, pe, k, ps, ident, x_hi, x_lo, L, wk):
        self.pe, self.k, self.ps, self.ident, self.L, self.wk = pe, k, ps, ident, L, wk
        self.x_hi, self.x_lo = x_hi, x_lo

    def hidden(self, h):
        L, a = self.L, slice(DM, DM + P)
        for c in range(CT):
            ins = mm3(self.pe, self.ps[:, 4 + h, :], (L.w_hi[:, c, a], L.w_lo[:, c, a]),
                      (self.x_hi[h][:, c, :], self.x_lo[h][:, c, :]), c == 0, c == CT - 1)
        ins.then_inc(self.wk.hid_done, 1)

    def logits(self, h):
        L = self.L
        self.pe.wait_ge(self.wk.route_lo_done, self.k + 1)
        for c in range(CT):
            ins = mm3(self.pe, self.ps[0:L.routes, 7 - h, :], (L.route_hi[:, c, :], L.route_lo[:, c, :]),
                      (self.x_hi[h][:, c, :], self.x_lo[h][:, c, :]), c == 0, c == CT - 1)
        ins.then_inc(self.wk.logits_wide, 1)

    def turn_logits(self):
        n = self.L.routes
        self.pe.wait_ge(self.wk.logits_copied, 2 * self.k + 2)
        for b in range(SEQS):
            ins = self.pe.transpose(self.ps[:, 7, b * n:b * n + n], self.wk.hg[0:n, b // 4, (b % 4) * P:(b % 4) * P + P], self.ident[0:n, 0:n])
        ins.then_inc(self.wk.logits_done, 1)

    def base(self, h, o, bank):
        L, w = self.L, slice(o * P, o * P + P)
        for c in range(CT):
            mm3(self.pe, self.ps[:, bank, :], (L.w_hi[:, c, w], L.w_lo[:, c, w]),
                (self.x_hi[h][:, c, :], self.x_lo[h][:, c, :]), c == 0, False)

    def turn_gates(self, h):
        pe, wk, k = self.pe, self.wk, self.k
        pe.wait_ge(wk.gates_wide, k + 1)
        if h or k:
            pe.wait_ge(wk.gated, 2 * k + h)
        for b in range(4):
            ins = pe.transpose(self.ps[:, 6, b * P:b * P + P], wk.gate_wide[:, 4 * h + b, :], self.ident)
        ins.then_inc(wk.gates_turned, 1)

    def experts(self, h, o, bank):
        wk, L, w = self.wk, self.L, slice(o * P, o * P + P)
        if o == 0:
            self.pe.wait_ge(wk.gated_lo, 2 * self.k + h + 1)
        mm3(self.pe, self.ps[:, bank, :], (L.b_hi[:, w], L.b_lo[:, w]), (wk.hg_hi[:, h, :], wk.hg_lo[:, h, :]),
            False, True).then_inc(wk.out_done, 1)


def layer_tensor(pe, k, ps, ident, x_hi, x_lo, L, wk, ident_in=None):
    part = LayerTensor(pe, k, ps, ident, x_hi, x_lo, L, wk)
    pe.wait_ge(wk.inputs_ready, 2 * k + 1)
    pe.wait_ge(wk.split_w, 2 * k + 2)
    if k:
        pe.wait_ge(wk.hid_copied, 2 * k)
    part.hidden(0)
    pe.wait_ge(wk.inputs_ready, 2 * k + 2)
    part.logits(0)
    part.logits(1)
    part.hidden(1)
    if ident_in:
        pe.wait_ge(ident_in, 64)
    part.turn_logits()

    def base(h, o):
        if 8 * k + 4 * h + o >= CT:
            pe.wait_ge(wk.bank_free, 8 * k + 4 * h + o - 3)
        part.base(h, o, o)

    for o in range(CT):
        if o == CT - 1:
            part.turn_gates(0)
        base(0, o)
    for o in range(CT):
        part.experts(0, o, o)
    for o in range(CT):
        base(1, o)
        if o == 0:
            part.turn_gates(1)
        else:
            part.experts(1, o - 1, o - 1)
    part.experts(1, CT - 1, CT - 1)


def layer_gated_vector(dve, k, h, ps, wk):
    dve.wait_ge(wk.hid_copied, 2 * k + h + 1)
    dve.wait_ge(wk.gates_turned, 2 * k + h + 1)
    if k:
        dve.wait_ge(wk.out_done, 8 * k)
    dve.tensor_tensor(wk.hg[:, h, :], wk.hid[:, h, :], ps[:, 6, :], ALU.mult).then_inc(wk.gated, 1)
    dve.wait_ge(wk.gated_hi, 2 * k + h + 1)
    dve.tensor_tensor(wk.hg_lo[:, h, :], wk.hg[:, h, :], wk.hg_hi[:, h, :].bitcast(F32), ALU.subtract).then_inc(wk.gated_lo, 1)


def layer_hidden_scalar(act, k, ps, wk):
    for h in range(2):
        act.wait_ge(wk.hid_done, 2 * k + h + 1)
        if k:
            act.wait_ge(wk.gated, 2 * k)
        act.activation(wk.hid[:, h, :], ps[:, 4 + h, :], ACT.Copy).then_inc(wk.hid_copied, 1)


def layer_gated_scalar(act, k, h, wk):
    act.wait_ge(wk.gated, 2 * k + h + 1)
    act.activation(wk.hg_hi[:, h, :], wk.hg[:, h, :], ACT.Copy).then_inc(wk.gated_hi, 1)


def layer_logits_scalar(act, k, ps, L, wk):
    if k:
        act.wait_ge(wk.gated_lo, 2 * k)
    for h in range(2):
        act.wait_ge(wk.logits_wide, 2 * k + h + 1)
        act.activation(wk.hg[0:L.routes, h, :], ps[0:L.routes, 7 - h, :], ACT.Copy).then_inc(wk.logits_copied, 1)


def bcast(ap, shape, at):
    return ap.unsqueeze(at).broadcast_to(shape)


def top2_gates(dve, link, lg, iota, buf, exp_wait, exp_in, gate_scale):
    for b in range(SEQS):
        ins = dve.max(buf["best"][:, b, :], lg[:, b, :])
    link(ins)
    for b in range(SEQS):
        ins = dve.max_index(buf["where"][:, b, :], buf["best"][:, b, :], lg[:, b, :])
    link(ins)
    best, where_f, sm = buf["best"], buf["where_f"], buf["small"]
    link(dve.tensor_copy(where_f[:, :, :], buf["where"][:, :, :]))
    dve.tensor_tensor(sm[:, 0, :], best[:, :, 1], best[:, :, 0], ALU.subtract).then_inc(exp_in, 1)
    shape = [P, SEQS, EXP]
    for c in range(2):
        link(dve.tensor_tensor(buf["hot"][:, :, c, :], bcast(iota, shape, 1),
                               where_f[:, :, c:c + 1].broadcast_to(shape), ALU.is_equal))
    exp_wait()
    link(dve.tensor_scalar(sm[:, 2, :], sm[:, 1, :], 1.0, None, ALU.add))
    link(dve.reciprocal(sm[:, 3, :], sm[:, 2, :]))
    link(dve.tensor_scalar(sm[:, 4, :], sm[:, 3, :], gate_scale, None, ALU.mult))
    link(dve.tensor_tensor(sm[:, 5, :], sm[:, 4, :], sm[:, 1, :], ALU.mult))
    for c in range(2):
        link(dve.tensor_tensor(buf["hot_g"][:, :, c, :], buf["hot"][:, :, c, :], bcast(sm[:, 4 + c, :], shape, 2), ALU.mult))


def top2_buffers(sb, name):
    return dict(best=sb(name + "_best", [P, SEQS, 8]), where=sb(name + "_where", [P, SEQS, 8], U32),
                where_f=sb(name + "_where_f", [P, SEQS, 8]), hot=sb(name + "_hot", [P, SEQS, 2, EXP]),
                hot_g=sb(name + "_hot_g", [P, SEQS, 2, EXP]), small=sb(name + "_small", [P, 6, SEQS]))


def widen_gates(dve, wk):
    dve.tensor_copy(wk.gate_wide[:, :, :].rearrange("p b (e r) -> p b e r", r=RANK),
                    wk.gate[:, :, :].unsqueeze(3).broadcast_to([P, SEQS, EXP, RANK])).then_inc(wk.gates_wide, 1)


def first_block(nc, t, ps, cst, ones, prob, ahead, x1_split, rope_tab, mask_tab):
    ident, iota = cst[:, C_ID:C_ID + P], cst[:, C_IOTA:C_IOTA + EXP]
    with ExitStack() as ctx:
        sb = lambda n, s, d=F32: ctx.enter_context(nc.sbuf_tensor(n, s, d))
        sem = lambda n: ctx.enter_context(nc.semaphore(n))
        x = sb("x", [P, CT, TOK])
        first, second, other = ([sb(f"split{i}_{n}", [P, CT, HALF], F32R) for n in ("hi", "lo")] for i in range(3))
        x_hi, x_lo = zip(first, second)
        y_hi, y_lo = zip(first, other)
        raw_w = sb("raw_w", [P, CT, DM + P])
        raw_b = sb("raw_b", [P, DM])
        tab = Tables(sb, sem, cst, rope_tab, mask_tab)
        L = [Layer(sb, "cond0", EXP), Layer(sb, "ffn0", NR1)]
        wk = Work(sb, sem, "b0")
        lang, lang_f = sb("lang", [P, SEQS], I32), sb("lang_f", [P, SEQS])
        base_b, route_b = sb("base_b", [P, CT]), sb("route_b", [P, NR1])
        emap, emap_f = sb("emap", [P, NR1], I32), sb("emap_f", [P, NR1])
        onehot = sb("onehot", [P, EXP, NR1])
        lg0, bias0 = sb("lg0", [P, SEQS, EXP]), sb("bias0", [P, SEQS, EXP])
        t2 = top2_buffers(sb, "t2")
        lg1, pr1, rest1 = (sb(n, [P, SEQS, NR1]) for n in ("lg1", "pr1", "rest1"))
        st1 = sb("st1", [P, 3, SEQS])
        best1 = sb("best1", [P, SEQS, 8])
        spread = sb("spread", [P, SEQS, EXP, NR1])
        s_x, s_w, s_small = [sem("x_in0"), sem("x_in1")], [sem("w_in0"), sem("w_in1")], sem("small_in")
        x_hi_done, w_hi_done, chain, exp_in, exp_out, stored, group_in, x1_lo_done, route_in, pages_in, page_rows, half_stored, ahead_in = (
            sem(n) for n in ("x_hi_done", "w_hi_done", "chain", "exp_in", "exp_out", "stored", "group_in", "x1_lo_done", "route_in", "pages_in", "page_rows", "half_stored", "ahead_in"))
        block = ctx.enter_context(nc.Block())

        @block.sync
        def _(sp):
            def load_w(k):
                sp.dma_start(raw_w[:, :, :], t[L[k].name + "_w"]).then_inc(s_w[k], 16)
                sp.dma_start(raw_b[:, :], t[L[k].name + "_lb"]).then_inc(s_w[k], 16)

            load_w(0)
            for k in range(2):
                sp.dma_start(L[k].route_w[:, :, :], t[L[k].name + "_route"]).then_inc(route_in, 16)
            for h in range(2):
                sp.dma_start(x[:, :, halves(h)], t["x"][:, :, halves(h)]).then_inc(s_x[h], 16)
            for dst, src in ((lang[:, :], t["lang"]), (base_b[:, :], t["ffn0_b"]), (route_b[:, :], t["ffn0_route_b"]),
                             (emap[:, :], t["emap"])):
                sp.dma_start(dst, src).then_inc(s_small, 16)
            tab.load(sp, t)
            for dst, src in ((ahead.page_in, "pages"), (ahead.row_of, "row_of"), (ahead.head_no, "head_no")):
                sp.dma_start(dst[:, :], t[src]).then_inc(pages_in, 16)
            sp.wait_ge(wk.split_w, 2)
            load_w(1)
            sp.dma_start(prob[:, :, :, :].rearrange("p a h k -> p (a h k)").rearrange("p (a n) -> p a n", a=SEQS),
                         t["att_w"][0:SEQS, :, :].rearrange("a p n -> p a n")).then_inc(group_in, 16)
            tab.store_masks(sp)
            tab.store_tables(sp)
            for h in range(2):
                for o in range(CT):
                    sp.wait_ge(x1_lo_done, 4 * h + o + 1)
                    for j, part in enumerate((x_hi, x_lo)):
                        at = j * DM + o * P
                        sp.dma_start(x1_split[4 * h:4 * h + 4, :, at:at + P].rearrange("b p n -> p b n"),
                                     part[h][:, o, :].bitcast(F32).rearrange("p (b n) -> p b n", b=4)).then_inc(half_stored if h == 0 else stored, 16)
                if h == 0:
                    sp.wait_ge(half_stored, 16 * 2 * CT)
                    sp.dma_start(ahead.xs[0][:, :].bitcast(F32), x1_split[0]).then_inc(ahead_in, 16)
            sp.wait_ge(stored, 16 * 2 * CT)
            sp.wait_ge(ahead_in, 16)
            for p in range(2):
                sp.wait_ge(tab.mask_stored[p], 16 * 4)
                sp.wait_ge(tab.tab_stored[p], 16 * 2)
            sp.wait_ge(group_in, 16)

        @block.gpsimd
        def _(pool):
            tab.lengths(pool)
            tab.masks(pool)
            pool.wait_ge(pages_in, 48)
            pool.tensor_scalar(ahead.page_row[:, :], ahead.page_in[:, :], PSIZE * KVH, None, ALU.mult).then_inc(page_rows, 1)
            pool.wait_ge(page_rows, 1)
            pool.tensor_tensor(ahead.page_row[:, :], ahead.page_row[:, :], ahead.row_of[:, :], ALU.add)
            pool.wait_ge(w_hi_done, CT + 2)
            pool.tensor_tensor(L[1].w_lo[:, :, :], raw_w[:, :, :], L[1].w_hi[:, :, :].bitcast(F32), ALU.subtract).then_inc(wk.split_w, 1)
            pool.wait_ge(w_hi_done, CT + 3)
            pool.tensor_tensor(L[1].b_lo[:, :], raw_b[:, :], L[1].b_hi[:, :].bitcast(F32), ALU.subtract).then_inc(wk.split_w, 1)

        @block.scalar
        def _(act):
            act.wait_ge(s_w[0], 32)
            for c in range(CT):
                act.activation(L[0].w_hi[:, c, :], raw_w[:, c, :], ACT.Copy).then_inc(w_hi_done, 1)
            for h in range(2):
                act.wait_ge(s_x[h], 16)
                for c in range(CT):
                    act.activation(x_hi[h][:, c, :], x[:, c, halves(h)], ACT.Copy).then_inc(x_hi_done, 1)
                if h == 0:
                    act.activation(L[0].b_hi[:, :], raw_b[:, :], ACT.Copy).then_inc(w_hi_done, 1)
                    act.wait_ge(route_in, 32)
                    for k in range(2):
                        act.activation(L[k].route_hi[:, :, :], L[k].route_w[:, :, :], ACT.Copy).then_inc(wk.route_hi_done, 1)
            tab.sines(act)
            for k in range(2):
                layer_logits_scalar(act, k, ps, L[k], wk)
                act.wait_ge(exp_in, k + 1)
                if k == 0:
                    act.activation(t2["small"][:, 1, :], t2["small"][:, 0, :], ACT.Exp).then_inc(exp_out, 1)
                else:
                    act.activation(pr1[:, :, :], lg1[:, :, :], ACT.Exp).then_inc(exp_out, 1)
                layer_hidden_scalar(act, k, ps, wk)
                if k == 0:
                    act.wait_ge(s_w[1], 32)
                    act.activation(L[1].w_hi[:, :, :], raw_w[:, :, :], ACT.Copy).then_inc(w_hi_done, 1)
                    act.activation(L[1].b_hi[:, :], raw_b[:, :], ACT.Copy).then_inc(w_hi_done, 1)
                for h in range(2):
                    layer_gated_scalar(act, k, h, wk)
                    for o in range(CT):
                        if k == 0:
                            act.wait_ge(wk.out_done, 4 * h + o + 1)
                            act.activation(y_hi[h][:, o, :], ps[:, o, :], ACT.Copy).then_inc(wk.out_hi, 1)
                        else:
                            act.wait_ge(wk.bank_free, 8 + 4 * h + o + 1)
                            act.activation(x_hi[h][:, o, :], x[:, o, halves(h)], ACT.Copy).then_inc(wk.out_hi, 1)

        @block.vector
        def _(dve):
            n = [0]

            def link(ins):
                n[0] += 1
                ins.then_inc(chain, 1)
                dve.wait_ge(chain, n[0])

            link(dve.memset(ones[:, :], 1.0))
            for c in range(CT):
                dve.wait_ge(w_hi_done, c + 1)
                ins = dve.tensor_tensor(L[0].w_lo[:, c, :], raw_w[:, c, :], L[0].w_hi[:, c, :].bitcast(F32), ALU.subtract)
            ins.then_inc(wk.split_w, 1)
            for h in range(2):
                for c in range(CT):
                    dve.wait_ge(x_hi_done, CT * h + c + 1)
                    ins = dve.tensor_tensor(x_lo[h][:, c, :], x[:, c, halves(h)], x_hi[h][:, c, :].bitcast(F32), ALU.subtract)
                ins.then_inc(wk.inputs_ready, 1)
                if h == 0:
                    dve.wait_ge(w_hi_done, CT + 1)
                    dve.tensor_tensor(L[0].b_lo[:, :], raw_b[:, :], L[0].b_hi[:, :].bitcast(F32), ALU.subtract).then_inc(wk.split_w, 1)
                    for k in range(2):
                        dve.wait_ge(wk.route_hi_done, k + 1)
                        dve.tensor_tensor(L[k].route_lo[:, :, :], L[k].route_w[:, :, :], L[k].route_hi[:, :, :].bitcast(F32),
                                          ALU.subtract).then_inc(wk.route_lo_done, 1)
            tab.angles(dve, link)
            dve.wait_ge(s_small, 64)
            link(dve.tensor_copy(lang_f[:, :], lang[:, :]))
            shape = [P, SEQS, EXP]
            link(dve.tensor_tensor(bias0[:, :, :], bcast(iota, shape, 1), bcast(lang_f[:, :], shape, 2), ALU.is_equal))
            link(dve.tensor_copy(emap_f[:, :], emap[:, :]))
            hot_shape = [P, EXP, NR1]
            link(dve.tensor_tensor(onehot[:, :, :], bcast(iota, hot_shape, 2), bcast(emap_f[:, :], hot_shape, 1), ALU.is_equal))
            dve.wait_ge(wk.logits_done, 1)
            link(dve.scalar_tensor_tensor(out=lg0[:, :, :], in0=bias0[:, :, :], scalar=5.0,
                                          in1=ps[:, 7, 0:SEQS * EXP].rearrange("p (b e) -> p b e", b=SEQS),
                                          op0=ALU.mult, op1=ALU.add))
            top2_gates(dve, link, lg0, iota, t2, lambda: dve.wait_ge(exp_out, 1), exp_in, 2.0)
            link(dve.tensor_tensor(wk.gate[:, :, :], t2["hot_g"][:, :, 0, :], t2["hot_g"][:, :, 1, :], ALU.add))
            widen_gates(dve, wk)
            for h in range(2):
                layer_gated_vector(dve, 0, h, ps, wk)
                for o in range(CT):
                    dve.wait_ge(wk.out_hi, 4 * h + o + 1)
                    dve.tensor_tensor(y_lo[h][:, o, :], ps[:, o, :], y_hi[h][:, o, :].bitcast(F32), ALU.subtract).then_inc(wk.bank_free, 1)
                dve.wait_ge(wk.bank_free, 4 * h + CT)
                dve.sem_inc(wk.inputs_ready, 1)
            tab.tables(dve, link)
            dve.wait_ge(wk.logits_done, 2)
            lshape = [P, SEQS, NR1]
            link(dve.tensor_tensor(lg1[:, :, :], ps[:, 7, 0:SEQS * NR1].rearrange("p (b e) -> p b e", b=SEQS),
                                   bcast(route_b[:, :], lshape, 1), ALU.add))
            link(dve.tensor_reduce(st1[:, 0, :], lg1[:, :, :], AX.X, ALU.max))
            dve.tensor_tensor(lg1[:, :, :], lg1[:, :, :], bcast(st1[:, 0, :], lshape, 2), ALU.subtract).then_inc(exp_in, 1)
            dve.wait_ge(exp_out, 2)
            link(dve.tensor_reduce(st1[:, 1, :], pr1[:, :, :], AX.X, ALU.add))
            link(dve.reciprocal(st1[:, 2, :], st1[:, 1, :]))
            link(dve.tensor_tensor(pr1[:, :, :], pr1[:, :, :], bcast(st1[:, 2, :], lshape, 2), ALU.mult))
            for b in range(SEQS):
                ins = dve.max(best1[:, b, :], pr1[:, b, :])
            link(ins)
            for b in range(SEQS):
                ins = dve.match_replace(rest1[:, b, :], best1[:, b, :], pr1[:, b, :], 0.0)
            link(ins)
            link(dve.tensor_tensor(pr1[:, :, :], pr1[:, :, :], rest1[:, :, :], ALU.subtract))
            wide = [P, SEQS, EXP, NR1]
            link(dve.tensor_tensor(spread[:, :, :, :], pr1[:, :, :].unsqueeze(2).broadcast_to(wide),
                                   onehot[:, :, :].unsqueeze(1).broadcast_to(wide), ALU.mult))
            link(dve.tensor_reduce(wk.gate[:, :, :], spread[:, :, :, :], AX.X, ALU.add))
            link(dve.tensor_scalar(wk.gate[:, :, :], wk.gate[:, :, :], 2.0, None, ALU.mult))
            dve.wait_ge(wk.gates_turned, 2)
            widen_gates(dve, wk)
            for h in range(2):
                layer_gated_vector(dve, 1, h, ps, wk)
                for o in range(CT + 1):
                    if o < CT:
                        dve.wait_ge(wk.out_done, 8 + 4 * h + o + 1)
                        dve.scalar_tensor_tensor(out=x[:, o, halves(h)], in0=ps[:, o, :], scalar=base_b[:, o:o + 1],
                                                 in1=x[:, o, halves(h)], op0=ALU.add, op1=ALU.add).then_inc(wk.bank_free, 1)
                    if o:
                        dve.wait_ge(wk.out_hi, 8 + 4 * h + o)
                        dve.tensor_tensor(x_lo[h][:, o - 1, :], x[:, o - 1, halves(h)], x_hi[h][:, o - 1, :].bitcast(F32),
                                          ALU.subtract).then_inc(x1_lo_done, 1)

        @block.tensor
        def _(pe):
            layer_tensor(pe, 0, ps, ident, x_hi, x_lo, L[0], wk, tab.loaded)
            layer_tensor(pe, 1, ps, ident, y_hi, y_lo, L[1], wk)


BANK_S, BANK_T, BANK_O, BANK_P = 0, 4, 6, 7
BANK_KC, BANK_KN = 0, 1
SPARE = slice(KEYS // 2, KEYS // 2 + P)


def attention(nc, t, ps, cst, prob, ahead, w_hi, w_lo, x1_split, rope_tab, mask_tab, att):
    ident = cst[:, C_ID:C_ID + P]
    with ExitStack() as ctx:
        sb = lambda n, s, d=F32: ctx.enter_context(nc.sbuf_tensor(n, s, d))
        sem = lambda n: ctx.enter_context(nc.semaphore(n))
        pair = lambda n, s, d=F32: [sb(f"{n}{p}", s, d) for p in range(2)]
        w_raw = pair("w_raw", [P, CHUNK])
        xs, page_row, head_no = ahead.xs, ahead.page_row, ahead.head_no
        rope = pair("rope", [P, 4 * P])
        mask = pair("mask", [P, KEYS])
        kv = pair("kv", [P, KT + 1, 2 * P])
        rows = pair("rows", [P, KT], I32)
        q_raw, q_a, q_b = sb("q_raw", [P, QPK * P]), sb("q_a", [P, QPK * P]), sb("q_b", [P, QPK * P])
        k_a, k_b = sb("k_a", [P, P]), sb("k_b", [P, P])
        sq = sb("sq", [P, (QPK + 1) * P])
        ssq_q, ssq_k = sb("ssq_q", [P, QPK]), sb("ssq_k", [P, 1])
        rms_q, rms_k = sb("rms_q", [P, QPK]), sb("rms_k", [P, 1])
        minus_half = sb("minus_half", [P, QPK])
        r_q, neg_r_q = pair("r_q", [P, QPK]), pair("neg_r_q", [P, QPK])
        qt_hi, qt_lo = sb("qt_hi", [P, QPK * P], F32R), sb("qt_lo", [P, QPK * P], F32R)
        kt_hi, kt_lo = sb("kt_hi", [P, KEYS], F32R), sb("kt_lo", [P, KEYS], F32R)
        v_hi, v_lo = pair("v_hi", [P, KT + 1, P], F32R), pair("v_lo", [P, KT + 1, P], F32R)
        top, neg_top = sb("top", [P, QPK]), sb("neg_top", [P, QPK])
        den, inv = sb("den", [P, QPK]), sb("inv", [P, QPK])
        pt_hi, pt_lo = pair("pt_hi", [P, DM], F32R), pair("pt_lo", [P, DM], F32R)
        ot_hi, ot_lo = sb("ot_hi", [P, DM], F32R), sb("ot_lo", [P, DM], F32R)

        w_in, x_in, rope_in, mask_in, kv_in = ([sem(f"{n}{p}") for p in range(2)] for n in ("w_in", "x_in", "rope_in", "mask_in", "kv_in"))
        q_done, kv_done, s_done, turned, kc_turned, kn_turned, pv_done, o_done = (
            sem(n) for n in ("q_done", "kv_done", "s_done", "turned", "kc_turned", "kn_turned", "pv_done", "o_done"))
        q_copied, kv_copied, q_squared, k_squared, expd, normed_1, hi_done, kc_hi_done, kn_hi_done, v_hi_done, w_hi_done, o_hi_done = (
            sem(n) for n in ("q_copied", "kv_copied", "q_squared", "k_squared", "expd", "normed_1", "hi_done", "kc_hi_done", "kn_hi_done", "v_hi_done", "w_hi_done", "o_hi_done"))
        lo_done, kc_lo_done, kn_lo_done, maxed, biased, inverted, normed, q_scaled, q_cos, k_cos, k_roped, o_lo_done, summed, cleared = (
            sem(n) for n in ("lo_done", "kc_lo_done", "kn_lo_done", "maxed", "biased", "inverted", "normed", "q_scaled", "q_cos", "k_cos",
                             "k_roped", "o_lo_done", "summed", "cleared"))
        q_sin, q_roped, k_sin, q_mean, q_rms, k_mean, k_rms, v_lo_done, w_lo_done, rows_done, setup = (
            sem(n) for n in ("q_sin", "q_roped", "k_sin", "q_mean", "q_rms", "k_mean", "k_rms", "v_lo_done", "w_lo_done", "rows_done", "setup"))
        first_lo_done = sem("first_lo_done")
        dve_held, pool_held = sem("dve_held"), sem("pool_held")
        first_group = prob[:, :, :, :].rearrange("p a h k -> p (a h k)").rearrange("p (w n) -> p w n", w=SEQS)
        block = ctx.enter_context(nc.Block())

        def held(eng, sem):
            eng.sem_inc(sem, 1)

        def run(eng, body):
            body(Step(-1), False, False, True)
            body(Step(0), False, True, True)
            with eng.Fori(0, (STEPS - 4) // 2) as trip:
                body(Step(1, trip), True, True, True)
                body(Step(2, trip), True, True, True)
            body(Step(STEPS - 3), True, True, True)
            body(Step(STEPS - 2), True, True, True)
            body(Step(STEPS - 1), True, True, False)
            body(Step(STEPS), True, False, False)

        @block.sync
        def _(sp):
            def load_w(w):
                sp.dma_start(w_raw[w.parity][:, :], t["att_w"][ds(w.times(1), 1), :, :].rearrange("a p n -> (a p) n")).then_inc(w_in[w.parity], 16)

            def load_x(m):
                b = m.times(1) % SEQS
                sp.dma_start(xs[m.parity][:, :].bitcast(F32), x1_split[ds(b, 1), :, :].rearrange("a p n -> (a p) n")).then_inc(x_in[m.parity], 16)
                load_rope(m)

            def load_rope(m):
                b = m.times(1) % SEQS
                sp.dma_start(rope[m.parity][:, :], rope_tab[ds(b, 1), :, :].rearrange("a p n -> (a p) n")).then_inc(rope_in[m.parity], 16)

            def load_mask(m):
                sp.dma_start(mask[m.parity][:, :], mask_tab[ds(m.times(1) % SEQS, 1), :, :].rearrange("a p n -> (a p) n")).then_inc(mask_in[m.parity], 16)

            load_rope(Step(0))

            def body(i, prev, cur, nxt):
                w, m = i.plus(9), i.plus(2)
                if not nxt:
                    return
                if not (isinstance(i.trip, int) and i.off == STEPS - 2):
                    sp.wait_ge(w_lo_done, w.times(1, -1))
                    load_w(w)
                if not m.first and not (isinstance(m.trip, int) and m.off in (1,)):
                    sp.wait_ge(kv_done, m.times(1, -1))
                    sp.wait_ge(k_roped, m.times(1, -1))
                if not (isinstance(i.trip, int) and i.off == STEPS - 2):
                    load_x(m)
                k = i.plus(1)
                if not isinstance(k.trip, int) or k.off >= 2:
                    sp.wait_ge(maxed, k.times(4, -4))
                load_mask(k)

            run(sp, body)

        @block.gpsimd
        def _(pool):
            pool.memset(minus_half[:, :], -0.5).then_inc(setup, 1)
            pool.wait_ge(setup, 1)

            def gather(m, tiles):
                p = m.parity
                if tiles[0] == 0:
                    pool.tensor_tensor(rows[p][:, :], page_row[:, ds((m.times(1) % SEQS) * KT, KT)],
                                       head_no[:, ds((m.times(1) // SEQS) * KT, KT)], ALU.add).then_inc(rows_done, 1)
                    pool.wait_ge(rows_done, m.times(1, 1))
                    held(pool, pool_held)
                for j in tiles:
                    pool.indirect_dma_start(kv[p][:, j, :], None, t["kv"],
                                            bass.IndirectOffsetOnAxis(ap=rows[p][:, j:j + 1], axis=0)).then_inc(kv_in[p], 16)

            def split_w(w):
                p = w.parity
                at = ((w.times(1) // SEQS) % 2) * GW + (w.times(1) % SEQS) * CHUNK
                pool.wait_ge(w_hi_done, w.times(1, 1))
                pool.tensor_tensor(w_lo[:, ds(at, CHUNK)], w_raw[p][:, :], w_hi[:, ds(at, CHUNK)].bitcast(F32), ALU.subtract).then_inc(w_lo_done, 1)

            gather(Step(0), range(KT))
            for n_split in (5, SEQS):
                pool.wait_ge(first_lo_done, n_split)
                pool.sem_inc(w_lo_done, 5 if n_split == 5 else SEQS - 5)
                if n_split == 5:
                    pool.memset(att[:, :, :], 0.0).then_inc(cleared, 1)

            def body(i, prev, cur, nxt):
                n, m = i.plus(1), i.plus(2)
                more = nxt and not (isinstance(i.trip, int) and i.off >= STEPS - 2)
                if cur and nxt:
                    split_w(i.plus(SEQS))
                if nxt:
                    pool.wait_ge(q_copied, n.times(1, 1))
                    if not n.first:
                        pool.wait_ge(q_roped, n.times(1))
                    sine = rope[n.parity][:, P:2 * P].unsqueeze(1).broadcast_to([P, QPK, P])
                    pool.wait_ge(rope_in[n.parity], n.half(1) * 16)
                    pool.tensor_tensor(q_b[:, :].rearrange("p (h d) -> p h d", h=QPK), q_raw[:, :].rearrange("p (h d) -> p h d", h=QPK),
                                       sine, ALU.mult).then_inc(q_sin, 1)
                    pool.wait_ge(q_sin, n.times(1, 1))
                    pool.wait_ge(q_cos, n.times(1, 1))
                    by_half = [ap.rearrange("p (h s d) -> p h s d", h=QPK, s=2) for ap in (q_a[:, :], q_b[:, :])]
                    for s in range(2):
                        ins = pool.tensor_tensor(by_half[0][:, :, s, :], by_half[0][:, :, s, :], by_half[1][:, :, 1 - s, :], ALU.add)
                    ins.then_inc(q_roped, 1)
                if cur:
                    pool.wait_ge(v_hi_done, i.times(1, 1))
                    if i.off >= 2 or not isinstance(i.trip, int):
                        pool.wait_ge(pv_done, i.times(5, -5))
                    pool.tensor_tensor(v_lo[i.parity][:, :, :], kv[i.parity][:, :, P:2 * P], v_hi[i.parity][:, :, :].bitcast(F32),
                                       ALU.subtract).then_inc(v_lo_done, 1)
                if more:
                    if cur:
                        pool.wait_ge(v_lo_done, i.times(1, 1))
                        pool.wait_ge(kc_turned, i.times(1, 1))
                        pool.wait_ge(k_roped, i.times(1, 1))
                        gather(m, range(KT - 2))
                if nxt:
                    pool.wait_ge(k_squared, n.times(1, 1))
                    if not n.first:
                        pool.wait_ge(k_roped, n.times(1))
                    held(pool, pool_held)
                    pool.tensor_scalar(rms_k[:, :], ssq_k[:, :], 1.0 / P, 1e-6, ALU.mult, ALU.add).then_inc(k_mean, 1)
                    pool.wait_ge(k_mean, n.times(1, 1))
                    pool.tensor_tensor(rms_k[:, :], rms_k[:, :], minus_half[:, 0:1], ALU.pow).then_inc(k_rms, 1)
                    pool.tensor_tensor(k_b[:, :], kv[n.parity][:, KT, 0:P], rope[n.parity][:, 3 * P:4 * P], ALU.mult).then_inc(k_sin, 1)
                    pool.wait_ge(q_squared, n.times(1, 1))
                    if not n.first:
                        pool.wait_ge(q_scaled, n.times(1))
                    held(pool, pool_held)
                    pool.tensor_scalar(rms_q[:, :], ssq_q[:, :], 1.0 / P, 1e-6, ALU.mult, ALU.add).then_inc(q_mean, 1)
                    pool.wait_ge(q_mean, n.times(1, 1))
                    pool.tensor_tensor(rms_q[:, :], rms_q[:, :], minus_half[:, :], ALU.pow).then_inc(q_rms, 1)
                if more:
                    gather(m, range(KT - 2, KT) if cur else range(KT))

            run(pool, body)

        @block.scalar
        def _(act):
            def split_w(w):
                p = w.parity
                at = ((w.times(1) // SEQS) % 2) * GW + (w.times(1) % SEQS) * CHUNK
                act.wait_ge(w_in[p], w.half(1 - SEQS // 2) * 16)
                act.activation(w_hi[:, ds(at, CHUNK)], w_raw[p][:, :], ACT.Copy).then_inc(w_hi_done, 1)

            for w in range(SEQS):
                act.activation(w_hi[:, w * CHUNK:(w + 1) * CHUNK], first_group[:, w, :], ACT.Copy).then_inc(w_hi_done, 1)

            def hi(i, j, out, width):
                no = turn_no(i, j)
                act.wait_ge(turned, no + 1)
                bank = BANK_T + j % 2
                act.activation(out, ps[:, bank, 0:width], ACT.Copy).then_inc(hi_done, 1)

            def softmax_exp(i, h):
                act.wait_ge(biased, i.times(4, h + 1))
                act.activation(prob[:, i.parity, h, :], prob[:, i.parity, h, :], ACT.Exp, bias=neg_top[:, h:h + 1],
                               scale=r_q[i.parity][:, h:h + 1], accum_out=den[:, h:h + 1]).then_inc(expd, 1)

            def body(i, prev, cur, nxt):
                n = i.plus(1)
                if cur and nxt:
                    act.wait_ge(kv_done, i.times(1))
                    if prev and not (isinstance(i.trip, int) and i.off == 1):
                        act.wait_ge(o_done, i.times(1, -1))
                    split_w(i.plus(SEQS))
                if prev:
                    hi(i, 1, pt_hi[1][:, :], DM)
                if cur:
                    softmax_exp(i, 0)
                if nxt:
                    act.wait_ge(q_done, n.times(1, 1))
                    if not n.first:
                        act.wait_ge(q_sin, n.times(1))
                        act.wait_ge(q_cos, n.times(1))
                        act.wait_ge(q_squared, n.times(1))
                    act.activation(q_raw[:, :], ps[:, BANK_P, :], ACT.Copy).then_inc(q_copied, 1)
                if prev:
                    hi(i, 2, pt_hi[0][:, :], DM)
                if cur:
                    act.wait_ge(kv_in[i.parity], i.half(1) * 16 * KT)
                    act.wait_ge(kv_copied, i.times(1, 1))
                    if i.off >= 2 or not isinstance(i.trip, int):
                        act.wait_ge(pv_done, i.times(5, -5))
                    act.activation(v_hi[i.parity][:, :, :], kv[i.parity][:, :, P:2 * P], ACT.Copy).then_inc(v_hi_done, 1)
                if prev:
                    hi(i, 3, pt_hi[1][:, :], DM)
                if cur:
                    softmax_exp(i, 1)
                if prev:
                    hi(i, 4, pt_hi[0][:, :], DM)
                if cur:
                    softmax_exp(i, 2)
                    act.wait_ge(inverted, i.times(4, 2))
                    act.activation(prob[:, i.parity, 1, :], prob[:, i.parity, 1, :], ACT.Copy, scale=inv[:, 1:2]).then_inc(normed_1, 1)
                    softmax_exp(i, 3)
                if nxt:
                    act.wait_ge(kv_done, n.times(1, 1))
                    if i.off >= 1 or not isinstance(i.trip, int):
                        act.wait_ge(v_lo_done, n.times(1, -1))
                        act.wait_ge(k_rms, n.times(1))
                        act.wait_ge(k_squared, n.times(1))
                    act.activation(kv[n.parity][:, KT, :], ps[:, BANK_P, 0:2 * P], ACT.Copy).then_inc(kv_copied, 1)
                    act.wait_ge(kv_copied, n.times(1, 1))
                    act.activation(sq[:, QPK * P:], kv[n.parity][:, KT, 0:P], ACT.Square, accum_out=ssq_k[:, 0:1]).then_inc(k_squared, 1)
                if prev:
                    act.wait_ge(pv_done, i.times(5, 0))
                    act.activation(ot_hi[:, :], ps[:, BANK_O, :], ACT.Copy).then_inc(o_hi_done, 1)
                if nxt:
                    hi(i, QUERIES, qt_hi[:, :], DM)
                    act.wait_ge(kc_turned, n.times(1, 1))
                    act.activation(kt_hi[:, 0:CACHE], ps[:, BANK_KC, :], ACT.Copy).then_inc(kc_hi_done, 1)
                if cur:
                    hi(n, 0, pt_hi[0][:, :], DM)
                if nxt:
                    act.wait_ge(q_copied, n.times(1, 1))
                    if not n.first:
                        act.wait_ge(q_rms, n.times(1))
                    for h in range(QPK):
                        ins = act.activation(sq[:, h * P:h * P + P], q_raw[:, h * P:h * P + P], ACT.Square, accum_out=ssq_q[:, h:h + 1])
                    ins.then_inc(q_squared, 1)
                    act.wait_ge(kn_turned, n.times(1, 1))
                    act.activation(kt_hi[:, CACHE:KEYS], ps[:, BANK_KN, SPARE], ACT.Copy).then_inc(kn_hi_done, 1)

            run(act, body)

        @block.vector
        def _(dve):
            for w in range(SEQS):
                at = slice(w * CHUNK, (w + 1) * CHUNK)
                dve.wait_ge(w_hi_done, w + 1)
                dve.tensor_tensor(w_lo[:, at], first_group[:, w, :], w_hi[:, at].bitcast(F32), ALU.subtract).then_inc(first_lo_done, 1)
            dve.wait_ge(first_lo_done, SEQS)

            def lo(i, j, out, width, hi_part):
                no = turn_no(i, j)
                dve.wait_ge(hi_done, no + 1)
                bank = BANK_T + j % 2
                dve.tensor_tensor(out, ps[:, bank, 0:width], hi_part.bitcast(F32), ALU.subtract).then_inc(lo_done, 1)

            def masked_max(i, h):
                p = i.parity
                if h == 0:
                    dve.wait_ge(mask_in[p], i.half(1) * 16)
                    dve.wait_ge(q_scaled, i.times(1, 1))
                dve.wait_ge(s_done, i.times(4, h + 1))
                held(dve, dve_held)
                dve.tensor_tensor_reduce(prob[:, p, h, :].rearrange("p (a k) -> p a k", a=2),
                                         ps[:, BANK_S + 2 * (h % 2):BANK_S + 2 * (h % 2) + 2, 0:KEYS // 2],
                                         mask[p][:, :].rearrange("p (a k) -> p a k", a=2), 1.0, -3.0e38, ALU.add, ALU.max,
                                         top[:, h:h + 1]).then_inc(maxed, 1)
                dve.wait_ge(maxed, i.times(4, h + 1))
                if not i.first:
                    dve.wait_ge(expd, i.times(4, h - 3))
                dve.tensor_tensor(neg_top[:, h:h + 1], top[:, h:h + 1], neg_r_q[p][:, h:h + 1], ALU.mult).then_inc(biased, 1)

            def invert(i, h):
                dve.wait_ge(expd, i.times(4, h + 1))
                if not i.first:
                    dve.wait_ge(normed_1, i.times(1))
                dve.reciprocal(inv[:, h:h + 1], den[:, h:h + 1]).then_inc(inverted, 1)

            def normalise(i, h):
                p = i.parity
                invert(i, h)
                dve.wait_ge(inverted, i.times(4, h + 1))
                dve.tensor_scalar(prob[:, p, h, :], prob[:, p, h, :], inv[:, h:h + 1], None, ALU.mult).then_inc(normed, 1)

            def body(i, prev, cur, nxt):
                n = i.plus(1)
                if prev:
                    lo(i, 1, pt_lo[1][:, :], DM, pt_hi[1][:, :])
                if cur:
                    masked_max(i, 0)
                    normalise(i, 0)
                if nxt:
                    dve.wait_ge(q_copied, n.times(1, 1))
                    dve.wait_ge(rope_in[n.parity], n.half(1) * 16)
                    if not n.first:
                        dve.wait_ge(turned, turn_no(i.plus(-1), QUERIES) + 1)
                    cosine = rope[n.parity][:, 0:P].unsqueeze(1).broadcast_to([P, QPK, P])
                    dve.tensor_tensor(q_a[:, :].rearrange("p (h d) -> p h d", h=QPK), q_raw[:, :].rearrange("p (h d) -> p h d", h=QPK),
                                      cosine, ALU.mult).then_inc(q_cos, 1)
                if prev:
                    lo(i, 2, pt_lo[0][:, :], DM, pt_hi[0][:, :])
                if cur:
                    masked_max(i, 1)
                    masked_max(i, 2)
                if prev:
                    lo(i, 3, pt_lo[1][:, :], DM, pt_hi[1][:, :])
                if cur:
                    invert(i, 1)
                if cur:
                    masked_max(i, 3)
                if prev:
                    lo(i, 4, pt_lo[0][:, :], DM, pt_hi[0][:, :])
                if cur:
                    normalise(i, 2)
                    normalise(i, 3)
                if prev:
                    dve.wait_ge(o_hi_done, i.times(1, 0))
                    dve.tensor_tensor(ot_lo[:, :], ps[:, BANK_O, :], ot_hi[:, :].bitcast(F32), ALU.subtract).then_inc(o_lo_done, 1)
                if nxt:
                    dve.wait_ge(k_rms, n.times(1, 1))
                    if not n.first:
                        dve.wait_ge(kn_turned, n.times(1))
                    dve.scalar_tensor_tensor(out=k_a[:, :], in0=kv[n.parity][:, KT, 0:P], scalar=rms_k[:, 0:1],
                                             in1=rope[n.parity][:, 2 * P:3 * P], op0=ALU.mult, op1=ALU.mult).then_inc(k_cos, 1)
                    dve.wait_ge(k_cos, n.times(1, 1))
                    dve.wait_ge(k_sin, n.times(1, 1))
                    dve.scalar_tensor_tensor(out=k_a[:, 0:64], in0=k_b[:, 64:P], scalar=rms_k[:, 0:1], in1=k_a[:, 0:64],
                                             op0=ALU.mult, op1=ALU.add)
                    dve.scalar_tensor_tensor(out=k_a[:, 64:P], in0=k_b[:, 0:64], scalar=rms_k[:, 0:1], in1=k_a[:, 64:P],
                                             op0=ALU.mult, op1=ALU.add).then_inc(k_roped, 1)
                    lo(i, QUERIES, qt_lo[:, :], DM, qt_hi[:, :])
                    dve.wait_ge(kc_hi_done, n.times(1, 1))
                    dve.tensor_tensor(kt_lo[:, 0:CACHE], ps[:, BANK_KC, :], kt_hi[:, 0:CACHE].bitcast(F32), ALU.subtract).then_inc(kc_lo_done, 1)
                if cur:
                    lo(n, 0, pt_lo[0][:, :], DM, pt_hi[0][:, :])
                if nxt:
                    dve.wait_ge(kn_hi_done, n.times(1, 1))
                    dve.tensor_tensor(kt_lo[:, CACHE:KEYS], ps[:, BANK_KN, SPARE], kt_hi[:, CACHE:KEYS].bitcast(F32),
                                      ALU.subtract).then_inc(kn_lo_done, 1)
                if prev:
                    dve.wait_ge(o_done, i.times(1, 0))
                    dve.wait_ge(cleared, 1)
                    if not (isinstance(i.trip, int) and i.off == 1):
                        dve.wait_ge(summed, i.times(1, -1))
                    here = att[:, ds(i.plus(-1).times(1) % SEQS, 1), :].rearrange("p a n -> p (a n)")
                    dve.tensor_tensor(here, ps[:, BANK_P, :], here, ALU.add).then_inc(summed, 1)
                if nxt:
                    dve.wait_ge(q_rms, n.times(1, 1))
                    if i.off >= 1 or not isinstance(i.trip, int):
                        dve.wait_ge(expd, n.times(4, -4))
                    dve.tensor_scalar(r_q[n.parity][:, :], rms_q[:, :], SCALE, None, ALU.mult)
                    dve.tensor_scalar(neg_r_q[n.parity][:, :], rms_q[:, :], -SCALE, None, ALU.mult).then_inc(q_scaled, 1)

            run(dve, body)

        @block.tensor
        def _(pe):
            def group_base(m):
                base = ((m.times(1) // SEQS) % 2) * GW
                return base if isinstance(base, int) else pe.snap(base)

            def project(n, base, at, width, out, done):
                for c in range(CT):
                    x = xs[n.parity][:, c * P:c * P + P], xs[n.parity][:, DM + c * P:DM + c * P + P]
                    w = [part[:, ds(base + (at + c * width), width)] for part in (w_hi, w_lo)]
                    ins = mm3(pe, out, x, w, c == 0, c == CT - 1)
                ins.then_inc(done, 1)

            def turn(i, j, blocks):
                no = turn_no(i, j)
                if i.first:
                    pe.wait_ge(lo_done, no)
                else:
                    pe.wait_ge(lo_done, no - 1)
                bank = BANK_T + j % 2
                for n, block_ap in enumerate(blocks):
                    ins = pe.transpose(ps[:, bank, n * P:n * P + P], block_ap, ident)
                ins.then_inc(turned, 1)

            def turn_probs(i, j):
                if j == 0:
                    pe.wait_ge(normed, i.times(3, 0))
                    pe.wait_ge(normed_1, i.times(1, 0))
                turn(i, j, [prob[:, 1 - i.parity, h, j * P:j * P + P] for h in range(QPK)])

            def scores(i, h):
                if h == 0:
                    pe.wait_ge(lo_done, turn_no(i.plus(-1), QUERIES) + 1)
                    pe.wait_ge(kc_lo_done, i.times(1, 1))
                if not (isinstance(i.trip, int) and i.off == 0 and h < 2):
                    pe.wait_ge(maxed, i.times(4, h - 1))
                q = slice(h * P, h * P + P)
                for a in range(2):
                    out, k = ps[:, BANK_S + 2 * (h % 2) + a, 0:KEYS // 2], slice(a * KEYS // 2, (a + 1) * KEYS // 2)
                    if h == 0 and a == 1:
                        pe.wait_ge(kn_lo_done, i.times(1, 1))
                    ins = mm3(pe, out, (qt_hi[:, q], qt_lo[:, q]), (kt_hi[:, k], kt_lo[:, k]), True, True)
                ins.then_inc(s_done, 1)

            def values(i, j):
                v = 1 - i.parity
                if j == 0:
                    pe.wait_ge(v_lo_done, i.times(1, 0))
                    if not (isinstance(i.trip, int) and i.off == 1):
                        pe.wait_ge(o_lo_done, i.times(1, -1))
                out, p_hi, p_lo = ps[:, BANK_O, :], pt_hi[j % 2][:, :], pt_lo[j % 2][:, :]
                pe.wait_ge(hi_done, turn_no(i, j) + 1)
                pe.matmul(out, v_hi[v][:, j, :], p_hi, start=(j == 0), stop=False)
                pe.matmul(out, v_lo[v][:, j, :], p_hi, start=False, stop=False)
                pe.wait_ge(lo_done, turn_no(i, j) + 1)
                pe.matmul(out, v_hi[v][:, j, :], p_lo, start=False, stop=(j == KT)).then_inc(pv_done, 1)

            def output_hi(base):
                for h in range(QPK):
                    at = base + (QW + KVW + h * DM)
                    for part in (w_hi, w_lo):
                        pe.matmul(ps[:, BANK_P, :], ot_hi[:, h * P:h * P + P], part[:, ds(at, DM)], start=(h == 0 and part is w_hi), stop=False)

            def output_lo(base):
                for h in range(QPK):
                    ins = pe.matmul(ps[:, BANK_P, :], ot_lo[:, h * P:h * P + P], w_hi[:, ds(base + (QW + KVW + h * DM), DM)],
                                    start=False, stop=(h == QPK - 1))
                return ins

            def body(i, prev, cur, nxt):
                n = i.plus(1)
                if nxt:
                    qkv_base = group_base(n)
                if prev:
                    o_base = group_base(i.plus(-1))
                    turn_probs(i, 1)
                if nxt:
                    if not n.first:
                        pe.wait_ge(x_in[n.parity], n.half(n.parity) * 16)
                    if cur:
                        pe.wait_ge(w_lo_done, i.times(1, 6))
                    else:
                        pe.wait_ge(first_lo_done, 4)
                if cur:
                    scores(i, 0)
                if nxt:
                    if prev and not (isinstance(i.trip, int) and i.off == 1):
                        pe.wait_ge(summed, i.times(1, -1))
                    project(n, qkv_base, 0, DM, ps[:, BANK_P, :], q_done)
                if prev:
                    values(i, 0)
                    turn_probs(i, 2)
                if cur:
                    scores(i, 1)
                if prev:
                    values(i, 1)
                    turn_probs(i, 3)
                if cur:
                    scores(i, 2)
                if prev:
                    values(i, 2)
                    turn_probs(i, 4)
                if cur:
                    scores(i, 3)
                if nxt:
                    if not cur:
                        pe.wait_ge(first_lo_done, 5)
                    pe.wait_ge(q_copied, n.times(1, 1))
                    project(n, qkv_base, QW, 2 * P, ps[:, BANK_P, 0:2 * P], kv_done)
                if prev:
                    values(i, 3)
                    values(i, 4)
                if nxt:
                    pe.wait_ge(q_roped, n.times(1, 1))
                    turn(i, QUERIES, [q_a[:, h * P:h * P + P] for h in range(QPK)])
                    pe.wait_ge(kv_in[n.parity], n.half(1) * 16 * KT)
                    if cur:
                        pe.wait_ge(maxed, i.times(4, 3))
                    for j in range(KT):
                        ins = pe.transpose(ps[:, BANK_KC, j * P:j * P + P], kv[n.parity][:, j, 0:P], ident)
                    ins.then_inc(kc_turned, 1)
                if prev:
                    if nxt:
                        pe.wait_ge(kv_copied, n.times(1, 1))
                    elif not cur:
                        pe.wait_ge(summed, i.times(1, -1))
                    pe.wait_ge(w_lo_done, (i.times(1, 7) if nxt else STEPS + SEQS - 1))
                if cur:
                    turn_probs(n, 0)
                if prev:
                    pe.wait_ge(o_hi_done, i.times(1, 0))
                    output_hi(o_base)
                if nxt:
                    pe.wait_ge(k_roped, n.times(1, 1))
                    pe.transpose(ps[:, BANK_KN, SPARE], k_a[:, :], ident).then_inc(kn_turned, 1)
                if prev:
                    pe.wait_ge(o_lo_done, i.times(1, 0))
                    output_lo(o_base).then_inc(o_done, 1)

            run(pe, body)


def last_layer(nc, t, ps, cst, ones, prob, w_hi, w_lo, x1_split, att):
    ident, iota = cst[:, C_ID:C_ID + P], cst[:, C_IOTA:C_IOTA + EXP]
    with ExitStack() as ctx:
        sb = lambda n, s, d=F32: ctx.enter_context(nc.sbuf_tensor(n, s, d))
        sem = lambda n: ctx.enter_context(nc.semaphore(n))
        x1 = sb("x1", [P, CT, TOK])
        x1_lo = prob[:, :, :, :].rearrange("p a h k -> p (a h k)")[:, 0:CT * TOK].rearrange("p (c n) -> p c n", c=CT)
        z_hi, z_lo = (part[:, GW:GW + CT * TOK].rearrange("p (c n) -> p c n", c=CT) for part in (w_hi, w_lo))
        L = Layer(sb, "ffn1", GH, (w_hi, w_lo))
        wk = Work(sb, sem, "b1")
        small = sb("small1", [P, 4 * GH + EXP])
        gw2 = sb("gw2", [GH, EXP])
        hid = sb("ghid", [P, SEQS, GH])
        cen = sb("gcen", [P, SEQS, GH])
        st = sb("gst", [P, 4, SEQS])
        hid_t = sb("ghid_t", [GH, SEQS, P])
        lg = sb("glg", [P, SEQS, EXP])
        t2 = top2_buffers(sb, "t3")
        allowed = sb("allowed", [P, 2, EXP])
        late_banks = (4, 5, 0, 1)
        s_x1, s_small, x1_ready = sem("x1_in"), sem("small1_in"), sem("x1_ready")
        blk_turned, blk_hi, blk_lo, chain, exp_in, exp_out, hid_ready, hid_turned, hid_t_done, logits2, hot_ready, counted, out_ready, stored, var_ready, std_ready = (
            sem(n) for n in ("blk_turned", "blk_hi", "blk_lo", "chain1", "exp1_in", "exp1_out", "hid_ready", "hid_turned",
                             "hid_t_done", "logits2", "hot_ready", "counted", "out_ready", "stored1", "var_ready", "std_ready"))
        block = ctx.enter_context(nc.Block())

        @block.sync
        def _(sp):
            sp.dma_start(L.route_w[:, :, :], t["ffn1_route"]).then_inc(s_small, 16)
            sp.dma_start(small[:, :], t["ffn1_small"]).then_inc(s_small, 16)
            sp.dma_start(gw2[:, :], t["ffn1_gw2"]).then_inc(s_small, 16)
            for j, part in enumerate((x1, x1_lo)):
                for b in range(SEQS):
                    sp.dma_start(part[:, :, b * P:b * P + P],
                                 x1_split[b, :, j * DM:(j + 1) * DM].rearrange("p (c n) -> p c n", c=CT)).then_inc(s_x1, 16)
            for h in range(2):
                for o in range(CT):
                    sp.wait_ge(out_ready, 4 * h + o + 1)
                    sp.dma_start(t["out"][:, o, halves(h)], x1[:, o, halves(h)]).then_inc(stored, 16)
            sp.wait_ge(stored, 16 * 8)

        @block.gpsimd
        def _(pool):
            pool.wait_ge(var_ready, 1)
            pool.tensor_tensor(st[:, 2, :], st[:, 1, :], st[:, 3, :], ALU.pow).then_inc(std_ready, 1)
            pool.wait_ge(s_x1, 16 * 2 * SEQS)
            pool.tensor_tensor(x1[:, :, :], x1[:, :, :], x1_lo, ALU.add).then_inc(x1_ready, 1)

        @block.scalar
        def _(act):
            def split_block(b):
                act.wait_ge(blk_turned, b + 1)
                turned = ps[:, b % 4, :].rearrange("p (c n) -> p c n", c=CT)
                act.activation(z_hi[:, :, b * P:b * P + P], turned, ACT.Copy).then_inc(blk_hi, 1)

            for b in range(SEQS):
                split_block(b)
                if b == 3:
                    act.wait_ge(s_small, 48)
                    act.activation(L.route_hi[:, :, :], L.route_w[:, :, :], ACT.Copy).then_inc(wk.route_hi_done, 1)
            layer_logits_scalar(act, 0, ps, L, wk)
            act.wait_ge(exp_in, 1)
            act.activation(t2["small"][:, 1, :], t2["small"][:, 0, :], ACT.Exp).then_inc(exp_out, 1)
            layer_hidden_scalar(act, 0, ps, wk)
            for h in range(2):
                layer_gated_scalar(act, 0, h, wk)

        @block.vector
        def _(dve):
            n = [0]

            def link(ins):
                n[0] += 1
                ins.then_inc(chain, 1)
                dve.wait_ge(chain, n[0])

            for b in range(SEQS):
                dve.wait_ge(blk_hi, b + 1)
                dve.tensor_tensor(z_lo[:, :, b * P:b * P + P], ps[:, b % 4, :].rearrange("p (c n) -> p c n", c=CT),
                                  z_hi[:, :, b * P:b * P + P].bitcast(F32), ALU.subtract).then_inc(blk_lo, 1)
                if b == 3:
                    dve.wait_ge(wk.route_hi_done, 1)
                    dve.tensor_tensor(L.route_lo[:, :, :], L.route_w[:, :, :], L.route_hi[:, :, :].bitcast(F32),
                                      ALU.subtract).then_inc(wk.route_lo_done, 1)
            dve.wait_ge(s_small, 48)
            dve.wait_ge(wk.logits_done, 1)
            shape = [P, SEQS, GH]
            row = lambda k: bcast(small[:, k * GH:(k + 1) * GH], shape, 1)
            link(dve.tensor_tensor(hid[:, :, :], ps[:, 7, 0:SEQS * GH].rearrange("p (b e) -> p b e", b=SEQS), row(0), ALU.add))
            link(dve.memset(st[:, 2, :], 0.0))
            link(dve.tensor_reduce(st[:, 0, :], hid[:, :, :], AX.X, ALU.add))
            link(dve.tensor_scalar(st[:, 0, :], st[:, 0, :], 1.0 / GH, None, ALU.mult))
            link(dve.tensor_tensor(hid[:, :, :], hid[:, :, :], bcast(st[:, 0, :], shape, 2), ALU.subtract))
            link(dve.tensor_tensor(cen[:, :, :], hid[:, :, :], hid[:, :, :], ALU.mult))
            link(dve.tensor_reduce(st[:, 1, :], cen[:, :, :], AX.X, ALU.add))
            link(dve.tensor_scalar(st[:, 1, :], st[:, 1, :], 1.0 / GH, 1e-5, ALU.mult, ALU.add))
            dve.tensor_scalar(st[:, 3, :], st[:, 2, :], 0.0, -0.5, ALU.mult, ALU.add).then_inc(var_ready, 1)
            dve.wait_ge(std_ready, 1)
            link(dve.tensor_tensor(hid[:, :, :], hid[:, :, :], bcast(st[:, 2, :], shape, 2), ALU.mult))
            link(dve.tensor_tensor(hid[:, :, :], hid[:, :, :], row(1), ALU.mult))
            link(dve.tensor_tensor(hid[:, :, :], hid[:, :, :], row(2), ALU.add))
            dve.tensor_scalar(hid[:, :, :], hid[:, :, :], 0.0, None, ALU.max).then_inc(hid_ready, 1)
            dve.wait_ge(hid_turned, 1)
            dve.tensor_copy(hid_t[:, :, :], ps[0:GH, 6:8, :].rearrange("p a (b n) -> p (a b) n", b=4)).then_inc(hid_t_done, 1)
            dve.wait_ge(logits2, 1)
            link(dve.tensor_tensor(lg[:, :, :], ps[:, 7, 0:SEQS * EXP].rearrange("p (b e) -> p b e", b=SEQS),
                                   bcast(small[:, 3 * GH:3 * GH + EXP], [P, SEQS, EXP], 1), ALU.add))
            top2_gates(dve, link, lg, iota, t2, lambda: dve.wait_ge(exp_out, 1), exp_in, 1.0 / RANK)
            dve.drain().then_inc(hot_ready, 1)
            dve.wait_ge(counted, 1)
            link(dve.tensor_scalar(allowed[:, :, :], ps[:, 7, 0:2 * EXP].rearrange("p (c e) -> p c e", c=2), float(CAPACITY), None, ALU.is_le))
            link(dve.tensor_tensor(t2["hot_g"][:, :, :, :], t2["hot_g"][:, :, :, :],
                                   allowed[:, :, :].unsqueeze(1).broadcast_to([P, SEQS, 2, EXP]), ALU.mult))
            link(dve.tensor_tensor(wk.gate[:, :, :], t2["hot_g"][:, :, 0, :], t2["hot_g"][:, :, 1, :], ALU.add))
            widen_gates(dve, wk)
            dve.wait_ge(x1_ready, 1)
            for h in range(2):
                layer_gated_vector(dve, 0, h, ps, wk)
                for o in range(CT):
                    dve.wait_ge(wk.out_done, 4 * h + o + 1)
                    dve.tensor_tensor(x1[:, o, halves(h)], ps[:, late_banks[o] if h else o, :], x1[:, o, halves(h)], ALU.add).then_inc(out_ready, 1)

        @block.tensor
        def _(pe):
            for b in range(SEQS):
                if b >= 4:
                    pe.wait_ge(blk_lo, b - 3)
                for c in range(CT):
                    ins = pe.transpose(ps[:, b % 4, c * P:c * P + P], att[:, b, c * P:c * P + P], ident)
                ins.then_inc(blk_turned, 1)

            def gate_turn(pe):
                pe.wait_ge(hid_ready, 1)
                for b in range(SEQS):
                    ins = pe.transpose(ps[0:GH, 6 + b // 4, (b % 4) * P:(b % 4) * P + P], hid[:, b, :], ident)
                ins.then_inc(hid_turned, 1)

            def gate_out(pe):
                pe.wait_ge(hid_t_done, 1)
                for b in range(SEQS):
                    ins = pe.matmul(ps[:, 7, b * EXP:b * EXP + EXP], hid_t[:, b, :], gw2[:, :], start=True, stop=True)
                ins.then_inc(logits2, 1)

            def count(pe):
                pe.wait_ge(hot_ready, 1)
                for b in range(SEQS):
                    ins = pe.matmul(ps[:, 7, 0:2 * EXP], ones[:, :], t2["hot"][:, b, :, :].rearrange("p c e -> p (c e)"),
                                    start=(b == 0), stop=(b == SEQS - 1))
                ins.then_inc(counted, 1)

            z_halves = [[part[:, :, halves(h)] for h in range(2)] for part in (z_hi, z_lo)]
            part = LayerTensor(pe, 0, ps, ident, z_halves[0], z_halves[1], L, wk)
            pe.wait_ge(blk_lo, SEQS // 2)
            part.logits(0)
            pe.wait_ge(blk_lo, SEQS)
            part.logits(1)
            part.hidden(0)
            part.turn_logits()
            part.hidden(1)
            part.base(0, 0, 0)
            gate_turn(pe)
            part.base(0, 1, 1)
            gate_out(pe)
            part.base(0, 2, 2)
            part.base(0, 3, 3)
            count(pe)
            pe.wait_ge(wk.hid_copied, 2)
            part.base(1, 0, late_banks[0])
            part.turn_gates(0)
            part.base(1, 1, late_banks[1])
            for o in range(CT):
                part.experts(0, o, o)
            part.turn_gates(1)
            pe.wait_ge(out_ready, 1)
            part.base(1, 2, late_banks[2])
            for o in range(3):
                part.experts(1, o, late_banks[o])
            pe.wait_ge(out_ready, 2)
            part.base(1, 3, late_banks[3])
            part.experts(1, 3, late_banks[3])


def _features_first(a):
    return np.ascontiguousarray(a.reshape(a.shape[0], CT, P).transpose(2, 1, 0))


def _on_all(a):
    return np.ascontiguousarray(np.broadcast_to(np.asarray(a).reshape(1, -1), (P, np.asarray(a).size)))


def _constants():
    c = np.zeros((P, C_ALL), np.float32)
    c[:, C_ID:C_ID + P] = np.eye(P)
    c[:, C_IOTA:C_IOTA + 16] = np.arange(16)
    c[:, C_FREQ:C_FREQ + 64] = np.float32(1.0) / (10000.0 ** (np.arange(0, P, 2) / P)).astype(np.float32)
    c[:, C_KEY:C_KEY + CACHE] = np.arange(CACHE)
    return c


def kernel(**inputs):
    import concourse.bacc as bacc
    from concourse.bass_utils import run_bass_kernel_spmd

    a = {k: np.asarray(v) for k, v in inputs.items()}

    def with_lora(w, la):
        return np.ascontiguousarray(np.concatenate([_features_first(w), _features_first(la)], axis=2))

    groups = []
    for g in range(KVH):
        q = _features_first(a["L1_cond_Wq"][g * DM:(g + 1) * DM]).reshape(P, QW)
        k = _features_first(a["L1_cond_Wk"][g * P:(g + 1) * P])
        v = _features_first(a["L1_cond_Wv"][g * P:(g + 1) * P])
        kv = np.concatenate([k, v], axis=2).reshape(P, KVW)
        o = _features_first(a["L1_cond_Wo"][:, g * DM:(g + 1) * DM]).reshape(P, OW)
        groups.append(np.concatenate([q, kv, o], axis=1).reshape(P, SEQS, CHUNK).transpose(1, 0, 2))
    last = np.zeros((P, GW), np.float32)
    last[:, 0:LW] = with_lora(a["L1_ffn_weight"], a["L1_ffn_lora_A"].transpose(0, 2, 1).reshape(P, DM)).reshape(P, LW)
    last[:, LW:LW + DM] = a["L1_ffn_lora_B"].reshape(P, DM)
    groups.append(last.reshape(P, SEQS, CHUNK).transpose(1, 0, 2))
    part = np.arange(P, dtype=np.int32)
    feed = {
        "consts": _constants(),
        "tokid": part.astype(np.float32).reshape(P, 1),
        "lens": _on_all(a["itok_B_207_1644"]),
        "normw": _on_all(np.concatenate([a["L1_cond_q_norm_w"], a["L1_cond_k_norm_w"]])),
        "x": _features_first(a["x"].reshape(TOK, DM)),
        "lang": _on_all(a["itok_B_0_7"]),
        "cond0_w": with_lora(a["L0_cond_W"], a["L0_cond_A"].reshape(P, DM)),
        "cond0_lb": np.ascontiguousarray(a["L0_cond_B"].transpose(0, 2, 1).reshape(P, DM)),
        "cond0_route": _features_first(a["L0_cond_Wr"]),
        "ffn0_w": with_lora(a["L0_ffn_base_W"], a["L0_ffn_A"].reshape(P, DM)),
        "ffn0_lb": np.ascontiguousarray(a["L0_ffn_B"].transpose(0, 2, 1).reshape(P, DM)),
        "ffn0_route": _features_first(a["L0_ffn_router_W"]),
        "ffn0_b": np.ascontiguousarray(a["L0_ffn_base_b"].reshape(CT, P).T),
        "ffn0_route_b": _on_all(a["L0_ffn_router_b"]),
        "emap": _on_all(a["L0_ffn_expert_map"]),
        "att_w": np.ascontiguousarray(np.concatenate(groups, axis=0)),
        "kv": np.ascontiguousarray(np.concatenate([a["L1_cond_k_cache"], a["L1_cond_v_cache"]], axis=3).reshape(-1, 2 * P)),
        "pages": np.ascontiguousarray(np.repeat(a["itok_Bx16_0_63"].reshape(SEQS, KT, P // PSIZE), PSIZE, axis=2).transpose(2, 0, 1).reshape(P, SEQS * KT)),
        "row_of": np.ascontiguousarray(np.broadcast_to(((part % PSIZE) * KVH)[:, None], (P, SEQS * KT))),
        "head_no": _on_all(np.repeat(np.arange(KVH, dtype=np.int32), KT)),
        "ffn1_route": _features_first(a["L1_ffn_gw1"]),
        "ffn1_small": _on_all(np.concatenate([a["L1_ffn_gb1"], a["L1_ffn_ln_gamma"], a["L1_ffn_ln_beta"], a["L1_ffn_gb2"],
                                              np.zeros(GH, np.float32)])),
        "ffn1_gw2": np.ascontiguousarray(a["L1_ffn_gw2"].T),
    }
    nc = bacc.Bacc("TRN2", target_bir_lowering=False, num_devices=1)
    t = {k: nc.dram_tensor("in_" + k, v.shape, mybir.dt.from_np(v.dtype), kind="ExternalInput").ap() for k, v in feed.items()}
    t["out"] = nc.dram_tensor("out_0", (P, CT, TOK), F32, kind="ExternalOutput").ap()
    build(nc, t)
    r = run_bass_kernel_spmd(nc, [{"in_" + k: v for k, v in feed.items()}], core_ids=[0])
    out = r.results[0]["out_0"]
    return np.ascontiguousarray(out.transpose(2, 1, 0).reshape(SEQS, P, DM))
```
